# Optimizing a Trainium2 kernel written in Bass

```python
import numpy as np
import jax
import jax.numpy as jnp

def _softmax(x, axis=-1):
    return jax.nn.softmax(x, axis=axis)

def _gelu(x):
    return jax.nn.gelu(x, approximate=True)

def _silu(x):
    return jax.nn.silu(x)

def _sigmoid(x):
    return jax.nn.sigmoid(x)

def _layernorm(x, axis=-1, eps=1e-05):
    m = jnp.mean(x, axis=axis, keepdims=True)
    v = jnp.var(x, axis=axis, keepdims=True)
    return (x - m) / jnp.sqrt(v + eps)

def _scatter_add(tgt, idx, src, axis=0):
    return tgt.at[idx].add(src)

def _segment_sum(src, seg, n):
    return jax.ops.segment_sum(src, seg, n)
kernel_name = 'mk_gnn_resnorm_d4_gnn_r32_8e0280'

def setup_inputs(seed: int=0):
    np.random.seed(seed)
    _w = jnp.asarray

    def _rec_inputs():
        import jax
        import jax.numpy as jnp
        _gk = jax.random.key(seed)
        x = -0.0003713 + 1 * jax.random.normal(jax.random.fold_in(_gk, 1), (3125, 256), jnp.float32)
        _s = jax.random.randint(jax.random.fold_in(_gk, 2), (25000,), 0, 3125, jnp.int32)
        _d = jax.random.randint(jax.random.fold_in(_gk, 3), (25000,), 0, 3125, jnp.int32)
        _loop = jnp.arange(3125, dtype=jnp.int32)
        src = jnp.concatenate([_s, _d, _loop])
        dst = jnp.concatenate([_d, _s, _loop])
        _o = jnp.argsort(dst, stable=True)
        src = src[_o]
        dst = dst[_o]
        edge_attr_128 = -5.16925e-05 + 1.00005 * jax.random.normal(jax.random.fold_in(_gk, 12), (53125, 128), jnp.float32)
        edge_type_16 = jax.random.randint(jax.random.fold_in(_gk, 14), (53125,), 0, 16, jnp.int32)
        return (x, src, dst, edge_attr_128, edge_type_16)
    x, src, dst, edge_attr_128, edge_type_16 = _rec_inputs()

    def _L0_gnn_setup():
        import jax, jax.numpy as jnp
        import numpy as np
        ALPHA = 0.2

        def _gat_head(node_feats, W, a, src, dst, N):
            h = node_feats @ W
            C = W.shape[1]
            a_l, a_r = (a[0, :C], a[0, C:])
            s_l = h @ a_l
            s_r = h @ a_r
            logits = s_l[src] + s_r[dst]
            e = jnp.exp(-jax.nn.leaky_relu(logits, negative_slope=ALPHA))
            row_sum = jax.ops.segment_sum(e, src, num_segments=N)
            h_prime = jax.ops.segment_sum(e[:, None] * h[dst], src, num_segments=N)
            return jax.nn.elu(h_prime / row_sum[:, None])
        key = jax.random.key(seed)
        k1, k2, k3, k4, k5, k6 = jax.random.split(key, 6)
        N, E, c_in, c_head = (50000, 25000, 256, 128)
        node_feats = jax.random.normal(k1, (N, c_in), dtype=jnp.float32)
        edge_index = jax.random.randint(k2, (2, E), 0, N, dtype=jnp.int64)
        std_W = 1.414 * np.sqrt(2.0 / (c_in + c_head))
        std_a = 1.414 * np.sqrt(2.0 / (1 + 2 * c_head))
        W1 = jax.random.normal(k3, (c_in, c_head), dtype=jnp.float32) * std_W
        a1 = jax.random.normal(k4, (1, 2 * c_head), dtype=jnp.float32) * std_a
        W2 = jax.random.normal(k5, (c_in, c_head), dtype=jnp.float32) * std_W
        a2 = jax.random.normal(k6, (1, 2 * c_head), dtype=jnp.float32) * std_a
        return {'node_feats': node_feats, 'W1': W1, 'a1': a1, 'W2': W2, 'a2': a2, 'edge_index': edge_index, 'N': N}
    _L0_gnn_all = _L0_gnn_setup()
    _L0_gnn_in = {k: v for k, v in _L0_gnn_all.items() if k in ('W1', 'a1', 'W2', 'a2')}
    del _L0_gnn_all

    def _L1_gnn_setup():
        import jax, jax.numpy as jnp
        import numpy as np
        N_NODES = 50000
        N_EDGES = 25000
        HDIM = 256
        NUMRELS = 16

        def _gru_cell(x, h, w_ih, w_hh, b_ih, b_hh):
            gi = x @ w_ih.T + b_ih
            gh = h @ w_hh.T + b_hh
            i_r, i_z, i_n = jnp.split(gi, 3, axis=-1)
            h_r, h_z, h_n = jnp.split(gh, 3, axis=-1)
            r = jax.nn.sigmoid(i_r + h_r)
            z = jax.nn.sigmoid(i_z + h_z)
            n = jnp.tanh(i_n + r * h_n)
            return (1.0 - z) * n + z * h
        key = jax.random.key(seed)
        ks = jax.random.split(key, 9)
        h = jax.random.normal(ks[0], (N_NODES, HDIM), dtype=jnp.float32)
        relvectors = jax.random.normal(ks[1], (NUMRELS, HDIM), dtype=jnp.float32)
        s = 1.0 / np.sqrt(HDIM)
        w_ih = jax.random.uniform(ks[2], (3 * HDIM, HDIM), minval=-s, maxval=s, dtype=jnp.float32)
        w_hh = jax.random.uniform(ks[3], (3 * HDIM, HDIM), minval=-s, maxval=s, dtype=jnp.float32)
        b_ih = jax.random.uniform(ks[4], (3 * HDIM,), minval=-s, maxval=s, dtype=jnp.float32)
        b_hh = jax.random.uniform(ks[5], (3 * HDIM,), minval=-s, maxval=s, dtype=jnp.float32)
        edge_src = jax.random.randint(ks[6], (N_EDGES,), 0, N_NODES, dtype=jnp.int32)
        edge_dst = jax.random.randint(ks[7], (N_EDGES,), 0, N_NODES, dtype=jnp.int32)
        edge_rel = jax.random.randint(ks[8], (N_EDGES,), 0, NUMRELS, dtype=jnp.int32)
        return {'h': h, 'relvectors': relvectors, 'w_ih': w_ih, 'w_hh': w_hh, 'b_ih': b_ih, 'b_hh': b_hh, 'edge_src': edge_src, 'edge_dst': edge_dst, 'edge_rel': edge_rel}
    _L1_gnn_all = _L1_gnn_setup()
    _L1_gnn_in = {k: v for k, v in _L1_gnn_all.items() if k in ('relvectors', 'w_ih', 'w_hh', 'b_ih', 'b_hh')}
    del _L1_gnn_all

    def _L2_gnn_setup():
        import jax, jax.numpy as jnp
        import numpy as np
        N_NODES = 10000
        N_EDGES = 10000
        D_IN = 256
        D_OUT = 256
        MAX_NORM = 0.95

        def _expmap0(u):
            un = jnp.linalg.norm(u, axis=-1, keepdims=True)
            un_c = jnp.maximum(un, 1e-15)
            return jnp.tanh(un_c) * u / un_c
        key = jax.random.key(seed)
        ks = jax.random.split(key, 7)
        x = jax.random.normal(ks[0], (N_NODES, D_IN), dtype=jnp.float32)
        edge_index = jax.random.randint(ks[1], (2, N_EDGES), 0, N_NODES, dtype=jnp.int64)
        W = jax.random.normal(ks[2], (D_OUT, D_IN), dtype=jnp.float32) * (1.0 / np.sqrt(D_IN))
        b = jax.random.normal(ks[3], (D_OUT,), dtype=jnp.float32) * 0.02
        mag_w = jax.random.normal(ks[4], (1, D_IN), dtype=jnp.float32) * 0.02
        mag_b = jax.random.normal(ks[5], (1,), dtype=jnp.float32) * 0.02
        attn_w = jax.random.normal(ks[6], (1, 2 * D_OUT), dtype=jnp.float32) * (1.0 / np.sqrt(2 * D_OUT))
        return {'x': x, 'edge_index': edge_index, 'W': W, 'b': b, 'mag_w': mag_w, 'mag_b': mag_b, 'attn_w': attn_w}
    _L2_gnn_all = _L2_gnn_setup()
    _L2_gnn_in = {k: v for k, v in _L2_gnn_all.items() if k in ('W', 'b', 'mag_w', 'mag_b', 'attn_w')}
    del _L2_gnn_all

    def _L3_gnn_setup():
        import jax, jax.numpy as jnp
        import numpy as np
        N = 50000
        E = 25000
        DIN = 256
        DOUT = 256
        H = 4
        C = DOUT // H
        ED = 128
        EPS = 1e-16

        def _transformer_conv(x, src, dst, edge_attr, Wq, bq, Wk, bk, Wv, bv, We, be, Ws, bs):
            n = x.shape[0]
            q = (x @ Wq + bq).reshape(n, H, C)
            k = (x @ Wk + bk).reshape(n, H, C)
            v = (x @ Wv + bv).reshape(n, H, C)
            e = (edge_attr @ We + be).reshape(-1, H, C)
            k_j = k[src] + e
            q_i = q[dst]
            alpha = jnp.einsum('ehc,ehc->eh', q_i, k_j) / jnp.sqrt(jnp.asarray(C, dtype=x.dtype))
            amax = jax.ops.segment_max(alpha, dst, num_segments=n)
            amax = jnp.where(jnp.isfinite(amax), amax, 0.0)
            ex = jnp.exp(alpha - amax[dst])
            denom = jax.ops.segment_sum(ex, dst, num_segments=n)
            alpha = ex / (denom[dst] + EPS)
            msg = (v[src] + e) * alpha[..., None]
            out = jax.ops.segment_sum(msg, dst, num_segments=n)
            out = out.reshape(n, H * C)
            return out + x @ Ws + bs
        key = jax.random.key(seed)
        ks = jax.random.split(key, 32)
        w = lambda k, shp: jax.random.normal(k, shp, dtype=jnp.float32) * (1.0 / np.sqrt(shp[0]))
        b = lambda k, n_: jax.random.normal(k, (n_,), dtype=jnp.float32) * 0.01
        inp = {'x': jax.random.normal(ks[0], (N, DIN), dtype=jnp.float32), 'edge_index': jax.random.randint(ks[1], (2, E), 0, N, dtype=jnp.int32), 'edge_attr': jax.random.normal(ks[2], (E, ED), dtype=jnp.float32)}
        names = ['Wq', 'Wk', 'Wv', 'We', 'Ws']
        dims1 = [DIN, DIN, DIN, ED, DIN]
        dims2 = [DOUT, DOUT, DOUT, ED, DOUT]
        i = 3
        for nm, d in zip(names, dims1):
            inp[nm + '1'] = w(ks[i], (d, DOUT))
            i += 1
            inp['b' + nm[1:].lower() + '1'] = b(ks[i], DOUT)
            i += 1
        for nm, d in zip(names, dims2):
            inp[nm + '2'] = w(ks[i], (d, DOUT))
            i += 1
            inp['b' + nm[1:].lower() + '2'] = b(ks[i], DOUT)
            i += 1
        return inp
    _L3_gnn_all = _L3_gnn_setup()
    _L3_gnn_in = {k: v for k, v in _L3_gnn_all.items() if k in ('Wq1', 'bq1', 'Wk1', 'bk1', 'Wv1', 'bv1', 'We1', 'be1', 'Ws1', 'bs1', 'Wq2', 'bq2', 'Wk2', 'bk2', 'Wv2', 'bv2', 'We2', 'be2', 'Ws2', 'bs2')}
    del _L3_gnn_all
    return {'x': x, 'src': src, 'dst': dst, 'edge_attr_128': edge_attr_128, 'edge_type_16': edge_type_16, 'L0_gnn_W1': _L0_gnn_in['W1'], 'L0_gnn_a1': _L0_gnn_in['a1'], 'L0_gnn_W2': _L0_gnn_in['W2'], 'L0_gnn_a2': _L0_gnn_in['a2'], 'L1_gnn_relvectors': _L1_gnn_in['relvectors'], 'L1_gnn_w_ih': _L1_gnn_in['w_ih'], 'L1_gnn_w_hh': _L1_gnn_in['w_hh'], 'L1_gnn_b_ih': _L1_gnn_in['b_ih'], 'L1_gnn_b_hh': _L1_gnn_in['b_hh'], 'L2_gnn_W': _L2_gnn_in['W'], 'L2_gnn_b': _L2_gnn_in['b'], 'L2_gnn_mag_w': _L2_gnn_in['mag_w'], 'L2_gnn_mag_b': _L2_gnn_in['mag_b'], 'L2_gnn_attn_w': _L2_gnn_in['attn_w'], 'L3_gnn_Wq1': _L3_gnn_in['Wq1'], 'L3_gnn_bq1': _L3_gnn_in['bq1'], 'L3_gnn_Wk1': _L3_gnn_in['Wk1'], 'L3_gnn_bk1': _L3_gnn_in['bk1'], 'L3_gnn_Wv1': _L3_gnn_in['Wv1'], 'L3_gnn_bv1': _L3_gnn_in['bv1'], 'L3_gnn_We1': _L3_gnn_in['We1'], 'L3_gnn_be1': _L3_gnn_in['be1'], 'L3_gnn_Ws1': _L3_gnn_in['Ws1'], 'L3_gnn_bs1': _L3_gnn_in['bs1'], 'L3_gnn_Wq2': _L3_gnn_in['Wq2'], 'L3_gnn_bq2': _L3_gnn_in['bq2'], 'L3_gnn_Wk2': _L3_gnn_in['Wk2'], 'L3_gnn_bk2': _L3_gnn_in['bk2'], 'L3_gnn_Wv2': _L3_gnn_in['Wv2'], 'L3_gnn_bv2': _L3_gnn_in['bv2'], 'L3_gnn_We2': _L3_gnn_in['We2'], 'L3_gnn_be2': _L3_gnn_in['be2'], 'L3_gnn_Ws2': _L3_gnn_in['Ws2'], 'L3_gnn_bs2': _L3_gnn_in['bs2']}

def reference(x, src, dst, edge_attr_128, edge_type_16, L0_gnn_W1, L0_gnn_a1, L0_gnn_W2, L0_gnn_a2, L1_gnn_relvectors, L1_gnn_w_ih, L1_gnn_w_hh, L1_gnn_b_ih, L1_gnn_b_hh, L2_gnn_W, L2_gnn_b, L2_gnn_mag_w, L2_gnn_mag_b, L2_gnn_attn_w, L3_gnn_Wq1, L3_gnn_bq1, L3_gnn_Wk1, L3_gnn_bk1, L3_gnn_Wv1, L3_gnn_bv1, L3_gnn_We1, L3_gnn_be1, L3_gnn_Ws1, L3_gnn_bs1, L3_gnn_Wq2, L3_gnn_bq2, L3_gnn_Wk2, L3_gnn_bk2, L3_gnn_Wv2, L3_gnn_bv2, L3_gnn_We2, L3_gnn_be2, L3_gnn_Ws2, L3_gnn_bs2):
    import jax
    import jax.numpy as jnp

    def _L0_gnn_ref(node_feats, W1, a1, W2, a2, edge_index, N):
        import jax, jax.numpy as jnp
        import numpy as np
        ALPHA = 0.2

        def _gat_head(node_feats, W, a, src, dst, N):
            h = node_feats @ W
            C = W.shape[1]
            a_l, a_r = (a[0, :C], a[0, C:])
            s_l = h @ a_l
            s_r = h @ a_r
            logits = s_l[src] + s_r[dst]
            e = jnp.exp(-jax.nn.leaky_relu(logits, negative_slope=ALPHA))
            row_sum = jax.ops.segment_sum(e, src, num_segments=N)
            h_prime = jax.ops.segment_sum(e[:, None] * h[dst], src, num_segments=N)
            return jax.nn.elu(h_prime / row_sum[:, None])
        src, dst = (edge_index[0], edge_index[1])
        out1 = _gat_head(node_feats, W1, a1, src, dst, N)
        out2 = _gat_head(node_feats, W2, a2, src, dst, N)
        return jnp.concatenate([out1, out2], axis=1)

    def _L1_gnn_ref(h, relvectors, w_ih, w_hh, b_ih, b_hh, edge_src, edge_dst, edge_rel):
        import jax, jax.numpy as jnp
        import numpy as np
        N_NODES = 50000
        N_EDGES = 25000
        HDIM = 256
        NUMRELS = 16

        def _gru_cell(x, h, w_ih, w_hh, b_ih, b_hh):
            gi = x @ w_ih.T + b_ih
            gh = h @ w_hh.T + b_hh
            i_r, i_z, i_n = jnp.split(gi, 3, axis=-1)
            h_r, h_z, h_n = jnp.split(gh, 3, axis=-1)
            r = jax.nn.sigmoid(i_r + h_r)
            z = jax.nn.sigmoid(i_z + h_z)
            n = jnp.tanh(i_n + r * h_n)
            return (1.0 - z) * n + z * h
        msg = h[edge_src] + relvectors[edge_rel]
        red = jax.ops.segment_sum(msg, edge_dst, num_segments=h.shape[0])
        return _gru_cell(red, h, w_ih, w_hh, b_ih, b_hh)

    def _L2_gnn_ref(x, edge_index, W, b, mag_w, mag_b, attn_w):
        import jax, jax.numpy as jnp
        import numpy as np
        N_NODES = 10000
        N_EDGES = 10000
        D_IN = 256
        D_OUT = 256
        MAX_NORM = 0.95

        def _expmap0(u):
            un = jnp.linalg.norm(u, axis=-1, keepdims=True)
            un_c = jnp.maximum(un, 1e-15)
            return jnp.tanh(un_c) * u / un_c
        N = x.shape[0]
        F_out = W.shape[0]
        h_raw = x @ W.T + b
        h_dir = h_raw / jnp.maximum(jnp.linalg.norm(h_raw, axis=-1, keepdims=True), 1e-12)
        h_mag = jax.nn.sigmoid(x @ mag_w.T + mag_b) * 1.5
        h = h_dir * h_mag
        src, tgt = (edge_index[0], edge_index[1])
        h_src = h[src]
        h_tgt = h[tgt]
        a_s, a_t = (attn_w[0, :F_out], attn_w[0, F_out:])
        scores = h_src @ a_s + h_tgt @ a_t
        mx = jnp.maximum(jax.ops.segment_max(scores, tgt, num_segments=N), -1000000000.0)
        ex = jnp.exp(scores - mx[tgt])
        se = jax.ops.segment_sum(ex, tgt, num_segments=N)
        attn_weights = ex / (se[tgt] + 1e-10)
        agg = jax.ops.segment_sum(h_src * attn_weights[:, None], tgt, num_segments=N)
        h_combined = h + agg
        h_poincare = _expmap0(h_combined)
        norms = jnp.linalg.norm(h_poincare, axis=1, keepdims=True)
        return jnp.where(norms > MAX_NORM, h_poincare * (MAX_NORM / (norms + 1e-08)), h_poincare)

    def _L3_gnn_ref(x, edge_index, edge_attr, Wq1, bq1, Wk1, bk1, Wv1, bv1, We1, be1, Ws1, bs1, Wq2, bq2, Wk2, bk2, Wv2, bv2, We2, be2, Ws2, bs2):
        import jax, jax.numpy as jnp
        import numpy as np
        N = 50000
        E = 25000
        DIN = 256
        DOUT = 256
        H = 4
        C = DOUT // H
        ED = 128
        EPS = 1e-16

        def _transformer_conv(x, src, dst, edge_attr, Wq, bq, Wk, bk, Wv, bv, We, be, Ws, bs):
            n = x.shape[0]
            q = (x @ Wq + bq).reshape(n, H, C)
            k = (x @ Wk + bk).reshape(n, H, C)
            v = (x @ Wv + bv).reshape(n, H, C)
            e = (edge_attr @ We + be).reshape(-1, H, C)
            k_j = k[src] + e
            q_i = q[dst]
            alpha = jnp.einsum('ehc,ehc->eh', q_i, k_j) / jnp.sqrt(jnp.asarray(C, dtype=x.dtype))
            amax = jax.ops.segment_max(alpha, dst, num_segments=n)
            amax = jnp.where(jnp.isfinite(amax), amax, 0.0)
            ex = jnp.exp(alpha - amax[dst])
            denom = jax.ops.segment_sum(ex, dst, num_segments=n)
            alpha = ex / (denom[dst] + EPS)
            msg = (v[src] + e) * alpha[..., None]
            out = jax.ops.segment_sum(msg, dst, num_segments=n)
            out = out.reshape(n, H * C)
            return out + x @ Ws + bs
        src, dst = (edge_index[0], edge_index[1])
        h = _transformer_conv(x, src, dst, edge_attr, Wq1, bq1, Wk1, bk1, Wv1, bv1, We1, be1, Ws1, bs1)
        h = jax.nn.relu(h)
        out = _transformer_conv(h, src, dst, edge_attr, Wq2, bq2, Wk2, bk2, Wv2, bv2, We2, be2, Ws2, bs2)
        return out
    edge_index = jnp.stack([src, dst])
    x = _layernorm(x + _L0_gnn_ref(x, L0_gnn_W1, L0_gnn_a1, L0_gnn_W2, L0_gnn_a2, edge_index, 3125), axis=-1)
    x = _layernorm(x + _L1_gnn_ref(x, L1_gnn_relvectors, L1_gnn_w_ih, L1_gnn_w_hh, L1_gnn_b_ih, L1_gnn_b_hh, src, dst, edge_type_16), axis=-1)
    x = _layernorm(x + _L2_gnn_ref(x, edge_index, L2_gnn_W, L2_gnn_b, L2_gnn_mag_w, L2_gnn_mag_b, L2_gnn_attn_w), axis=-1)
    x = _layernorm(x + _L3_gnn_ref(x, edge_index, edge_attr_128, L3_gnn_Wq1, L3_gnn_bq1, L3_gnn_Wk1, L3_gnn_bk1, L3_gnn_Wv1, L3_gnn_bv1, L3_gnn_We1, L3_gnn_be1, L3_gnn_Ws1, L3_gnn_bs1, L3_gnn_Wq2, L3_gnn_bq2, L3_gnn_Wk2, L3_gnn_bk2, L3_gnn_Wv2, L3_gnn_bv2, L3_gnn_We2, L3_gnn_be2, L3_gnn_Ws2, L3_gnn_bs2), axis=-1)
    return x

_drawn_inputs = setup_inputs


def setup_inputs(seed=0):
    import zlib

    import numpy as np

    out = dict(_drawn_inputs(seed))
    spreads = {}
    factors = {'L1_gnn_b_ih': 8.0,
     'L1_gnn_b_hh': 8.0,
     'L2_gnn_b': 33.988,
     'L2_gnn_mag_w': 23.533,
     'L2_gnn_attn_w': 64.0,
     'L3_gnn_bq1': 8.0,
     'L3_gnn_bk1': 64.0,
     'L3_gnn_bv1': 8.0,
     'L3_gnn_be1': 8.0,
     'L3_gnn_bs1': 8.0,
     'L3_gnn_bq2': 8.0,
     'L3_gnn_bk2': 64.0,
     'L3_gnn_bv2': 8.0,
     'L3_gnn_be2': 8.0,
     'L3_gnn_bs2': 8.0}
    for name, (base, spread) in spreads.items():
        noise = np.random.default_rng([zlib.crc32(name.encode()), seed]).standard_normal(out[name].shape)
        drawn = base * np.exp(spread * noise) if base else spread * noise
        out[name] = jnp.asarray(drawn.astype(out[name].dtype))
    for name, factor in factors.items():
        out[name] = (out[name] * factor).astype(out[name].dtype)
    return out
```

```python
from contextlib import ExitStack

import concourse.bass as bass
from concourse import mybir

F32 = mybir.dt.float32
I32 = mybir.dt.int32
BF16 = mybir.dt.bfloat16
ALU = mybir.AluOpType
ACT = mybir.ActivationFunctionType
AX = mybir.AxisListType.X

P = 128
N, F = 3125, 256
E = 53125
NT = -(-N // P)
NP = NT * P
ET = 416
EP = ET * P
CL = 512
CP = EP // CL
J = CL // P
LOHI = P
NH = NP // P
HB = 8
BODY = 2 * HB
TRIPS = ET // BODY
GRP = 5
NG = NT // GRP
ACCW = NP + P
PADN = NP - 1
BIG = 1.0e30
H3, C3 = 4, 64
ED = 128
NREL = 16
TAIL = N - (NT - 1) * P
ETAIL = E - (CP - 1) * CL


class Chain:

    def __init__(self, eng, sem):
        self.eng, self.sem, self.base, self.n = eng, sem, 0, 0

    def __call__(self, ins):
        self.n += 1
        ins.then_inc(self.sem, 1)
        self.eng.wait_ge(self.sem, self.base + self.n)

    def enter(self, i, per_trip):
        self.start = self.base + self.n
        self.base, self.n = self.start + i * per_trip, 0

    def leave(self, trips, per_trip):
        assert self.n == per_trip, (self.n, per_trip)
        self.base, self.n = self.start + trips * per_trip, 0


def graph_layers(nc, a, out, dump=None, stop=99):
    ctx = ExitStack()
    with ctx:
        def sb(name, shape, dt=F32):
            return ctx.enter_context(nc.sbuf_tensor(name, shape, dt))

        phase_sems = []

        def lasting_sem(name):
            return ctx.enter_context(nc.semaphore(name))

        def sem(name):
            phase_sems.append(nc.alloc_semaphore(name=name))
            return phase_sems[-1]

        def end_of_phase():
            nc.clear_and_free_semaphores(list(phase_sems))
            phase_sems.clear()
            nc.all_engine_barrier()

        def dram(name, shape, dt=F32):
            return nc.dram_tensor(name, shape, dt, kind="Internal").ap()

        x_tab = dram("x_tab", [NP, F])
        h_tab = dram("h_tab", [NP, F + 2])
        h2_tab = dram("h2_tab", [NP, F])
        k_tab = dram("k_tab", [NP, F])
        v_tab = dram("v_tab", [NP, F])
        q_tab = dram("q_tab", [ACCW, F])
        lo_tab = dram("lo_tab", [2, EP], BF16)

        X = sb("X", [P, NT, F])
        H = sb("H", [P, NT, F])
        acc = sb("acc", [P, 3, ACCW])
        work = sb("work", [P, 13440])

        def carve(*shapes):
            at, views = 0, []
            for s in shapes:
                n = 1
                for d in s:
                    n *= d
                v = work[:, at:at + n]
                names = " ".join("abcd"[:len(s)])
                if len(s) > 1:
                    v = v.rearrange(f"p ({names}) -> p {names}", **dict(zip("abcd", s)))
                views.append(v)
                at += n
            assert at <= 13440, at
            return views

        accg, xg, xTg, g5, stage = carve((3, GRP * P), (GRP, F), (2, GRP * P), (GRP, 1024), (3, GRP, F))
        grow, qrow, oh, arow, aT, ohT, both = carve((BODY, F + 2), (HB, F), (HB, 2, P), (BODY, ED), (4, P), (4, P), (4, F))
        wbig = sb("wbig", [P, 2, 2, 768])
        ident = sb("ident", [P, P])
        iota_n = sb("iota_n", [P, P])
        iota_p = sb("iota_p", [P, 1])
        sel = sb("sel", [P, 2, P])
        ones = sb("ones", [1, P])
        srcT = sb("srcT", [P, ET], I32)
        dstT = sb("dstT", [P, ET])
        dloc = sb("dloc", [P, ET])
        typT = sb("typT", [P, ET])
        hiT = sb("hiT", [P, 2, ET])
        base_i = sb("base_i", [1, ET], I32)
        idx_st = sb("idx_st", [P, 2, HB], I32)
        w_e = sb("w_e", [P, ET, H3])
        w_flat = w_e[:, :, :].rearrange("p t h -> p (t h)")
        w0 = w_flat[:, 0:2 * F].rearrange("p (k f) -> p k f", k=2)
        bc_a = w_flat[:, 2 * F:2 * F + 4 * P].rearrange("p (a c) -> p a c", a=4)
        relr = w_flat[0:NREL, 2 * F + 4 * P:3 * F + 4 * P]
        s_e = sb("s_e", [P, ET, 2])
        cont = sb("cont", [CP, CL])
        contn = sb("contn", [CP, CL])
        notn = sb("notn", [CP, CL])
        pen = sb("pen", [CP, CL])
        ends = sb("ends", [CP, 2], I32)
        endf = sb("endf", [CP, 2])
        all4 = sb("all4", [CP, 2, H3])
        allr = sb("allr", [H3, 3, CP])
        lastv = sb("lastv", [CP, H3])
        rowc = sb("rowc", [H3, 2, CP + 1])
        carry = sb("carry", [CP, H3])
        s_tab = sb("s_tab", [P, NT, 2])
        s_rem = sb("s_rem", [P, NT, 2])
        s_bf = sb("s_bf", [P, 3, 2, NT], BF16)
        w2T = sb("w2T", [P, 2, F + 1])
        bc_a2 = sb("bc_a2", [P, 2, F])
        bc_b = sb("bc_b", [P, 1024])
        bc_b2 = sb("bc_b2", [P, F + 1])
        bc_t = sb("bc_t", [P, 1024])
        relw = sb("relw", [NREL, 768])
        relT = sb("relT", [P, 2, NREL])
        small = sb("small", [P, 16, GRP])
        we = sb("we", [ED, F])

        PS = [ctx.enter_context(nc.psum_tensor(f"bank{i}", [P, 512], F32)) for i in range(8)]

        accf = acc[:, :, :].rearrange("p a b -> p (a b)")

        def ds(start, n):
            return bass.ds(start, n)

        g_ready = [lasting_sem(f"g_ready{u}") for u in range(BODY)]
        q_ready = [lasting_sem(f"q_ready{u}") for u in range(HB)]
        g_base, q_base = [0], [0]

        def setup():
            ld_w, ld_i, ld_x, ld_e = sem("ld_w"), sem("ld_i"), sem("ld_x"), sem("ld_e")
            padded, consts = sem("padded"), sem("consts")
            dv, pl = sem("setup_dve"), sem("setup_pool")
            floats_ready, t_ready, t_taken = sem("floats_ready"), sem("t_ready"), sem("t_taken")
            lo_ready, lo_out = sem("lo_ready"), sem("lo_out")
            wt_ready, wt_taken = sem("wt_ready"), sem("wt_taken")
            zrow_ready = sem("zrow_ready")
            base_ready, base_done, rows_ready, rows_done = sem("base_ready"), sem("base_done"), sem("rows_ready"), sem("rows_done")
            rel_ready, rel_taken, relw_ready = sem("rel_ready"), sem("rel_taken"), sem("relw_ready")

            wih_r = accf[:, 0:1536].rearrange("p (o k) -> p o k", o=6)
            whh_r = accf[:, 1536:3072].rearrange("p (o k) -> p o k", o=6)
            w2_r = accf[:, 3072:3584].rearrange("p (o k) -> p o k", o=2)
            I = accf[0:CP, 3584:5120].bitcast(I32).rearrange("p (a e) -> p a e", a=3)
            Ff = accf[0:CP, 5120:7680].rearrange("p (a e) -> p a e", a=5)
            LH = accf[0:CP, 7680:9728].bitcast(I32).rearrange("p (a e) -> p a e", a=4)
            lo_b = stage[0:CP, 0, 0:4, :].rearrange("p a e -> p (a e)").bitcast(BF16)[:, 0:2 * CL].rearrange("p (a e) -> p a e", a=2)
            names = ("src", "dst", "edge_type_16")

            with nc.Block() as block:
                @block.sync
                def _(sp):
                    sp.dma_start(wih_r, a["L1_gnn_w_ih"].rearrange("(o p) k -> p o k", p=P)).then_inc(ld_w, 16)
                    sp.dma_start(whh_r, a["L1_gnn_w_hh"].rearrange("(o p) k -> p o k", p=P)).then_inc(ld_w, 16)
                    sp.dma_start(w2_r, a["L2_gnn_W"].rearrange("(o p) k -> p o k", p=P)).then_inc(ld_w, 16)
                    sp.dma_start(relr, a["L1_gnn_relvectors"]).then_inc(ld_w, 16)
                    sp.wait_ge(padded, 1)
                    for n, name in enumerate(names):
                        whole = (CP - 1) * CL
                        sp.dma_start(I[0:CP - 1, n, :], a[name][0:whole].rearrange("(p e) -> p e", e=CL)).then_inc(ld_i, 16)
                        sp.dma_start(I[CP - 1:CP, n, 0:ETAIL], a[name][whole:E].unsqueeze(0)).then_inc(ld_i, 16)
                    sp.dma_start(ends[1:CP - 1, 0:1], a["dst"][CL - 1:CL - 1 + (CP - 2) * CL].rearrange("(p e) -> p e", e=CL)[:, 0:1],
                                 allow_slow_non_contiguous=True).then_inc(ld_e, 16)
                    sp.dma_start(ends[CP - 1:CP, 0:1], a["dst"][(CP - 1) * CL - 1:(CP - 1) * CL].unsqueeze(0)).then_inc(ld_e, 16)
                    sp.dma_start(ends[0:CP - 2, 1:2], a["dst"][CL:CL + (CP - 2) * CL].rearrange("(p e) -> p e", e=CL)[:, 0:1],
                                 allow_slow_non_contiguous=True).then_inc(ld_e, 16)
                    sp.dma_start(ends[CP - 2:CP - 1, 1:2], a["dst"][(CP - 1) * CL:(CP - 1) * CL + 1].unsqueeze(0)).then_inc(ld_e, 16)
                    sp.dma_start(X[:, 0:NT - 1, :], a["x"][0:(NT - 1) * P, :].rearrange("(t p) f -> p t f", p=P)).then_inc(ld_x, 16)
                    sp.dma_start(X[0:TAIL, NT - 1, :], a["x"][(NT - 1) * P:N, :]).then_inc(ld_x, 16)
                    sp.dma_start(w0[:, :, 0:P], a["L0_gnn_W1"].rearrange("(k p) f -> p k f", p=P)).then_inc(ld_x, 16)
                    sp.dma_start(w0[:, :, P:F], a["L0_gnn_W2"].rearrange("(k p) f -> p k f", p=P)).then_inc(ld_x, 16)
                    for n, name in enumerate(("L0_gnn_a1", "L0_gnn_a2")):
                        sp.dma_start(bc_a[:, 2 * n:2 * n + 2, :].rearrange("p a c -> p (a c)"), a[name].broadcast_to([P, F])).then_inc(ld_x, 16)
                    for n in range(2):
                        sp.dma_start(bc_a2[:, n, :], a["L2_gnn_attn_w"][:, n * F:(n + 1) * F].broadcast_to([P, F])).then_inc(ld_x, 16)
                    sp.dma_start(bc_b2[:, 0:F], a["L2_gnn_b"].unsqueeze(0).broadcast_to([P, F])).then_inc(ld_x, 16)
                    sp.dma_start(bc_b2[:, F:F + 1], a["L2_gnn_mag_b"].unsqueeze(0).broadcast_to([P, 1])).then_inc(ld_x, 16)
                    for k in range(2):
                        sp.dma_start(w2T[:, k, F:F + 1], a["L2_gnn_mag_w"][0:1, k * P:(k + 1) * P].rearrange("a p -> p a"),
                                     allow_slow_non_contiguous=True).then_inc(ld_x, 16)
                    sp.dma_start(bc_t[:, 0:768], a["L1_gnn_b_ih"].unsqueeze(0).broadcast_to([P, 768])).then_inc(ld_x, 16)
                    sp.dma_start(bc_b[:, 0:768], a["L1_gnn_b_hh"].unsqueeze(0).broadcast_to([P, 768])).then_inc(ld_x, 16)
                    sp.wait_ge(lo_ready, 1)
                    for n in range(2):
                        sp.dma_start(lo_tab[n, :].rearrange("(p e) -> p e", e=CL), lo_b[:, n, :]).then_inc(lo_out, 16)
                    sp.dma_start(q_tab[NP:ACCW, :], qrow[:, 0, :]).then_inc(lo_out, 16)
                    sp.wait_ge(lo_out, 48)
                    sp.wait_ge(ld_w, 16 * 4)
                    sp.wait_ge(ld_x, 16 * 14)

                @block.gpsimd
                def _(pool):
                    nc.gpsimd.iota(iota_n[:, :], pattern=[[1, P]], base=0, channel_multiplier=0, allow_small_or_imprecise_dtypes=True)
                    nc.gpsimd.iota(iota_p[:, :], pattern=[[1, 1]], base=0, channel_multiplier=1, allow_small_or_imprecise_dtypes=True)
                    nc.gpsimd.memset(sel[:, :, :], 0.0)
                    nc.gpsimd.memset(ident[:, :], 0.0).then_inc(pl, 1)
                    pool.wait_ge(pl, 1)
                    nc.gpsimd.affine_select(out=ident[:, :], in_=ident[:, :], compare_op=ALU.not_equal, fill=1.0, base=0,
                                            pattern=[[-1, P]], channel_multiplier=1)
                    for h in range(2):
                        nc.gpsimd.memset(sel[:, h, h:h + 1], 1.0)
                    nc.gpsimd.memset(ones[:, :], 1.0).then_inc(consts, 1)

                @block.vector
                def _(dve):
                    step = Chain(dve, dv)
                    nc.vector.memset(qrow[:, 0, :], 0.0)
                    nc.vector.memset(I[:, 0, :], 0)
                    nc.vector.memset(I[:, 1, :], PADN)
                    nc.vector.memset(I[:, 2, :], 0)
                    nc.vector.memset(ends[:, :], -1)
                    nc.vector.memset(X[:, NT - 1, :], 0.0).then_inc(padded, 1)
                    dve.wait_ge(ld_i, 16 * 6)
                    nc.vector.tensor_scalar(LH[:, 0:2, :], I[:, 0:2, :], 7, None, ALU.logical_shift_right)
                    step(nc.vector.tensor_scalar(LH[:, 2:4, :], I[:, 0:2, :], LOHI - 1, None, ALU.bitwise_and))
                    nc.vector.tensor_copy(Ff[:, 0:3, :], I[:, :, :])
                    nc.vector.tensor_copy(Ff[:, 3:5, :], LH[:, 0:2, :]).then_inc(floats_ready, 1)
                    nc.vector.tensor_copy(lo_b[:, :, :], LH[:, 2:4, :]).then_inc(lo_ready, 1)
                    dve.wait_ge(floats_ready, 1)
                    dve.wait_ge(ld_e, 64)
                    step(nc.vector.tensor_copy(endf[:, :], ends[:, :]))
                    nc.vector.tensor_tensor(cont[:, 1:CL], Ff[:, 1, 1:CL], Ff[:, 1, 0:CL - 1], ALU.is_equal)
                    nc.vector.tensor_tensor(cont[:, 0:1], Ff[:, 1, 0:1], endf[:, 0:1], ALU.is_equal)
                    nc.vector.tensor_tensor(contn[:, 0:CL - 1], Ff[:, 1, 1:CL], Ff[:, 1, 0:CL - 1], ALU.is_equal)
                    step(nc.vector.tensor_tensor(contn[:, CL - 1:CL], Ff[:, 1, CL - 1:CL], endf[:, 1:2], ALU.is_equal))
                    nc.vector.tensor_scalar(notn[:, :], contn[:, :], -1.0, 1.0, ALU.mult, ALU.add)
                    nc.vector.tensor_scalar(pen[:, :], cont[:, :], BIG, -BIG, ALU.mult, ALU.add)
                    nc.vector.tensor_reduce(all4[:, 0, 0:1], cont[:, :], AX, ALU.min)
                    step(nc.vector.tensor_reduce(all4[:, 1, 0:1], contn[:, :], AX, ALU.min))
                    for n in range(2):
                        last = nc.vector.tensor_copy(all4[:, n, 1:H3], all4[:, n, 0:1].broadcast_to([CP, H3 - 1]))
                    last.then_inc(rows_ready, 1)
                    for n in range(5):
                        dve.wait_ge(t_ready, n + 1)
                        dst_ap = (srcT[:, :], dstT[:, :], typT[:, :], hiT[:, 0, :], hiT[:, 1, :])[n]
                        nc.vector.tensor_copy(dst_ap.rearrange("q (p j) -> q j p", j=J),
                                              PS[n % 2][:, 0:ET].rearrange("q (j p) -> q j p", j=J)).then_inc(t_taken, 1)
                    dve.wait_ge(t_taken, 5)
                    nc.vector.tensor_copy(base_i[:, :], dstT[0:1, :]).then_inc(base_ready, 1)
                    dve.wait_ge(base_done, 1)
                    nc.vector.tensor_tensor(dloc[:, :], dstT[:, :], PS[2][:, 0:ET], ALU.subtract)
                    dve.wait_ge(rows_done, 1)
                    step(nc.vector.tensor_copy(allr[:, 0:2, :], PS[3][0:H3, 0:2 * CP].rearrange("h (n p) -> h n p", n=2)))
                    nc.vector.tensor_scalar(allr[:, 2, :], allr[:, 0, :], BIG, -BIG, ALU.mult, ALU.add)

                @block.tensor
                def _(pe):
                    pe.wait_ge(consts, 1)
                    pe.wait_ge(floats_ready, 1)
                    for n in range(5):
                        if n >= 2:
                            pe.wait_ge(t_taken, n - 1)
                        for j in range(J):
                            mm = nc.tensor.transpose(PS[n % 2][:, j * CP:(j + 1) * CP], Ff[:, n, j * P:(j + 1) * P], ident[0:CP, 0:CP])
                        mm.then_inc(t_ready, 1)
                    pe.wait_ge(t_taken, 2)
                    pe.wait_ge(base_ready, 1)
                    nc.tensor.matmul(PS[2][:, 0:ET], ones[:, :], dstT[0:1, :], start=True, stop=True).then_inc(base_done, 1)
                    pe.wait_ge(rows_ready, 1)
                    for n in range(2):
                        mm = nc.tensor.transpose(PS[3][0:H3, n * CP:(n + 1) * CP], all4[:, n, :], ident[0:CP, 0:CP])
                    mm.then_inc(rows_done, 1)
                    pe.wait_ge(ld_w, 64)
                    n = 0
                    for m, rows in enumerate((wih_r, whh_r)):
                        for k in range(2):
                            for half in range(2):
                                if n >= 2:
                                    pe.wait_ge(wt_taken, n - 1)
                                for o in range(3):
                                    mm = nc.tensor.transpose(PS[4 + n % 2][:, o * P:(o + 1) * P], rows[:, half * 3 + o, k * P:(k + 1) * P], ident[:, :])
                                mm.then_inc(wt_ready, 1)
                                n += 1
                    for k in range(2):
                        pe.wait_ge(wt_taken, n - 1)
                        for o in range(2):
                            mm = nc.tensor.transpose(PS[4 + n % 2][:, o * P:(o + 1) * P], w2_r[:, o, k * P:(k + 1) * P], ident[:, :])
                        mm.then_inc(wt_ready, 1)
                        n += 1
                    for k in range(2):
                        mm = nc.tensor.transpose(PS[6][:, k * NREL:(k + 1) * NREL], relr[:, k * P:(k + 1) * P], ident[0:NREL, 0:NREL])
                    mm.then_inc(rel_ready, 1)
                    pe.wait_ge(rel_taken, 1)
                    pe.wait_ge(wt_taken, 10)
                    for c0, c1, bank in ((0, 512, 4), (512, 768, 5)):
                        for k in range(2):
                            mm = nc.tensor.matmul(PS[bank][0:NREL, 0:c1 - c0], relT[:, k, :], wbig[:, 0, k, c0:c1], start=(k == 0), stop=(k == 1))
                    mm.then_inc(relw_ready, 1)

                @block.scalar
                def _(act):
                    n = 0
                    for m in range(2):
                        for k in range(2):
                            for half in range(2):
                                act.wait_ge(wt_ready, n + 1)
                                nc.scalar.copy(wbig[:, m, k, half * 384:(half + 1) * 384], PS[4 + n % 2][:, 0:384]).then_inc(wt_taken, 1)
                                n += 1
                    act.wait_ge(ld_x, 16 * 14)
                    for k in range(2):
                        act.wait_ge(wt_ready, n + 1)
                        nc.scalar.copy(w2T[:, k, 0:F], PS[4 + n % 2][:, 0:F]).then_inc(wt_taken, 1)
                        n += 1
                    act.wait_ge(rel_ready, 1)
                    nc.scalar.copy(relT[:, :, :], PS[6][:, 0:2 * NREL].rearrange("p (k r) -> p k r", k=2)).then_inc(rel_taken, 1)
                    act.wait_ge(relw_ready, 1)
                    nc.scalar.copy(relw[:, 0:512], PS[4][0:NREL, :])
                    nc.scalar.copy(relw[:, 512:768], PS[5][0:NREL, 0:256])


        def xg_transposes(pe, i, rows_at, xt_free, xt_ready):
            pe.wait_ge(rows_at, i + 1)
            for n in range(GRP):
                pe.wait_ge(xt_free, i * GRP + n + 1)
                for k in range(2):
                    mm = nc.tensor.transpose(PS[6 + n % 2][:, k * P:(k + 1) * P], xg[:, n, k * P:(k + 1) * P], ident[:, :])
                mm.then_inc(xt_ready, 1)

        def xg_evacuate(act, i, xt_ready, xt_free, xt_held):
            act.wait_ge(xt_held, i + 1)
            for n in range(GRP):
                act.wait_ge(xt_ready, i * GRP + n + 1)
                nc.scalar.copy(xTg[:, :, n * P:(n + 1) * P], PS[6 + n % 2][:, 0:2 * P].rearrange("p (k c) -> p k c", k=2)).then_inc(xt_free, 1)

        def credit(eng, signal, n):
            eng.sem_inc(signal, n)

        def group_rows(t, i):
            return t[:, ds(i * GRP, GRP), :]

        def table_rows(tab, i, width=F):
            return tab[ds(i * GRP * P, GRP * P), :].rearrange("(t p) f -> p t f", p=P)

        def bc_last(ap, n):
            return ap.unsqueeze(2).broadcast_to([P, GRP, n])

        def layer_norm(dve, step, rows, to, var_ready, std_ready, count):
            mean, var = small[:, 0, :], small[:, 1, :]
            step(nc.vector.tensor_reduce(mean, rows, AX, ALU.add))
            step(nc.vector.tensor_scalar(mean, mean, 1.0 / F, None, ALU.mult))
            step(nc.vector.tensor_tensor(rows, rows, bc_last(mean, F), ALU.subtract))
            step(nc.vector.tensor_tensor(stage[:, 2, :, :], rows, rows, ALU.mult))
            step(nc.vector.tensor_reduce(var, stage[:, 2, :, :], AX, ALU.add))
            nc.vector.tensor_scalar(var, var, 1.0 / F, 1.0e-5, ALU.mult, ALU.add).then_inc(var_ready, 1)
            dve.wait_ge(std_ready, count)
            step(nc.vector.reciprocal(small[:, 3, :], small[:, 2, :]))
            return nc.vector.tensor_tensor(to, rows, bc_last(small[:, 3, :], F), ALU.mult)

        def act_root(act, var_ready, std_ready, count):
            act.wait_ge(var_ready, count)
            nc.scalar.activation(small[:, 2, :], small[:, 1, :], ACT.Sqrt).then_inc(std_ready, 1)

        def project0():
            names = "rows_at rows_free xt_ready xt_free xt_held h_ready h_free hrow_ready hrow_out hrow_free scal_dve".split()
            rows_at, rows_free, xt_ready, xt_free, xt_held, h_ready, h_free, hrow_ready, hrow_out, hrow_free, dv = [sem("p0_" + n) for n in names]
            hrow = g5[:, :, 0:F + 2]
            with nc.Block() as block:
                @block.gpsimd
                def _(pool):
                    with nc.gpsimd.Fori(0, NG) as i:
                        pool.wait_ge(rows_free, i * GRP)
                        nc.gpsimd.tensor_copy(xg[:, :, :], group_rows(X, i)).then_inc(rows_at, 1)

                @block.tensor
                def _(pe):
                    credit(pe, xt_free, 2)
                    credit(pe, h_free, GRP)
                    with nc.tensor.Fori(0, NG) as i:
                        pe.wait_ge(rows_at, i + 1)
                        for n in range(GRP):
                            pe.wait_ge(xt_free, i * GRP + n + 1)
                            for k in range(2):
                                mm = nc.tensor.transpose(PS[6 + n % 2][:, k * P:(k + 1) * P], xg[:, n, k * P:(k + 1) * P], ident[:, :])
                            mm.then_inc(rows_free, 1)
                        for n in range(GRP):
                            pe.wait_ge(xt_free, i * GRP + n + 3)
                            pe.wait_ge(h_free, i * GRP + n + 1)
                            for k in range(2):
                                mm = nc.tensor.matmul(PS[n][:, 0:F], xTg[:, k, n * P:(n + 1) * P], w0[:, k, :], start=(k == 0), stop=(k == 1))
                            mm.then_inc(h_ready, 1)

                @block.scalar
                def _(act):
                    with nc.scalar.Fori(0, NG) as i:
                        act.wait_ge(h_ready, i * GRP)
                        for n in range(GRP):
                            act.wait_ge(rows_free, i * GRP + n + 1)
                            nc.scalar.copy(xTg[:, :, n * P:(n + 1) * P], PS[6 + n % 2][:, 0:2 * P].rearrange("p (k c) -> p k c", k=2)).then_inc(xt_free, 1)
                        act.wait_ge(hrow_out, i * 16)
                        for n in range(GRP):
                            act.wait_ge(h_ready, i * GRP + n + 1)
                            last = nc.scalar.copy(hrow[:, n, 0:F], PS[n][:, 0:F])
                            last.then_inc(h_free, 1)

                @block.vector
                def _(dve):
                    step = Chain(dve, dv)
                    with nc.vector.Fori(0, NG) as i:
                        step.enter(i, 3)
                        dve.wait_ge(hrow_ready, i)
                        dve.wait_ge(h_free, (i + 2) * GRP)
                        for lr in range(2):
                            prod = stage[:, lr, :, :].rearrange("p t (h c) -> p t h c", h=2)
                            for h in range(2):
                                last = nc.vector.tensor_tensor(prod[:, :, h, :], hrow[:, :, h * P:(h + 1) * P],
                                                               bc_a[:, 2 * h + lr, :].unsqueeze(1).broadcast_to([P, GRP, P]), ALU.mult)
                            step(last)
                        step(nc.vector.tensor_reduce(s_tab[:, ds(i * GRP, GRP), 0:2], stage[:, 0, :, :].rearrange("p t (h c) -> p t h c", h=2), AX, ALU.add))
                        nc.vector.tensor_reduce(hrow[:, :, F:F + 2], stage[:, 1, :, :].rearrange("p t (h c) -> p t h c", h=2), AX, ALU.add).then_inc(hrow_ready, 1)
                    step.leave(NG, 3)
                    split3(step, 2)

                @block.sync
                def _(sp):
                    with nc.sync.Fori(0, NG) as i:
                        sp.wait_ge(hrow_ready, i + 1)
                        sp.dma_start(table_rows(h_tab, i), hrow).then_inc(hrow_out, 16)
                    sp.wait_ge(hrow_out, NG * 16)

        def split3(step, c):
            s = s_tab[:, :, 0:c]
            bf = lambda part: s_bf[:, part, 0:c, :].rearrange("p c t -> p t c")
            step(nc.vector.tensor_copy(bf(0), s))
            step(nc.vector.tensor_tensor(s_rem[:, :, 0:c], s, bf(0), ALU.subtract))
            step(nc.vector.tensor_copy(bf(1), s_rem[:, :, 0:c]))
            step(nc.vector.tensor_tensor(s_rem[:, :, 0:c], s_rem[:, :, 0:c], bf(1), ALU.subtract))
            step(nc.vector.tensor_copy(bf(2), s_rem[:, :, 0:c]))

        def look_up(tag, jobs):
            lo_at, oht_ready, mm_ready, taken, dv = [sem(f"{tag}_{n}") for n in "lo_at oht_ready mm_ready taken dve".split()]
            lo_even, lo_odd = sem(tag + "_lo_even"), sem(tag + "_lo_odd")
            lo_b = g5[:, 0:2, 0:512].bitcast(BF16)
            oht = g5[:, 2:4, 0:512].bitcast(BF16)
            ohh = stage[:, 0, :, :].rearrange("p a b -> p (a b)")[:, 0:HB * NH].rearrange("p (u t) -> p u t", u=HB)
            prod = stage[:, 1:3, :, :].rearrange("p a b c -> p (a b c)")
            with nc.Block() as block:
                @block.sync
                def _(sp):
                    credit(sp, oht_ready, 2)
                    for jn, (end, c0, c, e0) in enumerate(jobs):
                        done = jn * ET // HB
                        with nc.sync.Fori(0, TRIPS) as i:
                            for half in range(2):
                                sp.wait_ge(oht_ready, done + i * 2 + half + 1)
                                sp.dma_start(lo_b[:, half, :], lo_tab[end:end + 1, ds((i * 2 + half) * HB * P, HB * P)].broadcast_to([P, HB * P])
                                             ).then_inc((lo_even, lo_odd)[half], 16)

                @block.vector
                def _(dve):
                    step = Chain(dve, dv)
                    for jn, (end, c0, c, e0) in enumerate(jobs):
                        done = jn * ET // HB
                        pr = prod[:, 0:HB * c * NH].rearrange("p (u c t) -> p u c t", u=HB, c=c)
                        with nc.vector.Fori(0, TRIPS) as i:
                            step.enter(i, 4)
                            for half in range(2):
                                dve.wait_ge((lo_even, lo_odd)[half], (done // 2 + i + 1) * 16)
                                nc.vector.tensor_scalar(oht[:, half, :], lo_b[:, half, :], iota_p[:, 0:1], None, ALU.is_equal).then_inc(oht_ready, 1)
                            for half in range(2):
                                t0 = i * BODY + half * HB
                                step(nc.vector.tensor_tensor(ohh, iota_n[:, 0:NH].unsqueeze(1).broadcast_to([P, HB, NH]),
                                                             hiT[:, end, ds(t0, HB)].unsqueeze(2).broadcast_to([P, HB, NH]), ALU.is_equal))
                                dve.wait_ge(mm_ready, done + i * 2 + half + 1)
                                ps = PS[half][:, 0:HB * c * NH].rearrange("p (u c t) -> p u c t", u=HB, c=c)
                                for cc in range(c):
                                    last = nc.vector.tensor_tensor(pr[:, :, cc, :], ps[:, :, cc, :], ohh, ALU.mult)
                                step(last)
                                nc.vector.tensor_reduce(s_e[:, ds(t0, HB), e0:e0 + c], pr, AX, ALU.add).then_inc(taken, 1)
                                dve.wait_ge(taken, done + i * 2 + half + 1)
                        step.leave(TRIPS, 4)

                @block.tensor
                def _(pe):
                    for jn, (end, c0, c, e0) in enumerate(jobs):
                        done = jn * ET // HB
                        with nc.tensor.Fori(0, TRIPS) as i:
                            for half in range(2):
                                pe.wait_ge(oht_ready, done + i * 2 + half + 3)
                                pe.wait_ge(taken, done + i * 2)
                                for u in range(HB):
                                    for part in range(3):
                                        mm = nc.tensor.matmul(PS[half][:, u * c * NH:(u + 1) * c * NH], oht[:, half, u * P:(u + 1) * P],
                                                              s_bf[:, part, c0:c0 + c, :], start=(part == 0), stop=(part == 2))
                                mm.then_inc(mm_ready, 1)


        def gather_rows(pool, tab, width, idx_ready, products, begun):
            base = g_base[0]
            credit(pool, products, BODY)
            with nc.gpsimd.Fori(0, TRIPS) as i:
                for half in range(2):
                    pool.wait_ge(idx_ready, i * 2 + half + 1)
                    for u in range(HB):
                        pool.wait_ge(products, i * BODY + half * HB + u + 1)
                        pool.sem_inc(begun, 1)
                        s = half * HB + u
                        nc.gpsimd.indirect_dma_start(out=grow[:, s, 0:width], out_offset=None, in_=tab,
                                                     in_offset=bass.IndirectOffsetOnAxis(ap=idx_st[:, half, u:u + 1], axis=0)
                                                     ).then_inc(g_ready[s], 16)
            g_base[0] = base + TRIPS

        def aggregate(tag, tab, width, mode):
            names = "idx_ready products begun z_ready w_ready oh_ready win_free zeroed dve".split()
            idx_ready, products, begun, z_ready, w_ready, oh_ready, win_free, zeroed, dv = [sem(f"{tag}_{n}") for n in names]
            slots = 2 if mode == "one" else 3
            gb = g_base[0]
            zl = both[:, 0, 0:2 * HB * 2].rearrange("p (h u c) -> p h u c", h=2, u=HB)
            wl = both[:, 1, 0:2 * HB * 2].rearrange("p (h u c) -> p h u c", h=2, u=HB)
            with nc.Block() as block:
                @block.gpsimd
                def _(pool):
                    gather_rows(pool, tab, width, idx_ready, products, begun)

                @block.scalar
                def _(act):
                    with nc.scalar.Fori(0, TRIPS) as i:
                        for half in range(2):
                            act.wait_ge(products, i * BODY + (half + 1) * HB)
                            nc.scalar.copy(idx_st[:, half, :], srcT[:, ds(i * BODY + half * HB, HB)]).then_inc(idx_ready, 1)
                        if mode == "gat":
                            for half in range(2):
                                act.wait_ge(z_ready, i * 2 + half + 1)
                                nc.scalar.activation(wl[:, half, :, :], zl[:, half, :, :], ACT.Exp, scale=-1.0).then_inc(w_ready, 1)

                @block.vector
                def _(dve):
                    nc.vector.memset(acc[:, :, :], 0.0).then_inc(zeroed, 1)
                    dve.wait_ge(zeroed, 1)
                    step = Chain(dve, dv)
                    with nc.vector.Fori(0, TRIPS) as i:
                        step.enter(i, 2 if mode == "gat" else 0)
                        for half in range(2):
                            t0 = i * BODY + half * HB
                            _, first = nc.values_load_multi_w_load_instructions(
                                base_i[0:1, ds(t0, HB)], engines=[mybir.EngineType.DVE], min_val=0, max_val=NP - 1)
                            if mode == "gat":
                                for u in range(HB):
                                    dve.wait_ge(g_ready[half * HB + u], (gb + i + 1) * 16)
                                step(nc.vector.tensor_tensor(zl[:, half, :, :], grow[:, half * HB:(half + 1) * HB, F:F + 2],
                                                             s_e[:, ds(t0, HB), :], ALU.add))
                                nc.vector.scalar_tensor_tensor(zl[:, half, :, :], zl[:, half, :, :], 0.2, zl[:, half, :, :],
                                                               ALU.mult, ALU.max).then_inc(z_ready, 1)
                                dve.wait_ge(w_ready, i * 2 + half + 1)
                            for u in range(HB):
                                d = dloc[:, ds(t0 + u, 1)]
                                if mode == "gat":
                                    for h in range(2):
                                        last = nc.vector.tensor_scalar(oh[:, u, h, :], iota_n[:, :], d, wl[:, half, u, h:h + 1],
                                                                       ALU.is_equal, ALU.mult)
                                elif mode == "rel":
                                    nc.vector.tensor_scalar(oh[:, u, 0, :], iota_n[:, :], d, None, ALU.is_equal)
                                    last = nc.vector.tensor_scalar(oh[:, u, 1, :], iota_n[:, :], typT[:, ds(t0 + u, 1)], None, ALU.is_equal)
                                else:
                                    last = nc.vector.tensor_scalar(oh[:, u, 0, :], iota_n[:, :], d, w_e[:, ds(t0 + u, 1), 0:1].rearrange("p a b -> p (a b)"),
                                                                   ALU.is_equal, ALU.mult)
                                last.then_inc(oh_ready, 1)
                            for u in range(HB):
                                dve.wait_ge(products, t0 + u + 1 + BODY)
                                dve.wait_ge(win_free, t0 + u + 4)
                                window = acc[:, 0:slots, ds(first[u], P)]
                                nc.vector.tensor_tensor(window, window, PS[u % 4][:, 0:slots * P].rearrange("p (s n) -> p s n", s=slots),
                                                        ALU.add).then_inc(win_free, 1)
                    step.leave(TRIPS, 2 if mode == "gat" else 0)

                @block.tensor
                def _(pe):
                    credit(pe, win_free, 4)
                    with nc.tensor.Fori(0, TRIPS) as i:
                        for s in range(BODY):
                            u = s % HB
                            pe.wait_ge(g_ready[s], (gb + i + 1) * 16)
                            pe.wait_ge(oh_ready, i * BODY + s + 1)
                            pe.wait_ge(win_free, i * BODY + s + 1)
                            ps = PS[u % 4]
                            for half in range(2):
                                rhs = oh[:, u, half if mode == "gat" else 0, :]
                                mm = nc.tensor.matmul(ps[:, half * P:(half + 1) * P], grow[:, s, half * P:(half + 1) * P], rhs, start=True, stop=True)
                            if mode == "gat":
                                for h in range(2):
                                    mm = nc.tensor.matmul(ps[:, 2 * P:3 * P], sel[:, h, :], oh[:, u, h, :], start=(h == 0), stop=(h == 1))
                            elif mode == "rel":
                                mm = nc.tensor.matmul(ps[:, 2 * P:3 * P], oh[:, u, 1, :], oh[:, u, 0, :], start=True, stop=True)
                            mm.then_inc(products, 1)


        def stage_groups(pool, i, free, at, rows=None, aggregate=True):
            pool.wait_ge(free, i + 1)
            if rows is not None:
                nc.gpsimd.tensor_copy(xg[:, :, :], group_rows(rows, i))
            for s in range(3 if aggregate else 0):
                last = nc.gpsimd.tensor_copy(accg[:, s, :], acc[:, s, ds(i * GRP * P, GRP * P)])
            last.then_inc(at, 1)

        def finish0():
            at, free, back, m_ready, e_ready, var_ready, std_ready, x_out, x_ready, dv = [
                sem("f0_" + n) for n in "at free back m_ready e_ready var_ready std_ready x_out x_ready dve".split()]
            with nc.Block() as block:
                @block.gpsimd
                def _(pool):
                    with nc.gpsimd.Fori(0, NG) as i:
                        pool.wait_ge(free, i * GRP)
                        for s in range(3):
                            last = nc.gpsimd.tensor_copy(accg[:, s, :], acc[:, s, ds(i * GRP * P, GRP * P)])
                        last.then_inc(at, 1)

                @block.tensor
                def _(pe):
                    credit(pe, back, 1)
                    with nc.tensor.Fori(0, NG) as i:
                        pe.wait_ge(at, i + 1)
                        pe.wait_ge(back, i + 1)
                        for n in range(GRP):
                            for s in range(3):
                                mm = nc.tensor.transpose(PS[n][:, s * P:(s + 1) * P], accg[:, s, n * P:(n + 1) * P], ident[:, :])
                            mm.then_inc(free, 1)

                @block.vector
                def _(dve):
                    step = Chain(dve, dv)
                    rows, low = stage[:, 0, :, :], stage[:, 1, :, :]
                    den = small[:, 4:6, :].rearrange("p h n -> p n h")
                    with nc.vector.Fori(0, NG) as i:
                        step.enter(i, 10)
                        for n in range(GRP):
                            dve.wait_ge(free, i * GRP + n + 1)
                            last = nc.vector.tensor_scalar(den[:, n, :], PS[n][:, 2 * P:2 * P + 2], 1.0e-38, None, ALU.max)
                        step(last)
                        step(nc.vector.reciprocal(small[:, 6:8, :], small[:, 4:6, :]))
                        rden = small[:, 6:8, :].rearrange("p h n -> p n h")
                        for n in range(GRP):
                            for h in range(2):
                                last = nc.vector.tensor_scalar(rows[:, n, h * P:(h + 1) * P], PS[n][:, h * P:(h + 1) * P], rden[:, n, h:h + 1], None, ALU.mult)
                        last.then_inc(back, 1)
                        dve.wait_ge(back, i + 2)
                        nc.vector.tensor_scalar(low, rows, 0.0, None, ALU.min).then_inc(m_ready, 1)
                        dve.wait_ge(e_ready, i + 1)
                        step(nc.vector.scalar_tensor_tensor(rows, rows, 0.0, low, ALU.max, ALU.add))
                        step(nc.vector.scalar_tensor_tensor(rows, rows, -1.0, group_rows(X, i), ALU.add, ALU.add))
                        layer_norm(dve, step, rows, group_rows(X, i), var_ready, std_ready, i + 1).then_inc(x_ready, 1)
                        dve.wait_ge(x_ready, i + 1)
                    step.leave(NG, 10)

                @block.scalar
                def _(act):
                    with nc.scalar.Fori(0, NG) as i:
                        act.wait_ge(m_ready, i + 1)
                        nc.scalar.activation(stage[:, 1, :, :], stage[:, 1, :, :], ACT.Exp).then_inc(e_ready, 1)
                        act_root(act, var_ready, std_ready, i + 1)

                @block.sync
                def _(sp):
                    with nc.sync.Fori(0, NG) as i:
                        sp.wait_ge(x_ready, i + 1)
                        sp.dma_start(table_rows(x_tab, i), group_rows(X, i)).then_inc(x_out, 16)
                    sp.wait_ge(x_out, NG * 16)


        def transpose_rows(pe, i, at, xt_free, xt_ready):
            pe.wait_ge(at, i + 1)
            for n in range(GRP):
                pe.wait_ge(xt_free, i * GRP + n + 1)
                for k in range(2):
                    mm = nc.tensor.transpose(PS[6 + n % 2][:, k * P:(k + 1) * P], xg[:, n, k * P:(k + 1) * P], ident[:, :])
                mm.then_inc(xt_ready, 1)

        def take_transposed(act, i, xt_ready, xt_free, used):
            act.wait_ge(used, i * GRP)
            for n in range(GRP):
                act.wait_ge(xt_ready, i * GRP + n + 1)
                nc.scalar.copy(xTg[:, :, n * P:(n + 1) * P], PS[6 + n % 2][:, 0:2 * P].rearrange("p (k c) -> p k c", k=2)).then_inc(xt_free, 1)

        def finish1():
            at, xt_ready, xt_free, mm_ready, mm_free, sig_ready, tanh_ask, tanh_ready, var_ready, std_ready, done, dv = [
                sem("f1_" + n) for n in "at xt_ready xt_free mm_ready mm_free sig_ready tanh_ask tanh_ready var_ready std_ready done dve".split()]
            with nc.Block() as block:
                @block.gpsimd
                def _(pool):
                    with nc.gpsimd.Fori(0, NG) as i:
                        pool.wait_ge(mm_ready, i * GRP)
                        nc.gpsimd.tensor_copy(xg[:, :, :], group_rows(X, i))
                        for s in range(3):
                            last = nc.gpsimd.tensor_copy(accg[:, s, :], acc[:, s, ds(i * GRP * P, GRP * P)])
                        last.then_inc(at, 1)

                @block.tensor
                def _(pe):
                    credit(pe, xt_free, 2)
                    credit(pe, mm_free, 1)
                    with nc.tensor.Fori(0, NG) as i:
                        transpose_rows(pe, i, at, xt_free, xt_ready)
                        for n in range(GRP):
                            pe.wait_ge(xt_free, i * GRP + n + 3)
                            pe.wait_ge(mm_free, i * GRP + n + 1)
                            rz, nn = PS[0], PS[1]
                            cols = slice(n * P, (n + 1) * P)
                            for ps, c0, c1, gates in ((rz[:, :], 0, 512, "ih"), (nn[:, 0:F], 512, 768, "i"), (nn[:, F:512], 512, 768, "h")):
                                terms = []
                                if "i" in gates:
                                    terms += [(accg[:, k, cols], wbig[:, 0, k, c0:c1]) for k in range(2)]
                                    terms += [(accg[0:NREL, 2, cols], relw[:, c0:c1])]
                                if "h" in gates:
                                    terms += [(xTg[:, k, cols], wbig[:, 1, k, c0:c1]) for k in range(2)]
                                for m, (left, right) in enumerate(terms):
                                    mm = nc.tensor.matmul(ps, left, right, start=(m == 0), stop=(m == len(terms) - 1))
                            mm.then_inc(mm_ready, 1)

                @block.scalar
                def _(act):
                    with nc.scalar.Fori(0, NG) as i:
                        take_transposed(act, i, xt_ready, xt_free, mm_ready)
                        act.wait_ge(mm_free, (i + 1) * GRP + 1)
                        nc.scalar.activation(g5[:, :, 0:512], g5[:, :, 0:512], ACT.Sigmoid).then_inc(sig_ready, 1)
                        act.wait_ge(tanh_ask, i + 1)
                        nc.scalar.activation(stage[:, 0, :, :], stage[:, 0, :, :], ACT.Tanh).then_inc(tanh_ready, 1)
                        act_root(act, var_ready, std_ready, i + 1)

                @block.vector
                def _(dve):
                    step = Chain(dve, dv)
                    step(nc.vector.tensor_tensor(bc_t[:, 0:512], bc_t[:, 0:512], bc_b[:, 0:512], ALU.add))
                    nn, u = stage[:, 0, :, :], stage[:, 1, :, :]
                    r, z, n_i, n_h = (g5[:, :, q * F:(q + 1) * F] for q in range(4))
                    with nc.vector.Fori(0, NG) as i:
                        step.enter(i, 11)
                        for n in range(GRP):
                            dve.wait_ge(mm_ready, i * GRP + n + 1)
                            nc.vector.tensor_tensor(g5[:, n, 0:512], PS[0][:, :], bc_t[:, 0:512], ALU.add)
                            nc.vector.tensor_tensor(n_i[:, n, :], PS[1][:, 0:F], bc_t[:, 512:768], ALU.add)
                            last = nc.vector.tensor_tensor(n_h[:, n, :], PS[1][:, F:512], bc_b[:, 512:768], ALU.add)
                            last.then_inc(mm_free, 1)
                        dve.wait_ge(mm_free, (i + 1) * GRP + 1)
                        dve.wait_ge(sig_ready, i + 1)
                        step(nc.vector.tensor_tensor(nn, r, n_h, ALU.mult))
                        nc.vector.tensor_tensor(nn, nn, n_i, ALU.add).then_inc(tanh_ask, 1)
                        dve.wait_ge(tanh_ready, i + 1)
                        step(nc.vector.tensor_tensor(u, group_rows(X, i), nn, ALU.subtract))
                        step(nc.vector.tensor_tensor(u, u, z, ALU.mult))
                        step(nc.vector.tensor_tensor(nn, nn, u, ALU.add))
                        step(nc.vector.tensor_tensor(nn, nn, group_rows(X, i), ALU.add))
                        layer_norm(dve, step, nn, group_rows(X, i), var_ready, std_ready, i + 1).then_inc(done, 1)
                        dve.wait_ge(done, i + 1)
                    step.leave(NG, 11)

        def project2():
            at, xt_ready, xt_free, mm_ready, mm_free, nrm_ask, nrm_ready, h_ready, h_out, dv = [
                sem("p2_" + n) for n in "at xt_ready xt_free mm_ready mm_free nrm_ask nrm_ready h_ready h_out dve".split()]
            with nc.Block() as block:
                @block.gpsimd
                def _(pool):
                    with nc.gpsimd.Fori(0, NG) as i:
                        pool.wait_ge(xt_ready, i * GRP)
                        nc.gpsimd.tensor_copy(xg[:, :, :], group_rows(X, i)).then_inc(at, 1)

                @block.tensor
                def _(pe):
                    credit(pe, xt_free, 2)
                    credit(pe, mm_free, GRP)
                    with nc.tensor.Fori(0, NG) as i:
                        transpose_rows(pe, i, at, xt_free, xt_ready)
                        for n in range(GRP):
                            pe.wait_ge(xt_free, i * GRP + n + 3)
                            pe.wait_ge(mm_free, i * GRP + n + 1)
                            for k in range(2):
                                mm = nc.tensor.matmul(PS[n][:, 0:F + 1], xTg[:, k, n * P:(n + 1) * P], w2T[:, k, :], start=(k == 0), stop=(k == 1))
                            mm.then_inc(mm_ready, 1)

                @block.scalar
                def _(act):
                    with nc.scalar.Fori(0, NG) as i:
                        take_transposed(act, i, xt_ready, xt_free, mm_ready)
                        act.wait_ge(nrm_ask, i + 1)
                        nc.scalar.activation(small[:, 5, :], small[:, 5, :], ACT.Sqrt)
                        nc.scalar.activation(small[:, 4, :], small[:, 4, :], ACT.Sigmoid).then_inc(nrm_ready, 1)

                @block.vector
                def _(dve):
                    step = Chain(dve, dv)
                    hr, sq, mag, nrm = stage[:, 0, :, :], stage[:, 1, :, :], small[:, 4, :], small[:, 5, :]
                    with nc.vector.Fori(0, NG) as i:
                        step.enter(i, 8)
                        for n in range(GRP):
                            dve.wait_ge(mm_ready, i * GRP + n + 1)
                            nc.vector.tensor_tensor(hr[:, n, :], PS[n][:, 0:F], bc_b2[:, 0:F], ALU.add)
                            nc.vector.tensor_tensor(mag[:, n:n + 1], PS[n][:, F:F + 1], bc_b2[:, F:F + 1], ALU.add).then_inc(mm_free, 1)
                        dve.wait_ge(mm_free, (i + 2) * GRP)
                        step(nc.vector.tensor_tensor(sq, hr, hr, ALU.mult))
                        nc.vector.tensor_reduce(nrm, sq, AX, ALU.add).then_inc(nrm_ask, 1)
                        dve.wait_ge(nrm_ready, i + 1)
                        step(nc.vector.tensor_scalar(nrm, nrm, 1.0e-12, None, ALU.max))
                        step(nc.vector.reciprocal(small[:, 6, :], nrm))
                        step(nc.vector.scalar_tensor_tensor(small[:, 7, :], mag, 1.5, small[:, 6, :], ALU.mult, ALU.mult))
                        nc.vector.tensor_tensor(group_rows(H, i), hr, bc_last(small[:, 7, :], F), ALU.mult).then_inc(h_ready, 1)
                        dve.wait_ge(h_ready, i + 1)
                        for st in range(2):
                            step(nc.vector.tensor_tensor(sq, group_rows(H, i), bc_a2[:, st, :].unsqueeze(1).broadcast_to([P, GRP, F]), ALU.mult))
                            step(nc.vector.tensor_reduce(s_tab[:, ds(i * GRP, GRP), st:st + 1].rearrange("p t a -> p (t a)"), sq, AX, ALU.add))
                    step.leave(NG, 8)
                    split3(step, 2)

                @block.sync
                def _(sp):
                    with nc.sync.Fori(0, NG) as i:
                        sp.wait_ge(h_ready, i + 1)
                        sp.dma_start(table_rows(h2_tab, i), group_rows(H, i)).then_inc(h_out, 16)
                    sp.wait_ge(h_out, NG * 16)

        xc, Rc, Tc = (accf[0:CP, q * H3 * CL:(q + 1) * H3 * CL].rearrange("p (h e) -> p h e", h=H3) for q in range(3))

        def edge_softmax(tag, heads, scale, eps, least, read):
            c_ready, c_taken, l_ask, l_ready, b_ask, b_ready, e_ask, e_ready, w_ask, w_ready, w_taken, dv = [
                sem(f"{tag}_{n}") for n in "c_ready c_taken l_ask l_ready b_ask b_ready e_ask e_ready w_ask w_ready w_taken dve".split()]

            def carries(dve, step, n, backward, maximum):
                dve.wait_ge(l_ready, n + 1)
                step(nc.vector.tensor_copy(rowc[0:heads, 1, 0:CP], PS[4][0:heads, 0:CP]))
                start = -BIG if maximum else 0.0
                op0, op1 = (ALU.add, ALU.max) if maximum else (ALU.mult, ALU.add)
                keep = allr[0:heads, 2 if maximum else (1 if backward else 0), :]
                if backward:
                    nc.vector.memset(rowc[0:heads, 0, CP:CP + 1], start)
                    nc.vector.tensor_tensor_scan(rowc[0:heads, 0, 0:CP][:, ::-1], keep[:, ::-1], rowc[0:heads, 1, 0:CP][:, ::-1], start, op0, op1).then_inc(b_ask, 1)
                else:
                    nc.vector.memset(rowc[0:heads, 0, 0:1], start)
                    nc.vector.tensor_tensor_scan(rowc[0:heads, 0, 1:CP + 1], keep, rowc[0:heads, 1, 0:CP], start, op0, op1).then_inc(b_ask, 1)
                dve.wait_ge(b_ready, n + 1)
                step(nc.vector.tensor_copy(carry[:, 0:heads], PS[5][0:CP, 0:heads]))

            def totals(dve, step, n, maximum):
                op0, op1 = (ALU.add, ALU.max) if maximum else (ALU.mult, ALU.add)
                keep = pen if maximum else cont
                for again in range(2):
                    for h in range(heads):
                        start = carry[:, h:h + 1] if again else (-BIG if maximum else 0.0)
                        last = nc.vector.tensor_tensor_scan(Rc[:, h, :], keep[:, :], xc[:, h, :], start, op0, op1)
                    step(last)
                    if not again:
                        nc.vector.tensor_copy(lastv[:, 0:heads], Rc[:, 0:heads, CL - 1:CL].rearrange("p h e -> p (h e)")).then_inc(l_ask, 1)
                        carries(dve, step, n, False, maximum)
                step(nc.vector.tensor_tensor(Tc[:, 0:heads, :], Rc[:, 0:heads, :], notn[:, :].unsqueeze(1).broadcast_to([CP, heads, CL]), ALU.mult))
                for again in range(2):
                    for h in range(heads):
                        start = carry[:, h:h + 1] if again else 0.0
                        last = nc.vector.tensor_tensor_scan(Rc[:, h, :][:, ::-1], contn[:, :][:, ::-1], Tc[:, h, :][:, ::-1], start, ALU.mult, ALU.add)
                    step(last)
                    if not again:
                        nc.vector.tensor_copy(lastv[:, 0:heads], Rc[:, 0:heads, 0:1].rearrange("p h e -> p (h e)")).then_inc(l_ask, 1)
                        carries(dve, step, n + 1, True, False)

            with nc.Block() as block:
                @block.vector
                def _(dve):
                    step = Chain(dve, dv)
                    for h in range(heads):
                        dve.wait_ge(c_ready, h + 1)
                        nc.vector.tensor_scalar(xc[:, h, :], PS[h][0:CP, :], scale, None, ALU.mult).then_inc(c_taken, 1)
                    dve.wait_ge(c_taken, heads)
                    totals(dve, step, 0, True)
                    if least is not None:
                        step(nc.vector.tensor_scalar(Rc[:, 0:heads, :], Rc[:, 0:heads, :], least, None, ALU.max))
                    nc.vector.tensor_tensor(xc[:, 0:heads, :], xc[:, 0:heads, :], Rc[:, 0:heads, :], ALU.subtract).then_inc(e_ask, 1)
                    dve.wait_ge(e_ready, 1)
                    totals(dve, step, 2, False)
                    step(nc.vector.tensor_scalar(Rc[:, 0:heads, :], Rc[:, 0:heads, :], eps, None, ALU.add))
                    step(nc.vector.reciprocal(Tc[:, 0:heads, :], Rc[:, 0:heads, :]))
                    nc.vector.tensor_tensor(xc[:, 0:heads, :], xc[:, 0:heads, :], Tc[:, 0:heads, :], ALU.mult).then_inc(w_ask, 1)
                    for h in range(heads):
                        dve.wait_ge(w_ready, h + 1)
                        nc.vector.tensor_copy(w_e[:, :, h].rearrange("q (p j) -> q j p", j=J), PS[h][:, 0:ET].rearrange("q (j p) -> q j p", j=J)).then_inc(w_taken, 1)
                    dve.wait_ge(w_taken, heads)

                @block.scalar
                def _(act):
                    act.wait_ge(e_ask, 1)
                    nc.scalar.activation(xc[:, 0:heads, :], xc[:, 0:heads, :], ACT.Exp).then_inc(e_ready, 1)

                @block.tensor
                def _(pe):
                    for h in range(heads):
                        for j in range(J):
                            mm = nc.tensor.transpose(PS[h][0:CP, j * P:(j + 1) * P], read(h)[:, j::J], ident[:, :])
                        mm.then_inc(c_ready, 1)
                    for n in range(4):
                        pe.wait_ge(l_ask, n + 1)
                        nc.tensor.transpose(PS[4][0:heads, 0:CP], lastv[:, 0:heads], ident[0:CP, 0:CP]).then_inc(l_ready, 1)
                        pe.wait_ge(b_ask, n + 1)
                        row = rowc[0:heads, 0, 1:CP + 1] if n % 2 else rowc[0:heads, 0, 0:CP]
                        nc.tensor.transpose(PS[5][0:CP, 0:heads], row, ident[0:heads, 0:heads]).then_inc(b_ready, 1)
                    pe.wait_ge(w_ask, 1)
                    for h in range(heads):
                        for j in range(J):
                            mm = nc.tensor.transpose(PS[h][:, j * CP:(j + 1) * CP], xc[:, h, j * P:(j + 1) * P], ident[0:CP, 0:CP])
                        mm.then_inc(w_ready, 1)

        def sum_scores():
            dv = sem("score_sum")
            with nc.Block() as block:
                @block.vector
                def _(dve):
                    nc.vector.tensor_tensor(s_e[:, :, 0], s_e[:, :, 0], s_e[:, :, 1], ALU.add).then_inc(dv, 1)
                    dve.wait_ge(dv, 1)

        def finish2():
            at, free, back, n_ask, n_ready, t_ready, m_ask, m_ready, var_ready, std_ready, done, dv = [
                sem("f2_" + n) for n in "at free back n_ask n_ready t_ready m_ask m_ready var_ready std_ready done dve".split()]
            with nc.Block() as block:
                @block.gpsimd
                def _(pool):
                    with nc.gpsimd.Fori(0, NG) as i:
                        pool.wait_ge(free, i * GRP)
                        for s in range(2):
                            last = nc.gpsimd.tensor_copy(accg[:, s, :], acc[:, s, ds(i * GRP * P, GRP * P)])
                        last.then_inc(at, 1)

                @block.tensor
                def _(pe):
                    credit(pe, back, GRP)
                    with nc.tensor.Fori(0, NG) as i:
                        pe.wait_ge(at, i + 1)
                        for n in range(GRP):
                            pe.wait_ge(back, i * GRP + n + 1)
                            for s in range(2):
                                mm = nc.tensor.transpose(PS[n][:, s * P:(s + 1) * P], accg[:, s, n * P:(n + 1) * P], ident[:, :])
                            mm.then_inc(free, 1)

                @block.vector
                def _(dve):
                    step = Chain(dve, dv)
                    hc, sq, nrm, tmp = stage[:, 0, :, :], stage[:, 1, :, :], small[:, 4, :], small[:, 6, :]
                    with nc.vector.Fori(0, NG) as i:
                        step.enter(i, 19)
                        for n in range(GRP):
                            dve.wait_ge(free, i * GRP + n + 1)
                            nc.vector.tensor_tensor(hc[:, n, :], PS[n][:, 0:F], H[:, ds(i * GRP + n, 1), :].rearrange("p a f -> p (a f)"), ALU.add).then_inc(back, 1)
                        dve.wait_ge(back, (i + 2) * GRP)
                        step(nc.vector.tensor_tensor(sq, hc, hc, ALU.mult))
                        nc.vector.tensor_reduce(nrm, sq, AX, ALU.add).then_inc(n_ask, 1)
                        dve.wait_ge(n_ready, i + 1)
                        step(nc.vector.tensor_scalar(nrm, nrm, 1.0e-15, None, ALU.max))
                        nc.vector.reciprocal(tmp, nrm).then_inc(m_ask, 1)
                        dve.wait_ge(t_ready, i + 1)
                        step(nc.vector.tensor_tensor(tmp, tmp, small[:, 5, :], ALU.mult))
                        step(nc.vector.tensor_tensor(hc, hc, bc_last(tmp, F), ALU.mult))
                        step(nc.vector.tensor_tensor(sq, hc, hc, ALU.mult))
                        nc.vector.tensor_reduce(nrm, sq, AX, ALU.add).then_inc(n_ask, 1)
                        dve.wait_ge(m_ready, i + 1)
                        step(nc.vector.tensor_scalar(tmp, nrm, 1.0e-8, None, ALU.add))
                        step(nc.vector.reciprocal(small[:, 7, :], tmp))
                        step(nc.vector.tensor_scalar(tmp, small[:, 7, :], 0.95, -1.0, ALU.mult, ALU.add))
                        step(nc.vector.tensor_scalar(nrm, nrm, 0.95, None, ALU.is_gt))
                        step(nc.vector.tensor_tensor(tmp, tmp, nrm, ALU.mult))
                        step(nc.vector.tensor_scalar(tmp, tmp, 1.0, None, ALU.add))
                        step(nc.vector.tensor_tensor(hc, hc, bc_last(tmp, F), ALU.mult))
                        step(nc.vector.tensor_tensor(hc, hc, group_rows(X, i), ALU.add))
                        layer_norm(dve, step, hc, group_rows(X, i), var_ready, std_ready, i + 1).then_inc(done, 1)
                        dve.wait_ge(done, i + 1)
                    step.leave(NG, 19)

                @block.scalar
                def _(act):
                    nrm = small[:, 4, :]
                    with nc.scalar.Fori(0, NG) as i:
                        act.wait_ge(n_ask, i * 2 + 1)
                        nc.scalar.activation(nrm, nrm, ACT.Sqrt).then_inc(n_ready, 1)
                        act.wait_ge(m_ask, i + 1)
                        nc.scalar.activation(small[:, 5, :], nrm, ACT.Tanh).then_inc(t_ready, 1)
                        act.wait_ge(n_ask, i * 2 + 2)
                        nc.scalar.activation(nrm, nrm, ACT.Sqrt).then_inc(m_ready, 1)
                        act_root(act, var_ready, std_ready, i + 1)

        def project3(layer, rows):
            ln = str(layer)
            ld, bias_ready, at, xt_ready, xt_free, mm_ready, mm_free, q_out, dv = [
                sem(f"p3{ln}_{n}") for n in "ld bias_ready at xt_ready xt_free mm_ready mm_free q_out dve".split()]
            wq = wbig[:, :, :, :].rearrange("p a k f -> p (a k f)")[:, 0:2048].rearrange("p (k f) -> p k f", k=2)
            with nc.Block() as block:
                @block.sync
                def _(sp):
                    for n, letter in enumerate("qkvs"):
                        sp.dma_start(wq[:, :, n * F:(n + 1) * F], a[f"L3_gnn_W{letter}{ln}"].rearrange("(k p) f -> p k f", p=P)).then_inc(ld, 16)
                        sp.dma_start(bc_b[:, n * F:(n + 1) * F], a[f"L3_gnn_b{letter}{ln}"].unsqueeze(0).broadcast_to([P, F])).then_inc(ld, 16)
                    sp.dma_start(bc_b2[:, 0:F], a[f"L3_gnn_be{ln}"].unsqueeze(0).broadcast_to([P, F])).then_inc(ld, 16)
                    sp.dma_start(we[:, :], a[f"L3_gnn_We{ln}"]).then_inc(ld, 16)
                    with nc.sync.Fori(0, NG) as i:
                        sp.wait_ge(mm_free, (i + 1) * GRP * 2 + 2)
                        for n, tab in enumerate((q_tab, k_tab, v_tab)):
                            sp.dma_start(table_rows(tab, i), g5[:, :, n * F:(n + 1) * F]).then_inc(q_out, 16)
                    sp.wait_ge(q_out, NG * 48)

                @block.gpsimd
                def _(pool):
                    with nc.gpsimd.Fori(0, NG) as i:
                        pool.wait_ge(xt_ready, i * GRP)
                        nc.gpsimd.tensor_copy(xg[:, :, :], group_rows(rows, i)).then_inc(at, 1)

                @block.tensor
                def _(pe):
                    credit(pe, xt_free, 2)
                    credit(pe, mm_free, 2)
                    pe.wait_ge(ld, 160)
                    with nc.tensor.Fori(0, NG) as i:
                        transpose_rows(pe, i, at, xt_free, xt_ready)
                        for n in range(GRP):
                            pe.wait_ge(xt_free, i * GRP + n + 3)
                            for b in range(2):
                                pe.wait_ge(mm_free, i * GRP * 2 + n * 2 + b + 1)
                                for k in range(2):
                                    mm = nc.tensor.matmul(PS[b][:, :], xTg[:, k, n * P:(n + 1) * P], wq[:, k, b * 512:(b + 1) * 512], start=(k == 0), stop=(k == 1))
                                mm.then_inc(mm_ready, 1)

                @block.scalar
                def _(act):
                    with nc.scalar.Fori(0, NG) as i:
                        act.wait_ge(mm_ready, i * GRP * 2)
                        for n in range(GRP):
                            act.wait_ge(xt_ready, i * GRP + n + 1)
                            nc.scalar.copy(xTg[:, :, n * P:(n + 1) * P], PS[6 + n % 2][:, 0:2 * P].rearrange("p (k c) -> p k c", k=2)).then_inc(xt_free, 1)

                @block.vector
                def _(dve):
                    step = Chain(dve, dv)
                    dve.wait_ge(ld, 160)
                    nc.vector.tensor_tensor(bc_b[:, F:2 * F], bc_b[:, F:2 * F], bc_b2[:, 0:F], ALU.add)
                    step(nc.vector.tensor_tensor(bc_b[:, 2 * F:3 * F], bc_b[:, 2 * F:3 * F], bc_b2[:, 0:F], ALU.add))
                    with nc.vector.Fori(0, NG) as i:
                        dve.wait_ge(q_out, i * 48)
                        for n in range(GRP):
                            dve.wait_ge(mm_ready, (i * GRP + n) * 2 + 1)
                            nc.vector.tensor_tensor(g5[:, n, 0:512], PS[0][:, :], bc_b[:, 0:512], ALU.add).then_inc(mm_free, 1)
                            dve.wait_ge(mm_ready, (i * GRP + n) * 2 + 2)
                            nc.vector.tensor_tensor(H[:, ds(i * GRP + n, 1), :].rearrange("p a f -> p (a f)"), PS[1][:, F:2 * F], bc_b[:, 3 * F:4 * F], ALU.add)
                            nc.vector.tensor_tensor(g5[:, n, 2 * F:3 * F], PS[1][:, 0:F], bc_b[:, 2 * F:3 * F], ALU.add).then_inc(mm_free, 1)

        a_ready = [lasting_sem(f"a_ready{h}") for h in range(2)]
        a_base, w_base = [0], [0]
        attr = a["edge_attr_128"]

        def load_attributes(sp, i, half, end=False):
            t0 = i * BODY + half * HB
            sp.dma_start(arow[:, half * HB:(half + 1) * HB - 1, :],
                         attr[ds(t0 * P, (HB - 1) * P), :].rearrange("(t p) c -> p t c", p=P)).then_inc(a_ready[half], 16)
            n = E - (ET - 1) * P if end else P
            sp.dma_start(arow[0:n, (half + 1) * HB - 1, :], attr[ds((t0 + HB - 1) * P, n), :]).then_inc(a_ready[half], 16)

        def scores3(tag, layer):
            names = "idx_ready products begun oh_ready tr_ready tr_taken e_ready e_taken sum_ready dve".split()
            idx_ready, products, begun, oh_ready, tr_ready, tr_taken, e_ready, e_taken, sum_ready, dv = [sem(f"{tag}_{n}") for n in names]
            gb, ab, wb = g_base[0], a_base[0], w_base[0]
            with nc.Block() as block:
                @block.gpsimd
                def _(pool):
                    gather_rows(pool, k_tab, F, idx_ready, sum_ready, begun)

                @block.sync
                def _(sp):
                    def half_body(i, half, end=False):
                        t0 = i * BODY + half * HB
                        sp.wait_ge(tr_ready, t0)
                        load_attributes(sp, i, half, end)
                        _, first = nc.values_load_multi_w_load_instructions(
                            base_i[0:1, ds(t0, HB)], engines=[mybir.EngineType.SP], min_val=0, max_val=NP - 1)
                        for u in range(HB):
                            sp.wait_ge(products, t0 + u + 1)
                            sp.dma_start(qrow[:, u, :], q_tab[ds(first[u], P), :]).then_inc(q_ready[u], 16)
                    credit(sp, tr_ready, HB)
                    credit(sp, products, HB)
                    with nc.sync.Fori(0, TRIPS - 1) as i:
                        for half in range(2):
                            half_body(i, half)
                    half_body(TRIPS - 1, 0)
                    half_body(TRIPS - 1, 1, end=True)

                @block.scalar
                def _(act):
                    with nc.scalar.Fori(0, TRIPS) as i:
                        for half in range(2):
                            act.wait_ge(sum_ready, i * BODY + (half + 1) * HB)
                            nc.scalar.copy(idx_st[:, half, :], srcT[:, ds(i * BODY + half * HB, HB)]).then_inc(idx_ready, 1)
                            for u in range(HB):
                                t = i * BODY + half * HB + u
                                act.wait_ge(tr_ready, t + 1 + HB)
                                act.wait_ge(products, t + 1 + HB - 4)
                                nc.scalar.copy(aT[:, u % 4, :], PS[u % 2][:, 0:P])
                                nc.scalar.copy(ohT[:, u % 4, :], PS[u % 2][:, P:2 * P]).then_inc(tr_taken, 1)

                @block.tensor
                def _(pe):
                    credit(pe, tr_taken, 2)
                    credit(pe, e_taken, 2)

                    def transposes(i, s):
                        t = i * BODY + s
                        if s % HB == 0:
                            pe.wait_ge(a_ready[s // HB], (ab + i + 1) * 32)
                        pe.wait_ge(oh_ready, t + 1)
                        pe.wait_ge(tr_taken, t + 1)
                        nc.tensor.transpose(PS[s % 2][:, 0:P], arow[:, s, :], ident[:, :])
                        nc.tensor.transpose(PS[s % 2][:, P:2 * P], oh[:, s % HB, s // HB, :], ident[:, :]).then_inc(tr_ready, 1)

                    def terms(i, s):
                        t, u = i * BODY + s, s % 4
                        pe.wait_ge(tr_taken, t + 3)
                        pe.wait_ge(e_taken, t + 1)
                        pe.wait_ge(q_ready[s % HB], (wb + i * 2 + s // HB + 1) * 16)
                        nc.tensor.matmul(PS[2 + s % 2][:, 0:F], aT[:, u, :], we[:, :], start=True, stop=True)
                        nc.tensor.matmul(PS[4 + s % 2][:, 0:F], ohT[:, u, :], qrow[:, s % HB, :], start=True, stop=True).then_inc(products, 1)

                    with nc.tensor.Fori(0, TRIPS) as i:
                        transposes(i, 0)
                        for s in range(BODY):
                            if s + 1 < BODY:
                                transposes(i, s + 1)
                            terms(i, s)

                @block.vector
                def _(dve):
                    step = Chain(dve, dv)
                    with nc.vector.Fori(0, TRIPS) as i:
                        step.enter(i, BODY)
                        for s in range(BODY):
                            nc.vector.tensor_scalar(oh[:, s % HB, s // HB, :], iota_n[:, :], dloc[:, ds(i * BODY + s, 1)], None, ALU.is_equal).then_inc(oh_ready, 1)
                        for half in range(2):
                            t0 = i * BODY + half * HB
                            for u in range(HB):
                                s = half * HB + u
                                dve.wait_ge(products, t0 + u + 1 + HB)
                                dve.wait_ge(g_ready[s], (gb + i + 1) * 16)
                                step(nc.vector.tensor_tensor(both[:, u % 4, :], grow[:, s, 0:F], PS[2 + s % 2][:, 0:F], ALU.add))
                                nc.vector.tensor_tensor(both[:, u % 4, :], both[:, u % 4, :], PS[4 + s % 2][:, 0:F], ALU.mult).then_inc(e_taken, 1)
                                dve.wait_ge(e_taken, t0 + u + 3)
                                nc.vector.tensor_reduce(w_e[:, ds(t0 + u, 1), :].rearrange("p a h -> p (a h)"),
                                                        both[:, u % 4, :].rearrange("p (h c) -> p h c", h=H3), AX, ALU.add).then_inc(sum_ready, 1)
                        dve.wait_ge(sum_ready, i * BODY + 2 * BODY)
                    step.leave(TRIPS, BODY)
            a_base[0] += TRIPS
            w_base[0] += 2 * TRIPS

        def messages3(tag, layer):
            names = "idx_ready products oh_ready begun tr_ready tr_taken e_ready e_taken msg_ready win_free zeroed w_ready".split()
            idx_ready, products, oh_ready, begun, tr_ready, tr_taken, e_ready, e_taken, msg_ready, win_free, zeroed, w_ready = [sem(f"{tag}_{n}") for n in names]
            gb, ab = g_base[0], a_base[0]
            with nc.Block() as block:
                @block.gpsimd
                def _(pool):
                    gather_rows(pool, v_tab, F, idx_ready, e_taken, begun)

                @block.sync
                def _(sp):
                    def half_body(i, half, end=False):
                        sp.wait_ge(tr_ready, i * BODY + half * HB + HB)
                        load_attributes(sp, i, half, end)
                    credit(sp, tr_ready, BODY)
                    with nc.sync.Fori(0, TRIPS - 1) as i:
                        for half in range(2):
                            half_body(i, half)
                    half_body(TRIPS - 1, 0)
                    half_body(TRIPS - 1, 1, end=True)

                @block.scalar
                def _(act):
                    with nc.scalar.Fori(0, TRIPS) as i:
                        for half in range(2):
                            act.wait_ge(e_taken, i * BODY + (half + 1) * HB)
                            nc.scalar.copy(idx_st[:, half, :], srcT[:, ds(i * BODY + half * HB, HB)]).then_inc(idx_ready, 1)
                            for u in range(HB):
                                t = i * BODY + half * HB + u
                                act.wait_ge(tr_ready, t + 1 + BODY)
                                act.wait_ge(e_ready, t + 1)
                                nc.scalar.copy(aT[:, u % 4, :], PS[4 + u % 2][:, 0:P]).then_inc(tr_taken, 1)

                @block.tensor
                def _(pe):
                    credit(pe, tr_taken, 2)
                    credit(pe, win_free, 2)
                    credit(pe, e_ready, 4)

                    def transposes(i, s):
                        t = i * BODY + s
                        if s % HB == 0:
                            pe.wait_ge(a_ready[s // HB], (ab + i + 1) * 32)
                        pe.wait_ge(tr_taken, t + 1)
                        nc.tensor.transpose(PS[4 + s % 2][:, 0:P], arow[:, s, :], ident[:, :]).then_inc(tr_ready, 1)

                    def edge_term(i, s):
                        t = i * BODY + s
                        pe.wait_ge(tr_taken, t + 3)
                        pe.wait_ge(e_taken, t + BODY - 1)
                        nc.tensor.matmul(PS[2 + s % 2][:, 0:F], aT[:, s % 4, :], we[:, :], start=True, stop=True).then_inc(e_ready, 1)

                    def window(i, s):
                        t = i * BODY + s
                        pe.wait_ge(msg_ready, t + 1)
                        pe.wait_ge(win_free, t + 1)
                        pe.wait_ge(oh_ready, t + 1)
                        for half in range(2):
                            mm = nc.tensor.matmul(PS[s % 2][:, half * P:(half + 1) * P], both[:, s % 4, half * P:(half + 1) * P], oh[:, s % HB, 0, :], start=True, stop=True)
                        mm.then_inc(products, 1)

                    with nc.tensor.Fori(0, TRIPS) as i:
                        transposes(i, 0)
                        transposes(i, 1)
                        edge_term(i, 0)
                        for s in range(BODY):
                            if s + 2 < BODY:
                                transposes(i, s + 2)
                            if s + 1 < BODY:
                                edge_term(i, s + 1)
                            window(i, s)

                @block.vector
                def _(dve):
                    nc.vector.memset(acc[:, 0:2, :], 0.0).then_inc(zeroed, 1)
                    dve.wait_ge(zeroed, 1)
                    with nc.vector.Fori(0, TRIPS) as i:
                        for half in range(2):
                            t0 = i * BODY + half * HB
                            _, first = nc.values_load_multi_w_load_instructions(
                                base_i[0:1, ds(t0, HB)], engines=[mybir.EngineType.DVE], min_val=0, max_val=NP - 1)

                            def add_window(u):
                                dve.wait_ge(products, t0 + u + 1)
                                dve.wait_ge(win_free, t0 + u + 2)
                                window = acc[:, 0:2, ds(first[u], P)]
                                nc.vector.tensor_tensor(window, window, PS[u % 2][:, 0:2 * P].rearrange("p (s n) -> p s n", s=2), ALU.add).then_inc(win_free, 1)

                            for u in range(HB):
                                nc.vector.tensor_scalar(oh[:, u, 0, :], iota_n[:, :], dloc[:, ds(t0 + u, 1)], None, ALU.is_equal).then_inc(oh_ready, 1)
                            for u in range(HB):
                                s = half * HB + u
                                dve.wait_ge(e_ready, t0 + u + 5)
                                dve.wait_ge(g_ready[s], (gb + i + 1) * 16)
                                msg = both[:, u % 4, :]
                                nc.vector.tensor_tensor(msg, grow[:, s, 0:F], PS[2 + s % 2][:, 0:F], ALU.add).then_inc(e_taken, 1)
                                dve.wait_ge(e_taken, t0 + u + 1 + BODY)
                                m4 = msg.rearrange("p (h c) -> p h c", h=H3)
                                nc.vector.tensor_tensor(m4, m4, w_e[:, ds(t0 + u, 1), :].rearrange("p a h -> p (a h)").unsqueeze(2).broadcast_to([P, H3, C3]),
                                                        ALU.mult).then_inc(msg_ready, 1)
                                if u >= 1:
                                    add_window(u - 1)
                            add_window(HB - 1)
            a_base[0] += TRIPS

        def finish3(tag, last_layer):
            at, free, back, var_ready, std_ready, y_ready, y_out, dv = [
                sem(f"{tag}_{n}") for n in "at free back var_ready std_ready y_ready y_out dve".split()]
            with nc.Block() as block:
                @block.gpsimd
                def _(pool):
                    with nc.gpsimd.Fori(0, NG) as i:
                        pool.wait_ge(free, i * GRP)
                        for s in range(2):
                            last = nc.gpsimd.tensor_copy(accg[:, s, :], acc[:, s, ds(i * GRP * P, GRP * P)])
                        last.then_inc(at, 1)

                @block.tensor
                def _(pe):
                    credit(pe, back, GRP)
                    with nc.tensor.Fori(0, NG) as i:
                        pe.wait_ge(at, i + 1)
                        for n in range(GRP):
                            pe.wait_ge(back, i * GRP + n + 1)
                            for s in range(2):
                                mm = nc.tensor.transpose(PS[n][:, s * P:(s + 1) * P], accg[:, s, n * P:(n + 1) * P], ident[:, :])
                            mm.then_inc(free, 1)

                @block.vector
                def _(dve):
                    step = Chain(dve, dv)
                    rows = stage[:, 0, :, :]
                    with nc.vector.Fori(0, NG) as i:
                        step.enter(i, 7 if last_layer else 1)
                        for n in range(GRP):
                            dve.wait_ge(free, i * GRP + n + 1)
                            nc.vector.tensor_tensor(rows[:, n, :], PS[n][:, 0:F], H[:, ds(i * GRP + n, 1), :].rearrange("p a f -> p (a f)"), ALU.add).then_inc(back, 1)
                        dve.wait_ge(back, (i + 2) * GRP)
                        if last_layer:
                            step(nc.vector.tensor_tensor(rows, rows, group_rows(X, i), ALU.add))
                            layer_norm(dve, step, rows, group_rows(X, i), var_ready, std_ready, i + 1).then_inc(y_ready, 1)
                            dve.wait_ge(y_ready, i + 1)
                        else:
                            step(nc.vector.tensor_scalar(group_rows(H, i), rows, 0.0, None, ALU.max))
                    step.leave(NG, 7 if last_layer else 1)

                if last_layer:
                    @block.scalar
                    def _(act):
                        with nc.scalar.Fori(0, NG) as i:
                            act_root(act, var_ready, std_ready, i + 1)

                    @block.sync
                    def _(sp):
                        sp.wait_ge(y_ready, NG)
                        sp.dma_start(out[0:(NT - 1) * P, :].rearrange("(t p) f -> p t f", p=P), X[:, 0:NT - 1, :]).then_inc(y_out, 16)
                        sp.dma_start(out[(NT - 1) * P:N, :], X[0:TAIL, NT - 1, :]).then_inc(y_out, 16)
                        sp.wait_ge(y_out, 32)

        phases = [setup, project0, lambda: look_up("l0", [(1, 0, 2, 0)]),
                  lambda: aggregate("a0", h_tab, F + 2, "gat"), finish0,
                  lambda: aggregate("a1", x_tab, F, "rel"), finish1, project2,
                  lambda: look_up("l2", [(0, 0, 1, 0), (1, 1, 1, 1)]),
                  lambda: sum_scores(), lambda: edge_softmax("s2", 1, 1.0, 1.0e-10, -1.0e9, lambda h: s_e[:, :, 0]),
                  lambda: aggregate("a2", h2_tab, F, "one"), finish2,
                  lambda: project3(1, X), lambda: scores3("s31", 1),
                  lambda: edge_softmax("x31", H3, 0.125, 1.0e-16, None, lambda h: w_e[:, :, h]),
                  lambda: messages3("m31", 1), lambda: finish3("f31", False),
                  lambda: project3(2, H), lambda: scores3("s32", 2),
                  lambda: edge_softmax("x32", H3, 0.125, 1.0e-16, None, lambda h: w_e[:, :, h]),
                  lambda: messages3("m32", 2), lambda: finish3("f32", True)]
        for n, phase in enumerate(phases):
            if n < stop:
                phase()
                end_of_phase()
        if dump:
            d = lasting_sem("dumped")
            views = dict(X=X[:, :, :], dloc=dloc[:, :], srcT=srcT[:, :], s_tab=s_tab[:, :, :], s_e=s_e[:, :, :], acc=acc[:, :, 0:NP],
                         wbig=wbig[:, :, :, :], relw=relw[:, :], cont=cont[:, :], contn=contn[:, :], allr=allr[:, :, :], H=H[:, :, :],
                         h_tab=h_tab, w_e=w_e[:, :, 0:dump['w_e'].shape[2]] if 'w_e' in dump else None, x_tab=x_tab, k_tab=k_tab, v_tab=v_tab, q_tab=q_tab[0:NP, :], w2T=w2T[:, :, :])
            with nc.Block() as block:
                @block.sync
                def _(sp):
                    for n, o in enumerate(dump):
                        sp.dma_start(dump[o], views[o], allow_slow_non_contiguous=True).then_inc(d, 16)
                        sp.wait_ge(d, 16 * n + 16)


_INS = (["x", "src", "dst", "edge_attr_128", "edge_type_16", "L0_gnn_W1", "L0_gnn_a1", "L0_gnn_W2", "L0_gnn_a2",
         "L1_gnn_relvectors", "L1_gnn_w_ih", "L1_gnn_w_hh", "L1_gnn_b_ih", "L1_gnn_b_hh",
         "L2_gnn_W", "L2_gnn_b", "L2_gnn_mag_w", "L2_gnn_mag_b", "L2_gnn_attn_w"]
        + [f"L3_gnn_{m}{letter}{layer}" for layer in (1, 2) for letter in "qkves" for m in "Wb"])


def kernel(**inputs):
    import numpy as np
    from concourse import bacc
    from concourse.bass_utils import run_bass_kernel_spmd

    nc = bacc.Bacc("TRN2", target_bir_lowering=False, num_devices=1)
    arrays, args = {}, {}
    for name in _INS:
        arr = np.ascontiguousarray(inputs[name])
        arrays[f"in_{name}"] = arr
        args[name] = nc.dram_tensor(f"in_{name}", arr.shape, mybir.dt.from_np(arr.dtype), kind="ExternalInput").ap()
    out = nc.dram_tensor("out_nodes", (N, F), F32, kind="ExternalOutput").ap()
    graph_layers(nc, args, out)
    r = run_bass_kernel_spmd(nc, [arrays], core_ids=[0])
    return r.results[0]["out_nodes"]
```

```python
from contextlib import ExitStack

import concourse.bass as bass
from concourse import mybir

F32 = mybir.dt.float32
I32 = mybir.dt.int32
BF16 = mybir.dt.bfloat16
ALU = mybir.AluOpType
ACT = mybir.ActivationFunctionType
AX = mybir.AxisListType.X

P = 128
N, F = 3125, 256
E = 53125
NT = -(-N // P)
NP = NT * P
ET = 416
EP = ET * P
CL = 512
CP = EP // CL
J = CL // P
LOHI = P
NH = NP // P
HB = 8
BODY = 2 * HB
TRIPS = ET // BODY
GRP = 5
NG = NT // GRP
ACCW = NP + P
PADN = NP - 1
BIG = 1.0e30
H3, C3 = 4, 64
ED = 128
NREL = 16
TAIL = N - (NT - 1) * P
ETAIL = E - (CP - 1) * CL


class Chain:

    def __init__(self, eng, sem):
        self.eng, self.sem, self.base, self.n = eng, sem, 0, 0

    def __call__(self, ins):
        self.n += 1
        ins.then_inc(self.sem, 1)
        self.eng.wait_ge(self.sem, self.base + self.n)

    def enter(self, i, per_trip):
        self.start = self.base + self.n
        self.base, self.n = self.start + i * per_trip, 0

    def leave(self, trips, per_trip):
        assert self.n == per_trip, (self.n, per_trip)
        self.base, self.n = self.start + trips * per_trip, 0


def graph_layers(nc, a, out, dump=None, stop=99):
    ctx = ExitStack()
    with ctx:
        def sb(name, shape, dt=F32):
            return ctx.enter_context(nc.sbuf_tensor(name, shape, dt))

        phase_sems = []

        def lasting_sem(name):
            return ctx.enter_context(nc.semaphore(name))

        def sem(name):
            phase_sems.append(nc.alloc_semaphore(name=name))
            return phase_sems[-1]

        def end_of_phase():
            nc.clear_and_free_semaphores(list(phase_sems))
            phase_sems.clear()
            nc.all_engine_barrier()

        def dram(name, shape, dt=F32):
            return nc.dram_tensor(name, shape, dt, kind="Internal").ap()

        x_tab = dram("x_tab", [NP, F])
        h_tab = dram("h_tab", [NP, F + 2])
        h2_tab = dram("h2_tab", [NP, F])
        k_tab = dram("k_tab", [NP, F])
        v_tab = dram("v_tab", [NP, F])
        q_tab = dram("q_tab", [ACCW, F])
        lo_tab = dram("lo_tab", [3, EP], BF16)

        X = sb("X", [P, NT, F])
        H = sb("H", [P, NT, F])
        acc = sb("acc", [P, 3, ACCW])
        work = sb("work", [P, 13440])

        def carve(*shapes):
            at, views = 0, []
            for s in shapes:
                n = 1
                for d in s:
                    n *= d
                v = work[:, at:at + n]
                names = " ".join("abcd"[:len(s)])
                if len(s) > 1:
                    v = v.rearrange(f"p ({names}) -> p {names}", **dict(zip("abcd", s)))
                views.append(v)
                at += n
            assert at <= 13440, at
            return views

        accg, xg, xTg, g5, stage = carve((3, GRP * P), (GRP, F), (2, GRP * P), (GRP, 1024), (3, GRP, F))
        grow, qrow, oh, arow, aT, places, both = carve((BODY, F + 2), (HB, F), (2, HB, P), (BODY, ED), (4, P), (2, HB * P // 2), (4, F))
        wbig = sb("wbig", [P, 2, 2, 768])
        ident = sb("ident", [P, P])
        iota_n = sb("iota_n", [P, P])
        iota_p = sb("iota_p", [P, 1])
        sel = sb("sel", [P, 2, P])
        ones = sb("ones", [1, P])
        srcT = sb("srcT", [P, ET + BODY], I32)
        dstT = sb("dstT", [P, ET])
        dloc = sb("dloc", [P, ET])
        typT = sb("typT", [P, ET])
        hiT = sb("hiT", [P, 2, ET])
        base_i = sb("base_i", [1, ET], I32)
        idx_st = sb("idx_st", [P, 2, HB], I32)
        w_e = sb("w_e", [P, ET, H3])
        w_flat = w_e[:, :, :].rearrange("p t h -> p (t h)")
        w0 = w_flat[:, 0:2 * F].rearrange("p (k f) -> p k f", k=2)
        bc_a = w_flat[:, 2 * F:2 * F + 4 * P].rearrange("p (a c) -> p a c", a=4)
        relr = w_flat[0:NREL, 2 * F + 4 * P:3 * F + 4 * P]
        s_e = sb("s_e", [P, ET, 2])
        cont = sb("cont", [CP, CL])
        contn = sb("contn", [CP, CL])
        notn = sb("notn", [CP, CL])
        pen = sb("pen", [CP, CL])
        ends = sb("ends", [CP, 2], I32)
        endf = sb("endf", [CP, 2])
        all4 = sb("all4", [CP, 2, H3])
        allr = sb("allr", [H3, 3, CP])
        lastv = sb("lastv", [CP, H3])
        rowc = sb("rowc", [H3, 2, CP + 1])
        carry = sb("carry", [CP, H3])
        s_tab = sb("s_tab", [P, NT, 2])
        s_rem = sb("s_rem", [P, NT, 2])
        s_bf = sb("s_bf", [P, 3, 2, NT], BF16)
        w2T = sb("w2T", [P, 2, F + 1])
        bc_a2 = sb("bc_a2", [P, 2, F])
        bc_b = sb("bc_b", [P, 1024])
        bc_b2 = sb("bc_b2", [P, F + 1])
        bc_t = sb("bc_t", [P, 1024])
        relw = sb("relw", [NREL, 768])
        relT = sb("relT", [P, 2, NREL])
        small = sb("small", [P, 16, GRP])
        we = sb("we", [ED, F])

        PS = [ctx.enter_context(nc.psum_tensor(f"bank{i}", [P, 512], F32)) for i in range(8)]

        accf = acc[:, :, :].rearrange("p a b -> p (a b)")

        def ds(start, n):
            return bass.ds(start, n)

        g_ready = [lasting_sem(f"g_ready{u}") for u in range(BODY)]
        q_ready = [lasting_sem(f"q_ready{u}") for u in range(HB)]
        g_base, q_base = [0], [0]

        def setup():
            ld_w, ld_i, ld_x, ld_e = sem("ld_w"), sem("ld_i"), sem("ld_x"), sem("ld_e")
            padded, consts = sem("padded"), sem("consts")
            dv, pl = sem("setup_dve"), sem("setup_pool")
            floats_ready, t_ready, t_taken = sem("floats_ready"), sem("t_ready"), sem("t_taken")
            lo_ready, lo_out = sem("lo_ready"), sem("lo_out")
            wt_ready, wt_taken = sem("wt_ready"), sem("wt_taken")
            zrow_ready = sem("zrow_ready")
            base_ready, base_done, rows_ready, rows_done = sem("base_ready"), sem("base_done"), sem("rows_ready"), sem("rows_done")
            rel_ready, rel_taken, relw_ready = sem("rel_ready"), sem("rel_taken"), sem("relw_ready")

            wih_r = accf[:, 0:1536].rearrange("p (o k) -> p o k", o=6)
            whh_r = accf[:, 1536:3072].rearrange("p (o k) -> p o k", o=6)
            w2_r = accf[:, 3072:3584].rearrange("p (o k) -> p o k", o=2)
            I = accf[0:CP, 3584:5120].bitcast(I32).rearrange("p (a e) -> p a e", a=3)
            Ff = accf[0:CP, 5120:7680].rearrange("p (a e) -> p a e", a=5)
            LH = accf[0:CP, 7680:9728].bitcast(I32).rearrange("p (a e) -> p a e", a=4)
            lo_b = stage[0:CP, 0, 0:4, :].rearrange("p a e -> p (a e)").bitcast(BF16)[:, 0:3 * CL].rearrange("p (a e) -> p a e", a=3)
            names = ("src", "dst", "edge_type_16")

            with nc.Block() as block:
                @block.sync
                def _(sp):
                    sp.dma_start(wih_r, a["L1_gnn_w_ih"].rearrange("(o p) k -> p o k", p=P)).then_inc(ld_w, 16)
                    sp.dma_start(whh_r, a["L1_gnn_w_hh"].rearrange("(o p) k -> p o k", p=P)).then_inc(ld_w, 16)
                    sp.dma_start(w2_r, a["L2_gnn_W"].rearrange("(o p) k -> p o k", p=P)).then_inc(ld_w, 16)
                    sp.dma_start(relr, a["L1_gnn_relvectors"]).then_inc(ld_w, 16)
                    sp.wait_ge(padded, 1)
                    for n, name in enumerate(names):
                        whole = (CP - 1) * CL
                        sp.dma_start(I[0:CP - 1, n, :], a[name][0:whole].rearrange("(p e) -> p e", e=CL)).then_inc(ld_i, 16)
                        sp.dma_start(I[CP - 1:CP, n, 0:ETAIL], a[name][whole:E].unsqueeze(0)).then_inc(ld_i, 16)
                    sp.dma_start(ends[1:CP - 1, 0:1], a["dst"][CL - 1:CL - 1 + (CP - 2) * CL].rearrange("(p e) -> p e", e=CL)[:, 0:1],
                                 allow_slow_non_contiguous=True).then_inc(ld_e, 16)
                    sp.dma_start(ends[CP - 1:CP, 0:1], a["dst"][(CP - 1) * CL - 1:(CP - 1) * CL].unsqueeze(0)).then_inc(ld_e, 16)
                    sp.dma_start(ends[0:CP - 2, 1:2], a["dst"][CL:CL + (CP - 2) * CL].rearrange("(p e) -> p e", e=CL)[:, 0:1],
                                 allow_slow_non_contiguous=True).then_inc(ld_e, 16)
                    sp.dma_start(ends[CP - 2:CP - 1, 1:2], a["dst"][(CP - 1) * CL:(CP - 1) * CL + 1].unsqueeze(0)).then_inc(ld_e, 16)
                    sp.dma_start(X[:, 0:NT - 1, :], a["x"][0:(NT - 1) * P, :].rearrange("(t p) f -> p t f", p=P)).then_inc(ld_x, 16)
                    sp.dma_start(X[0:TAIL, NT - 1, :], a["x"][(NT - 1) * P:N, :]).then_inc(ld_x, 16)
                    sp.dma_start(w0[:, :, 0:P], a["L0_gnn_W1"].rearrange("(k p) f -> p k f", p=P)).then_inc(ld_x, 16)
                    sp.dma_start(w0[:, :, P:F], a["L0_gnn_W2"].rearrange("(k p) f -> p k f", p=P)).then_inc(ld_x, 16)
                    for n, name in enumerate(("L0_gnn_a1", "L0_gnn_a2")):
                        sp.dma_start(bc_a[:, 2 * n:2 * n + 2, :].rearrange("p a c -> p (a c)"), a[name].broadcast_to([P, F])).then_inc(ld_x, 16)
                    for n in range(2):
                        sp.dma_start(bc_a2[:, n, :], a["L2_gnn_attn_w"][:, n * F:(n + 1) * F].broadcast_to([P, F])).then_inc(ld_x, 16)
                    sp.dma_start(bc_b2[:, 0:F], a["L2_gnn_b"].unsqueeze(0).broadcast_to([P, F])).then_inc(ld_x, 16)
                    sp.dma_start(bc_b2[:, F:F + 1], a["L2_gnn_mag_b"].unsqueeze(0).broadcast_to([P, 1])).then_inc(ld_x, 16)
                    for k in range(2):
                        sp.dma_start(w2T[:, k, F:F + 1], a["L2_gnn_mag_w"][0:1, k * P:(k + 1) * P].rearrange("a p -> p a"),
                                     allow_slow_non_contiguous=True).then_inc(ld_x, 16)
                    sp.dma_start(bc_t[:, 0:768], a["L1_gnn_b_ih"].unsqueeze(0).broadcast_to([P, 768])).then_inc(ld_x, 16)
                    sp.dma_start(bc_b[:, 0:768], a["L1_gnn_b_hh"].unsqueeze(0).broadcast_to([P, 768])).then_inc(ld_x, 16)
                    sp.wait_ge(lo_ready, 1)
                    for n in range(3):
                        sp.dma_start(lo_tab[n, :].rearrange("(p e) -> p e", e=CL), lo_b[:, n, :]).then_inc(lo_out, 16)
                    sp.dma_start(q_tab[NP:ACCW, :], qrow[:, 0, :]).then_inc(lo_out, 16)
                    sp.wait_ge(lo_out, 64)
                    sp.wait_ge(ld_w, 16 * 4)
                    sp.wait_ge(ld_x, 16 * 14)

                @block.gpsimd
                def _(pool):
                    nc.gpsimd.iota(iota_n[:, :], pattern=[[1, P]], base=0, channel_multiplier=0, allow_small_or_imprecise_dtypes=True)
                    nc.gpsimd.iota(iota_p[:, :], pattern=[[1, 1]], base=0, channel_multiplier=1, allow_small_or_imprecise_dtypes=True)
                    nc.gpsimd.memset(sel[:, :, :], 0.0)
                    nc.gpsimd.memset(ident[:, :], 0.0).then_inc(pl, 1)
                    pool.wait_ge(pl, 1)
                    nc.gpsimd.affine_select(out=ident[:, :], in_=ident[:, :], compare_op=ALU.not_equal, fill=1.0, base=0,
                                            pattern=[[-1, P]], channel_multiplier=1)
                    for h in range(2):
                        nc.gpsimd.memset(sel[:, h, h:h + 1], 1.0)
                    nc.gpsimd.memset(ones[:, :], 1.0).then_inc(consts, 1)

                @block.vector
                def _(dve):
                    step = Chain(dve, dv)
                    nc.vector.memset(qrow[:, 0, :], 0.0)
                    nc.vector.memset(I[:, 0, :], 0)
                    nc.vector.memset(I[:, 1, :], PADN)
                    nc.vector.memset(I[:, 2, :], 0)
                    nc.vector.memset(ends[:, :], -1)
                    nc.vector.memset(srcT[:, ET:ET + BODY], 0)
                    nc.vector.memset(X[:, NT - 1, :], 0.0).then_inc(padded, 1)
                    dve.wait_ge(ld_i, 16 * 6)
                    nc.vector.tensor_scalar(LH[:, 0:2, :], I[:, 0:2, :], 7, None, ALU.logical_shift_right)
                    step(nc.vector.tensor_scalar(LH[:, 2:4, :], I[:, 0:2, :], LOHI - 1, None, ALU.bitwise_and))
                    nc.vector.tensor_copy(Ff[:, 0:3, :], I[:, :, :])
                    nc.vector.tensor_copy(Ff[:, 3:5, :], LH[:, 0:2, :]).then_inc(floats_ready, 1)
                    nc.vector.tensor_copy(lo_b[:, 0:2, :], LH[:, 2:4, :])
                    dve.wait_ge(floats_ready, 1)
                    dst4 = Ff[:, 1, :].rearrange("p (j c) -> p j c", j=J)
                    nc.vector.tensor_tensor(lo_b[:, 2, :].rearrange("p (j c) -> p j c", j=J), dst4, dst4[:, :, 0:1].broadcast_to([CP, J, P]),
                                            ALU.subtract).then_inc(lo_ready, 1)
                    dve.wait_ge(ld_e, 64)
                    step(nc.vector.tensor_copy(endf[:, :], ends[:, :]))
                    nc.vector.tensor_tensor(cont[:, 1:CL], Ff[:, 1, 1:CL], Ff[:, 1, 0:CL - 1], ALU.is_equal)
                    nc.vector.tensor_tensor(cont[:, 0:1], Ff[:, 1, 0:1], endf[:, 0:1], ALU.is_equal)
                    nc.vector.tensor_tensor(contn[:, 0:CL - 1], Ff[:, 1, 1:CL], Ff[:, 1, 0:CL - 1], ALU.is_equal)
                    step(nc.vector.tensor_tensor(contn[:, CL - 1:CL], Ff[:, 1, CL - 1:CL], endf[:, 1:2], ALU.is_equal))
                    nc.vector.tensor_scalar(notn[:, :], contn[:, :], -1.0, 1.0, ALU.mult, ALU.add)
                    nc.vector.tensor_scalar(pen[:, :], cont[:, :], BIG, -BIG, ALU.mult, ALU.add)
                    nc.vector.tensor_reduce(all4[:, 0, 0:1], cont[:, :], AX, ALU.min)
                    step(nc.vector.tensor_reduce(all4[:, 1, 0:1], contn[:, :], AX, ALU.min))
                    for n in range(2):
                        last = nc.vector.tensor_copy(all4[:, n, 1:H3], all4[:, n, 0:1].broadcast_to([CP, H3 - 1]))
                    last.then_inc(rows_ready, 1)
                    for n in range(5):
                        dve.wait_ge(t_ready, n + 1)
                        dst_ap = (srcT[:, 0:ET], dstT[:, :], typT[:, :], hiT[:, 0, :], hiT[:, 1, :])[n]
                        nc.vector.tensor_copy(dst_ap.rearrange("q (p j) -> q j p", j=J),
                                              PS[n % 2][:, 0:ET].rearrange("q (j p) -> q j p", j=J)).then_inc(t_taken, 1)
                    dve.wait_ge(t_taken, 5)
                    nc.vector.tensor_copy(base_i[:, :], dstT[0:1, :]).then_inc(base_ready, 1)
                    dve.wait_ge(base_done, 1)
                    nc.vector.tensor_tensor(dloc[:, :], dstT[:, :], PS[2][:, 0:ET], ALU.subtract)
                    dve.wait_ge(rows_done, 1)
                    step(nc.vector.tensor_copy(allr[:, 0:2, :], PS[3][0:H3, 0:2 * CP].rearrange("h (n p) -> h n p", n=2)))
                    nc.vector.tensor_scalar(allr[:, 2, :], allr[:, 0, :], BIG, -BIG, ALU.mult, ALU.add)

                @block.tensor
                def _(pe):
                    pe.wait_ge(consts, 1)
                    pe.wait_ge(floats_ready, 1)
                    for n in range(5):
                        if n >= 2:
                            pe.wait_ge(t_taken, n - 1)
                        for j in range(J):
                            mm = nc.tensor.transpose(PS[n % 2][:, j * CP:(j + 1) * CP], Ff[:, n, j * P:(j + 1) * P], ident[0:CP, 0:CP])
                        mm.then_inc(t_ready, 1)
                    pe.wait_ge(t_taken, 2)
                    pe.wait_ge(base_ready, 1)
                    nc.tensor.matmul(PS[2][:, 0:ET], ones[:, :], dstT[0:1, :], start=True, stop=True).then_inc(base_done, 1)
                    pe.wait_ge(rows_ready, 1)
                    for n in range(2):
                        mm = nc.tensor.transpose(PS[3][0:H3, n * CP:(n + 1) * CP], all4[:, n, :], ident[0:CP, 0:CP])
                    mm.then_inc(rows_done, 1)
                    pe.wait_ge(ld_w, 64)
                    n = 0
                    for m, rows in enumerate((wih_r, whh_r)):
                        for k in range(2):
                            for half in range(2):
                                if n >= 2:
                                    pe.wait_ge(wt_taken, n - 1)
                                for o in range(3):
                                    mm = nc.tensor.transpose(PS[4 + n % 2][:, o * P:(o + 1) * P], rows[:, half * 3 + o, k * P:(k + 1) * P], ident[:, :])
                                mm.then_inc(wt_ready, 1)
                                n += 1
                    for k in range(2):
                        pe.wait_ge(wt_taken, n - 1)
                        for o in range(2):
                            mm = nc.tensor.transpose(PS[4 + n % 2][:, o * P:(o + 1) * P], w2_r[:, o, k * P:(k + 1) * P], ident[:, :])
                        mm.then_inc(wt_ready, 1)
                        n += 1
                    for k in range(2):
                        mm = nc.tensor.transpose(PS[6][:, k * NREL:(k + 1) * NREL], relr[:, k * P:(k + 1) * P], ident[0:NREL, 0:NREL])
                    mm.then_inc(rel_ready, 1)
                    pe.wait_ge(rel_taken, 1)
                    pe.wait_ge(wt_taken, 10)
                    for c0, c1, bank in ((0, 512, 4), (512, 768, 5)):
                        for k in range(2):
                            mm = nc.tensor.matmul(PS[bank][0:NREL, 0:c1 - c0], relT[:, k, :], wbig[:, 0, k, c0:c1], start=(k == 0), stop=(k == 1))
                    mm.then_inc(relw_ready, 1)

                @block.scalar
                def _(act):
                    n = 0
                    for m in range(2):
                        for k in range(2):
                            for half in range(2):
                                act.wait_ge(wt_ready, n + 1)
                                nc.scalar.copy(wbig[:, m, k, half * 384:(half + 1) * 384], PS[4 + n % 2][:, 0:384]).then_inc(wt_taken, 1)
                                n += 1
                    act.wait_ge(ld_x, 16 * 14)
                    for k in range(2):
                        act.wait_ge(wt_ready, n + 1)
                        nc.scalar.copy(w2T[:, k, 0:F], PS[4 + n % 2][:, 0:F]).then_inc(wt_taken, 1)
                        n += 1
                    act.wait_ge(rel_ready, 1)
                    nc.scalar.copy(relT[:, :, :], PS[6][:, 0:2 * NREL].rearrange("p (k r) -> p k r", k=2)).then_inc(rel_taken, 1)
                    act.wait_ge(relw_ready, 1)
                    nc.scalar.copy(relw[:, 0:512], PS[4][0:NREL, :])
                    nc.scalar.copy(relw[:, 512:768], PS[5][0:NREL, 0:256])


        def credit(eng, signal, n):
            eng.sem_inc(signal, n)

        def group_rows(t, i):
            return t[:, ds(i * GRP, GRP), :]

        def table_rows(tab, i, width=F):
            return tab[ds(i * GRP * P, GRP * P), :].rearrange("(t p) f -> p t f", p=P)

        def bc_last(ap, n):
            return ap.unsqueeze(2).broadcast_to([P, GRP, n])

        def layer_norm(dve, step, rows, to, var_ready, std_ready, count):
            mean, var = small[:, 0, :], small[:, 1, :]
            step(nc.vector.tensor_reduce(mean, rows, AX, ALU.add))
            step(nc.vector.tensor_scalar(mean, mean, 1.0 / F, None, ALU.mult))
            step(nc.vector.tensor_tensor(rows, rows, bc_last(mean, F), ALU.subtract))
            step(nc.vector.tensor_tensor(stage[:, 2, :, :], rows, rows, ALU.mult))
            step(nc.vector.tensor_reduce(var, stage[:, 2, :, :], AX, ALU.add))
            nc.vector.tensor_scalar(var, var, 1.0 / F, 1.0e-5, ALU.mult, ALU.add).then_inc(var_ready, 1)
            dve.wait_ge(std_ready, count)
            step(nc.vector.reciprocal(small[:, 3, :], small[:, 2, :]))
            return nc.vector.tensor_tensor(to, rows, bc_last(small[:, 3, :], F), ALU.mult)

        def act_root(act, var_ready, std_ready, count):
            act.wait_ge(var_ready, count)
            nc.scalar.activation(small[:, 2, :], small[:, 1, :], ACT.Sqrt).then_inc(std_ready, 1)

        def project0():
            names = "rows_at rows_free xt_ready xt_free xt_held h_ready h_free hrow_ready hrow_out hrow_free scal_dve".split()
            rows_at, rows_free, xt_ready, xt_free, xt_held, h_ready, h_free, hrow_ready, hrow_out, hrow_free, dv = [sem("p0_" + n) for n in names]
            hrow = g5[:, :, 0:F + 2]
            with nc.Block() as block:
                @block.gpsimd
                def _(pool):
                    with nc.gpsimd.Fori(0, NG) as i:
                        pool.wait_ge(rows_free, i * GRP)
                        nc.gpsimd.tensor_copy(xg[:, :, :], group_rows(X, i)).then_inc(rows_at, 1)

                @block.tensor
                def _(pe):
                    credit(pe, xt_free, 2)
                    credit(pe, h_free, GRP)
                    with nc.tensor.Fori(0, NG) as i:
                        pe.wait_ge(rows_at, i + 1)
                        for n in range(GRP):
                            pe.wait_ge(xt_free, i * GRP + n + 1)
                            for k in range(2):
                                mm = nc.tensor.transpose(PS[6 + n % 2][:, k * P:(k + 1) * P], xg[:, n, k * P:(k + 1) * P], ident[:, :])
                            mm.then_inc(rows_free, 1)
                        for n in range(GRP):
                            pe.wait_ge(xt_free, i * GRP + n + 3)
                            pe.wait_ge(h_free, i * GRP + n + 1)
                            for k in range(2):
                                mm = nc.tensor.matmul(PS[n][:, 0:F], xTg[:, k, n * P:(n + 1) * P], w0[:, k, :], start=(k == 0), stop=(k == 1))
                            mm.then_inc(h_ready, 1)

                @block.scalar
                def _(act):
                    with nc.scalar.Fori(0, NG) as i:
                        act.wait_ge(h_ready, i * GRP)
                        for n in range(GRP):
                            act.wait_ge(rows_free, i * GRP + n + 1)
                            nc.scalar.copy(xTg[:, :, n * P:(n + 1) * P], PS[6 + n % 2][:, 0:2 * P].rearrange("p (k c) -> p k c", k=2)).then_inc(xt_free, 1)
                        act.wait_ge(hrow_out, i * 16)
                        for n in range(GRP):
                            act.wait_ge(h_ready, i * GRP + n + 1)
                            last = nc.scalar.copy(hrow[:, n, 0:F], PS[n][:, 0:F])
                            last.then_inc(h_free, 1)

                @block.vector
                def _(dve):
                    step = Chain(dve, dv)
                    with nc.vector.Fori(0, NG) as i:
                        step.enter(i, 3)
                        dve.wait_ge(hrow_ready, i)
                        dve.wait_ge(h_free, (i + 2) * GRP)
                        for lr in range(2):
                            prod = stage[:, lr, :, :].rearrange("p t (h c) -> p t h c", h=2)
                            for h in range(2):
                                last = nc.vector.tensor_tensor(prod[:, :, h, :], hrow[:, :, h * P:(h + 1) * P],
                                                               bc_a[:, 2 * h + lr, :].unsqueeze(1).broadcast_to([P, GRP, P]), ALU.mult)
                            step(last)
                        step(nc.vector.tensor_reduce(s_tab[:, ds(i * GRP, GRP), 0:2], stage[:, 0, :, :].rearrange("p t (h c) -> p t h c", h=2), AX, ALU.add))
                        nc.vector.tensor_reduce(hrow[:, :, F:F + 2], stage[:, 1, :, :].rearrange("p t (h c) -> p t h c", h=2), AX, ALU.add).then_inc(hrow_ready, 1)
                    step.leave(NG, 3)
                    split3(step, 2)

                @block.sync
                def _(sp):
                    with nc.sync.Fori(0, NG) as i:
                        sp.wait_ge(hrow_ready, i + 1)
                        sp.dma_start(table_rows(h_tab, i), hrow).then_inc(hrow_out, 16)
                    sp.wait_ge(hrow_out, NG * 16)

        def split3(step, c):
            s = s_tab[:, :, 0:c]
            bf = lambda part: s_bf[:, part, 0:c, :].rearrange("p c t -> p t c")
            step(nc.vector.tensor_copy(bf(0), s))
            step(nc.vector.tensor_tensor(s_rem[:, :, 0:c], s, bf(0), ALU.subtract))
            step(nc.vector.tensor_copy(bf(1), s_rem[:, :, 0:c]))
            step(nc.vector.tensor_tensor(s_rem[:, :, 0:c], s_rem[:, :, 0:c], bf(1), ALU.subtract))
            step(nc.vector.tensor_copy(bf(2), s_rem[:, :, 0:c]))

        def look_up(tag, jobs):
            lo_at, oht_ready, mm_ready, taken, dv = [sem(f"{tag}_{n}") for n in "lo_at oht_ready mm_ready taken dve".split()]
            lo_even, lo_odd = sem(tag + "_lo_even"), sem(tag + "_lo_odd")
            lo_b = g5[:, 0:2, 0:512].bitcast(BF16)
            oht = g5[:, 2:4, 0:512].bitcast(BF16)
            ohh = stage[:, 0, :, :].rearrange("p a b -> p (a b)")[:, 0:HB * NH].rearrange("p (u t) -> p u t", u=HB)
            prod = stage[:, 1:3, :, :].rearrange("p a b c -> p (a b c)")
            with nc.Block() as block:
                @block.sync
                def _(sp):
                    credit(sp, oht_ready, 2)
                    for jn, (end, c0, c, e0) in enumerate(jobs):
                        done = jn * ET // HB
                        with nc.sync.Fori(0, TRIPS) as i:
                            for half in range(2):
                                sp.wait_ge(oht_ready, done + i * 2 + half + 1)
                                sp.dma_start(lo_b[:, half, :], lo_tab[end:end + 1, ds((i * 2 + half) * HB * P, HB * P)].broadcast_to([P, HB * P])
                                             ).then_inc((lo_even, lo_odd)[half], 16)

                @block.vector
                def _(dve):
                    step = Chain(dve, dv)
                    for jn, (end, c0, c, e0) in enumerate(jobs):
                        done = jn * ET // HB
                        pr = prod[:, 0:HB * c * NH].rearrange("p (u c t) -> p u c t", u=HB, c=c)
                        with nc.vector.Fori(0, TRIPS) as i:
                            step.enter(i, 4)
                            for half in range(2):
                                dve.wait_ge((lo_even, lo_odd)[half], (done // 2 + i + 1) * 16)
                                nc.vector.tensor_scalar(oht[:, half, :], lo_b[:, half, :], iota_p[:, 0:1], None, ALU.is_equal).then_inc(oht_ready, 1)
                            for half in range(2):
                                t0 = i * BODY + half * HB
                                step(nc.vector.tensor_tensor(ohh, iota_n[:, 0:NH].unsqueeze(1).broadcast_to([P, HB, NH]),
                                                             hiT[:, end, ds(t0, HB)].unsqueeze(2).broadcast_to([P, HB, NH]), ALU.is_equal))
                                dve.wait_ge(mm_ready, done + i * 2 + half + 1)
                                ps = PS[half][:, 0:HB * c * NH].rearrange("p (u c t) -> p u c t", u=HB, c=c)
                                for cc in range(c):
                                    last = nc.vector.tensor_tensor(pr[:, :, cc, :], ps[:, :, cc, :], ohh, ALU.mult)
                                step(last)
                                nc.vector.tensor_reduce(s_e[:, ds(t0, HB), e0:e0 + c], pr, AX, ALU.add).then_inc(taken, 1)
                                dve.wait_ge(taken, done + i * 2 + half + 1)
                        step.leave(TRIPS, 4)

                @block.tensor
                def _(pe):
                    for jn, (end, c0, c, e0) in enumerate(jobs):
                        done = jn * ET // HB
                        with nc.tensor.Fori(0, TRIPS) as i:
                            for half in range(2):
                                pe.wait_ge(oht_ready, done + i * 2 + half + 3)
                                pe.wait_ge(taken, done + i * 2)
                                for u in range(HB):
                                    for part in range(3):
                                        mm = nc.tensor.matmul(PS[half][:, u * c * NH:(u + 1) * c * NH], oht[:, half, u * P:(u + 1) * P],
                                                              s_bf[:, part, c0:c0 + c, :], start=(part == 0), stop=(part == 2))
                                mm.then_inc(mm_ready, 1)


        def gather_rows(pool, tab, width, idx_ready, rows_used, begun, per=1):
            base = g_base[0]
            credit(pool, rows_used, BODY // per)
            with nc.gpsimd.Fori(0, TRIPS) as i:
                for s in range(BODY):
                    if s % HB == 0:
                        pool.wait_ge(idx_ready, i * 2 + s // HB + 1)
                    if s % per == 0:
                        pool.wait_ge(rows_used, i * (BODY // per) + s // per + 1)
                    pool.sem_inc(begun, 1)
                    nc.gpsimd.indirect_dma_start(out=grow[:, s, 0:width], out_offset=None, in_=tab,
                                                 in_offset=bass.IndirectOffsetOnAxis(ap=idx_st[:, s // HB, s % HB:s % HB + 1], axis=0)
                                                 ).then_inc(g_ready[s], 16)
            g_base[0] = base + TRIPS

        def first_indices(act, idx_ready):
            for half in range(2):
                nc.scalar.copy(idx_st[:, half, :], srcT[:, half * HB:(half + 1) * HB]).then_inc(idx_ready, 1)

        def next_indices(act, i, half, gb, idx_ready):
            for u in range(HB):
                act.wait_ge(g_ready[half * HB + u], (gb + i + 1) * 16)
            nc.scalar.copy(idx_st[:, half, :], srcT[:, ds((i + 1) * BODY + half * HB, HB)]).then_inc(idx_ready, 1)

        def window_starts(i0, eng):
            return nc.values_load_multi_w_load_instructions(base_i[0:1, ds(i0, HB)], engines=[eng], min_val=0, max_val=NP - 1,
                                                                 skip_runtime_bounds_check_because="every destination is a node")[1]

        def aggregate(tag, tab, width, mode):
            names = "idx_ready products begun z_ready w_ready oh_ready win_free zeroed dve".split()
            idx_ready, products, begun, z_ready, w_ready, oh_ready, win_free, zeroed, dv = [sem(f"{tag}_{n}") for n in names]
            slots = 2 if mode == "one" else 3
            gb = g_base[0]
            zl = both[:, 0, 0:2 * HB * 2].rearrange("p (h u c) -> p h u c", h=2, u=HB)
            wl = both[:, 1, 0:2 * HB * 2].rearrange("p (h u c) -> p h u c", h=2, u=HB)
            oh2 = oh[:, :, :, :].rearrange("p a u n -> p (a u) n").rearrange("p (u a) n -> p u a n", a=2)
            with nc.Block() as block:
                @block.gpsimd
                def _(pool):
                    gather_rows(pool, tab, width, idx_ready, products, begun)

                @block.scalar
                def _(act):
                    first_indices(act, idx_ready)
                    with nc.scalar.Fori(0, TRIPS) as i:
                        for half in range(2):
                            if mode == "gat":
                                act.wait_ge(z_ready, i * 2 + half + 1)
                                nc.scalar.activation(wl[:, half, :, :], zl[:, half, :, :], ACT.Exp, scale=-1.0).then_inc(w_ready, 1)
                            next_indices(act, i, half, gb, idx_ready)

                @block.vector
                def _(dve):
                    nc.vector.memset(acc[:, :, :], 0.0).then_inc(zeroed, 1)
                    dve.wait_ge(zeroed, 1)
                    step = Chain(dve, dv)

                    def logits(i, half):
                        for u in range(HB):
                            dve.wait_ge(g_ready[half * HB + u], (gb + i + 1) * 16)
                        step(nc.vector.tensor_tensor(zl[:, half, :, :], grow[:, half * HB:(half + 1) * HB, F:F + 2],
                                                     s_e[:, ds(i * BODY + half * HB, HB), :], ALU.add))
                        nc.vector.scalar_tensor_tensor(zl[:, half, :, :], zl[:, half, :, :], 0.2, zl[:, half, :, :],
                                                       ALU.mult, ALU.max).then_inc(z_ready, 1)

                    def one_hot(i, half, u):
                        t = i * BODY + half * HB + u
                        d = dloc[:, ds(t, 1)]
                        if mode == "gat":
                            if u == 0:
                                dve.wait_ge(w_ready, i * 2 + half + 1)
                            for h in range(2):
                                last = nc.vector.tensor_scalar(oh2[:, u, h, :], iota_n[:, :], d, wl[:, half, u, h:h + 1],
                                                               ALU.is_equal, ALU.mult)
                        elif mode == "rel":
                            nc.vector.tensor_scalar(oh2[:, u, 0, :], iota_n[:, :], d, None, ALU.is_equal)
                            last = nc.vector.tensor_scalar(oh2[:, u, 1, :], iota_n[:, :], typT[:, ds(t, 1)], None, ALU.is_equal)
                        else:
                            last = nc.vector.tensor_scalar(oh2[:, u, 0, :], iota_n[:, :], d, w_e[:, ds(t, 1), 0:1].rearrange("p a b -> p (a b)"),
                                                           ALU.is_equal, ALU.mult)
                        last.then_inc(oh_ready, 1)

                    def add_window(i, half, u, first):
                        t = i * BODY + half * HB + u
                        dve.wait_ge(products, t + 1 + BODY)
                        dve.wait_ge(win_free, t + HB)
                        window = acc[:, 0:slots, ds(first[u], P)]
                        nc.vector.tensor_tensor(window, window, PS[u][:, 0:slots * P].rearrange("p (s n) -> p s n", s=slots),
                                                ALU.add).then_inc(win_free, 1)

                    def trip(i, end):
                        for half in range(2):
                            first = window_starts(i * BODY + half * HB, mybir.EngineType.DVE)
                            nxt = (i, 1) if half == 0 else None if end else (i + 1, 0)
                            if mode == "gat" and nxt:
                                logits(*nxt)
                            for u in range(HB):
                                add_window(i, half, u, first)
                                if nxt and (mode != "gat" or u):
                                    one_hot(*nxt, u - (mode == "gat"))
                            if nxt and mode == "gat":
                                one_hot(*nxt, HB - 1)

                    if mode == "gat":
                        logits(0, 0)
                    for u in range(HB):
                        one_hot(0, 0, u)
                    per = 2 if mode == "gat" else 0
                    with nc.vector.Fori(0, TRIPS - 1) as i:
                        step.enter(i, per)
                        trip(i, False)
                    step.leave(TRIPS - 1, per)
                    trip(TRIPS - 1, True)

                @block.tensor
                def _(pe):
                    credit(pe, win_free, HB)
                    with nc.tensor.Fori(0, TRIPS) as i:
                        for s in range(BODY):
                            u = s % HB
                            pe.wait_ge(g_ready[s], (gb + i + 1) * 16)
                            pe.wait_ge(oh_ready, i * BODY + s + 1)
                            pe.wait_ge(win_free, i * BODY + s + 1)
                            ps = PS[u]
                            for half in range(2):
                                rhs = oh2[:, u, half if mode == "gat" else 0, :]
                                mm = nc.tensor.matmul(ps[:, half * P:(half + 1) * P], grow[:, s, half * P:(half + 1) * P], rhs, start=True, stop=True)
                            if mode == "gat":
                                for h in range(2):
                                    mm = nc.tensor.matmul(ps[:, 2 * P:3 * P], sel[:, h, :], oh2[:, u, h, :], start=(h == 0), stop=(h == 1))
                            elif mode == "rel":
                                mm = nc.tensor.matmul(ps[:, 2 * P:3 * P], oh2[:, u, 1, :], oh2[:, u, 0, :], start=True, stop=True)
                            mm.then_inc(products, 1)

        def finish0():
            at, free, back, m_ready, e_ready, var_ready, std_ready, x_out, x_ready, dv = [
                sem("f0_" + n) for n in "at free back m_ready e_ready var_ready std_ready x_out x_ready dve".split()]
            with nc.Block() as block:
                @block.gpsimd
                def _(pool):
                    with nc.gpsimd.Fori(0, NG) as i:
                        pool.wait_ge(free, i * GRP)
                        for s in range(3):
                            last = nc.gpsimd.tensor_copy(accg[:, s, :], acc[:, s, ds(i * GRP * P, GRP * P)])
                        last.then_inc(at, 1)

                @block.tensor
                def _(pe):
                    credit(pe, back, 1)
                    with nc.tensor.Fori(0, NG) as i:
                        pe.wait_ge(at, i + 1)
                        pe.wait_ge(back, i + 1)
                        for n in range(GRP):
                            for s in range(3):
                                mm = nc.tensor.transpose(PS[n][:, s * P:(s + 1) * P], accg[:, s, n * P:(n + 1) * P], ident[:, :])
                            mm.then_inc(free, 1)

                @block.vector
                def _(dve):
                    step = Chain(dve, dv)
                    rows, low = stage[:, 0, :, :], stage[:, 1, :, :]
                    den = small[:, 4:6, :].rearrange("p h n -> p n h")
                    with nc.vector.Fori(0, NG) as i:
                        step.enter(i, 10)
                        for n in range(GRP):
                            dve.wait_ge(free, i * GRP + n + 1)
                            last = nc.vector.tensor_scalar(den[:, n, :], PS[n][:, 2 * P:2 * P + 2], 1.0e-38, None, ALU.max)
                        step(last)
                        step(nc.vector.reciprocal(small[:, 6:8, :], small[:, 4:6, :]))
                        rden = small[:, 6:8, :].rearrange("p h n -> p n h")
                        for n in range(GRP):
                            for h in range(2):
                                last = nc.vector.tensor_scalar(rows[:, n, h * P:(h + 1) * P], PS[n][:, h * P:(h + 1) * P], rden[:, n, h:h + 1], None, ALU.mult)
                        last.then_inc(back, 1)
                        dve.wait_ge(back, i + 2)
                        nc.vector.tensor_scalar(low, rows, 0.0, None, ALU.min).then_inc(m_ready, 1)
                        dve.wait_ge(e_ready, i + 1)
                        step(nc.vector.scalar_tensor_tensor(rows, rows, 0.0, low, ALU.max, ALU.add))
                        step(nc.vector.scalar_tensor_tensor(rows, rows, -1.0, group_rows(X, i), ALU.add, ALU.add))
                        layer_norm(dve, step, rows, group_rows(X, i), var_ready, std_ready, i + 1).then_inc(x_ready, 1)
                        dve.wait_ge(x_ready, i + 1)
                    step.leave(NG, 10)

                @block.scalar
                def _(act):
                    with nc.scalar.Fori(0, NG) as i:
                        act.wait_ge(m_ready, i + 1)
                        nc.scalar.activation(stage[:, 1, :, :], stage[:, 1, :, :], ACT.Exp).then_inc(e_ready, 1)
                        act_root(act, var_ready, std_ready, i + 1)

                @block.sync
                def _(sp):
                    with nc.sync.Fori(0, NG) as i:
                        sp.wait_ge(x_ready, i + 1)
                        sp.dma_start(table_rows(x_tab, i), group_rows(X, i)).then_inc(x_out, 16)
                    sp.wait_ge(x_out, NG * 16)


        def transpose_rows(pe, i, at, xt_free, xt_ready):
            pe.wait_ge(at, i + 1)
            for n in range(GRP):
                pe.wait_ge(xt_free, i * GRP + n + 1)
                for k in range(2):
                    mm = nc.tensor.transpose(PS[6 + n % 2][:, k * P:(k + 1) * P], xg[:, n, k * P:(k + 1) * P], ident[:, :])
                mm.then_inc(xt_ready, 1)

        def take_transposed(act, i, xt_ready, xt_free, used):
            act.wait_ge(used, i * GRP)
            for n in range(GRP):
                act.wait_ge(xt_ready, i * GRP + n + 1)
                nc.scalar.copy(xTg[:, :, n * P:(n + 1) * P], PS[6 + n % 2][:, 0:2 * P].rearrange("p (k c) -> p k c", k=2)).then_inc(xt_free, 1)

        def finish1():
            at, xt_ready, xt_free, mm_ready, mm_free, sig_ready, tanh_ask, tanh_ready, var_ready, std_ready, done, dv = [
                sem("f1_" + n) for n in "at xt_ready xt_free mm_ready mm_free sig_ready tanh_ask tanh_ready var_ready std_ready done dve".split()]
            with nc.Block() as block:
                @block.gpsimd
                def _(pool):
                    with nc.gpsimd.Fori(0, NG) as i:
                        pool.wait_ge(mm_ready, i * GRP)
                        nc.gpsimd.tensor_copy(xg[:, :, :], group_rows(X, i))
                        for s in range(3):
                            last = nc.gpsimd.tensor_copy(accg[:, s, :], acc[:, s, ds(i * GRP * P, GRP * P)])
                        last.then_inc(at, 1)

                @block.tensor
                def _(pe):
                    credit(pe, xt_free, 2)
                    credit(pe, mm_free, 1)
                    with nc.tensor.Fori(0, NG) as i:
                        transpose_rows(pe, i, at, xt_free, xt_ready)
                        for n in range(GRP):
                            pe.wait_ge(xt_free, i * GRP + n + 3)
                            pe.wait_ge(mm_free, i * GRP + n + 1)
                            rz, nn = PS[0], PS[1]
                            cols = slice(n * P, (n + 1) * P)
                            for ps, c0, c1, gates in ((rz[:, :], 0, 512, "ih"), (nn[:, 0:F], 512, 768, "i"), (nn[:, F:512], 512, 768, "h")):
                                terms = []
                                if "i" in gates:
                                    terms += [(accg[:, k, cols], wbig[:, 0, k, c0:c1]) for k in range(2)]
                                    terms += [(accg[0:NREL, 2, cols], relw[:, c0:c1])]
                                if "h" in gates:
                                    terms += [(xTg[:, k, cols], wbig[:, 1, k, c0:c1]) for k in range(2)]
                                for m, (left, right) in enumerate(terms):
                                    mm = nc.tensor.matmul(ps, left, right, start=(m == 0), stop=(m == len(terms) - 1))
                            mm.then_inc(mm_ready, 1)

                @block.scalar
                def _(act):
                    with nc.scalar.Fori(0, NG) as i:
                        take_transposed(act, i, xt_ready, xt_free, mm_ready)
                        act.wait_ge(mm_free, (i + 1) * GRP + 1)
                        nc.scalar.activation(g5[:, :, 0:512], g5[:, :, 0:512], ACT.Sigmoid).then_inc(sig_ready, 1)
                        act.wait_ge(tanh_ask, i + 1)
                        nc.scalar.activation(stage[:, 0, :, :], stage[:, 0, :, :], ACT.Tanh).then_inc(tanh_ready, 1)
                        act_root(act, var_ready, std_ready, i + 1)

                @block.vector
                def _(dve):
                    step = Chain(dve, dv)
                    step(nc.vector.tensor_tensor(bc_t[:, 0:512], bc_t[:, 0:512], bc_b[:, 0:512], ALU.add))
                    nn, u = stage[:, 0, :, :], stage[:, 1, :, :]
                    r, z, n_i, n_h = (g5[:, :, q * F:(q + 1) * F] for q in range(4))
                    with nc.vector.Fori(0, NG) as i:
                        step.enter(i, 11)
                        for n in range(GRP):
                            dve.wait_ge(mm_ready, i * GRP + n + 1)
                            nc.vector.tensor_tensor(g5[:, n, 0:512], PS[0][:, :], bc_t[:, 0:512], ALU.add)
                            nc.vector.tensor_tensor(n_i[:, n, :], PS[1][:, 0:F], bc_t[:, 512:768], ALU.add)
                            last = nc.vector.tensor_tensor(n_h[:, n, :], PS[1][:, F:512], bc_b[:, 512:768], ALU.add)
                            last.then_inc(mm_free, 1)
                        dve.wait_ge(mm_free, (i + 1) * GRP + 1)
                        dve.wait_ge(sig_ready, i + 1)
                        step(nc.vector.tensor_tensor(nn, r, n_h, ALU.mult))
                        nc.vector.tensor_tensor(nn, nn, n_i, ALU.add).then_inc(tanh_ask, 1)
                        dve.wait_ge(tanh_ready, i + 1)
                        step(nc.vector.tensor_tensor(u, group_rows(X, i), nn, ALU.subtract))
                        step(nc.vector.tensor_tensor(u, u, z, ALU.mult))
                        step(nc.vector.tensor_tensor(nn, nn, u, ALU.add))
                        step(nc.vector.tensor_tensor(nn, nn, group_rows(X, i), ALU.add))
                        layer_norm(dve, step, nn, group_rows(X, i), var_ready, std_ready, i + 1).then_inc(done, 1)
                        dve.wait_ge(done, i + 1)
                    step.leave(NG, 11)

        def project2():
            at, xt_ready, xt_free, mm_ready, mm_free, nrm_ask, nrm_ready, h_ready, h_out, dv = [
                sem("p2_" + n) for n in "at xt_ready xt_free mm_ready mm_free nrm_ask nrm_ready h_ready h_out dve".split()]
            with nc.Block() as block:
                @block.gpsimd
                def _(pool):
                    with nc.gpsimd.Fori(0, NG) as i:
                        pool.wait_ge(xt_ready, i * GRP)
                        nc.gpsimd.tensor_copy(xg[:, :, :], group_rows(X, i)).then_inc(at, 1)

                @block.tensor
                def _(pe):
                    credit(pe, xt_free, 2)
                    credit(pe, mm_free, GRP)
                    with nc.tensor.Fori(0, NG) as i:
                        transpose_rows(pe, i, at, xt_free, xt_ready)
                        for n in range(GRP):
                            pe.wait_ge(xt_free, i * GRP + n + 3)
                            pe.wait_ge(mm_free, i * GRP + n + 1)
                            for k in range(2):
                                mm = nc.tensor.matmul(PS[n][:, 0:F + 1], xTg[:, k, n * P:(n + 1) * P], w2T[:, k, :], start=(k == 0), stop=(k == 1))
                            mm.then_inc(mm_ready, 1)

                @block.scalar
                def _(act):
                    with nc.scalar.Fori(0, NG) as i:
                        take_transposed(act, i, xt_ready, xt_free, mm_ready)
                        act.wait_ge(nrm_ask, i + 1)
                        nc.scalar.activation(small[:, 5, :], small[:, 5, :], ACT.Sqrt)
                        nc.scalar.activation(small[:, 4, :], small[:, 4, :], ACT.Sigmoid).then_inc(nrm_ready, 1)

                @block.vector
                def _(dve):
                    step = Chain(dve, dv)
                    hr, sq, mag, nrm = stage[:, 0, :, :], stage[:, 1, :, :], small[:, 4, :], small[:, 5, :]
                    with nc.vector.Fori(0, NG) as i:
                        step.enter(i, 8)
                        for n in range(GRP):
                            dve.wait_ge(mm_ready, i * GRP + n + 1)
                            nc.vector.tensor_tensor(hr[:, n, :], PS[n][:, 0:F], bc_b2[:, 0:F], ALU.add)
                            nc.vector.tensor_tensor(mag[:, n:n + 1], PS[n][:, F:F + 1], bc_b2[:, F:F + 1], ALU.add).then_inc(mm_free, 1)
                        dve.wait_ge(mm_free, (i + 2) * GRP)
                        step(nc.vector.tensor_tensor(sq, hr, hr, ALU.mult))
                        nc.vector.tensor_reduce(nrm, sq, AX, ALU.add).then_inc(nrm_ask, 1)
                        dve.wait_ge(nrm_ready, i + 1)
                        step(nc.vector.tensor_scalar(nrm, nrm, 1.0e-12, None, ALU.max))
                        step(nc.vector.reciprocal(small[:, 6, :], nrm))
                        step(nc.vector.scalar_tensor_tensor(small[:, 7, :], mag, 1.5, small[:, 6, :], ALU.mult, ALU.mult))
                        nc.vector.tensor_tensor(group_rows(H, i), hr, bc_last(small[:, 7, :], F), ALU.mult).then_inc(h_ready, 1)
                        dve.wait_ge(h_ready, i + 1)
                        for st in range(2):
                            step(nc.vector.tensor_tensor(sq, group_rows(H, i), bc_a2[:, st, :].unsqueeze(1).broadcast_to([P, GRP, F]), ALU.mult))
                            step(nc.vector.tensor_reduce(s_tab[:, ds(i * GRP, GRP), st:st + 1].rearrange("p t a -> p (t a)"), sq, AX, ALU.add))
                    step.leave(NG, 8)
                    split3(step, 2)

                @block.sync
                def _(sp):
                    with nc.sync.Fori(0, NG) as i:
                        sp.wait_ge(h_ready, i + 1)
                        sp.dma_start(table_rows(h2_tab, i), group_rows(H, i)).then_inc(h_out, 16)
                    sp.wait_ge(h_out, NG * 16)

        xc, Rc, Tc = (accf[0:CP, q * H3 * CL:(q + 1) * H3 * CL].rearrange("p (h e) -> p h e", h=H3) for q in range(3))

        def edge_softmax(tag, heads, scale, eps, least, read):
            c_ready, c_taken, l_ask, l_ready, b_ask, b_ready, e_ask, e_ready, w_ask, w_ready, w_taken, dv = [
                sem(f"{tag}_{n}") for n in "c_ready c_taken l_ask l_ready b_ask b_ready e_ask e_ready w_ask w_ready w_taken dve".split()]

            def carries(dve, step, n, backward, maximum):
                dve.wait_ge(l_ready, n + 1)
                step(nc.vector.tensor_copy(rowc[0:heads, 1, 0:CP], PS[4][0:heads, 0:CP]))
                start = -BIG if maximum else 0.0
                op0, op1 = (ALU.add, ALU.max) if maximum else (ALU.mult, ALU.add)
                keep = allr[0:heads, 2 if maximum else (1 if backward else 0), :]
                if backward:
                    nc.vector.memset(rowc[0:heads, 0, CP:CP + 1], start)
                    nc.vector.tensor_tensor_scan(rowc[0:heads, 0, 0:CP][:, ::-1], keep[:, ::-1], rowc[0:heads, 1, 0:CP][:, ::-1], start, op0, op1).then_inc(b_ask, 1)
                else:
                    nc.vector.memset(rowc[0:heads, 0, 0:1], start)
                    nc.vector.tensor_tensor_scan(rowc[0:heads, 0, 1:CP + 1], keep, rowc[0:heads, 1, 0:CP], start, op0, op1).then_inc(b_ask, 1)
                dve.wait_ge(b_ready, n + 1)
                step(nc.vector.tensor_copy(carry[:, 0:heads], PS[5][0:CP, 0:heads]))

            def totals(dve, step, n, maximum):
                op0, op1 = (ALU.add, ALU.max) if maximum else (ALU.mult, ALU.add)
                keep = pen if maximum else cont
                for again in range(2):
                    for h in range(heads):
                        start = carry[:, h:h + 1] if again else (-BIG if maximum else 0.0)
                        last = nc.vector.tensor_tensor_scan(Rc[:, h, :], keep[:, :], xc[:, h, :], start, op0, op1)
                    step(last)
                    if not again:
                        nc.vector.tensor_copy(lastv[:, 0:heads], Rc[:, 0:heads, CL - 1:CL].rearrange("p h e -> p (h e)")).then_inc(l_ask, 1)
                        carries(dve, step, n, False, maximum)
                step(nc.vector.tensor_tensor(Tc[:, 0:heads, :], Rc[:, 0:heads, :], notn[:, :].unsqueeze(1).broadcast_to([CP, heads, CL]), ALU.mult))
                for again in range(2):
                    for h in range(heads):
                        start = carry[:, h:h + 1] if again else 0.0
                        last = nc.vector.tensor_tensor_scan(Rc[:, h, :][:, ::-1], contn[:, :][:, ::-1], Tc[:, h, :][:, ::-1], start, ALU.mult, ALU.add)
                    step(last)
                    if not again:
                        nc.vector.tensor_copy(lastv[:, 0:heads], Rc[:, 0:heads, 0:1].rearrange("p h e -> p (h e)")).then_inc(l_ask, 1)
                        carries(dve, step, n + 1, True, False)

            with nc.Block() as block:
                @block.vector
                def _(dve):
                    step = Chain(dve, dv)
                    for h in range(heads):
                        dve.wait_ge(c_ready, h + 1)
                        nc.vector.tensor_scalar(xc[:, h, :], PS[h][0:CP, :], scale, None, ALU.mult).then_inc(c_taken, 1)
                    dve.wait_ge(c_taken, heads)
                    totals(dve, step, 0, True)
                    if least is not None:
                        step(nc.vector.tensor_scalar(Rc[:, 0:heads, :], Rc[:, 0:heads, :], least, None, ALU.max))
                    nc.vector.tensor_tensor(xc[:, 0:heads, :], xc[:, 0:heads, :], Rc[:, 0:heads, :], ALU.subtract).then_inc(e_ask, 1)
                    dve.wait_ge(e_ready, 1)
                    totals(dve, step, 2, False)
                    step(nc.vector.tensor_scalar(Rc[:, 0:heads, :], Rc[:, 0:heads, :], eps, None, ALU.add))
                    step(nc.vector.reciprocal(Tc[:, 0:heads, :], Rc[:, 0:heads, :]))
                    nc.vector.tensor_tensor(xc[:, 0:heads, :], xc[:, 0:heads, :], Tc[:, 0:heads, :], ALU.mult).then_inc(w_ask, 1)
                    for h in range(heads):
                        dve.wait_ge(w_ready, h + 1)
                        nc.vector.tensor_copy(w_e[:, :, h].rearrange("q (p j) -> q j p", j=J), PS[h][:, 0:ET].rearrange("q (j p) -> q j p", j=J)).then_inc(w_taken, 1)
                    dve.wait_ge(w_taken, heads)

                @block.scalar
                def _(act):
                    act.wait_ge(e_ask, 1)
                    nc.scalar.activation(xc[:, 0:heads, :], xc[:, 0:heads, :], ACT.Exp).then_inc(e_ready, 1)

                @block.tensor
                def _(pe):
                    for h in range(heads):
                        for j in range(J):
                            mm = nc.tensor.transpose(PS[h][0:CP, j * P:(j + 1) * P], read(h)[:, j::J], ident[:, :])
                        mm.then_inc(c_ready, 1)
                    for n in range(4):
                        pe.wait_ge(l_ask, n + 1)
                        nc.tensor.transpose(PS[4][0:heads, 0:CP], lastv[:, 0:heads], ident[0:CP, 0:CP]).then_inc(l_ready, 1)
                        pe.wait_ge(b_ask, n + 1)
                        row = rowc[0:heads, 0, 1:CP + 1] if n % 2 else rowc[0:heads, 0, 0:CP]
                        nc.tensor.transpose(PS[5][0:CP, 0:heads], row, ident[0:heads, 0:heads]).then_inc(b_ready, 1)
                    pe.wait_ge(w_ask, 1)
                    for h in range(heads):
                        for j in range(J):
                            mm = nc.tensor.transpose(PS[h][:, j * CP:(j + 1) * CP], xc[:, h, j * P:(j + 1) * P], ident[0:CP, 0:CP])
                        mm.then_inc(w_ready, 1)

        def sum_scores():
            dv = sem("score_sum")
            with nc.Block() as block:
                @block.vector
                def _(dve):
                    nc.vector.tensor_tensor(s_e[:, :, 0], s_e[:, :, 0], s_e[:, :, 1], ALU.add).then_inc(dv, 1)
                    dve.wait_ge(dv, 1)

        def finish2():
            at, free, back, n_ask, n_ready, t_ready, m_ask, m_ready, var_ready, std_ready, done, dv = [
                sem("f2_" + n) for n in "at free back n_ask n_ready t_ready m_ask m_ready var_ready std_ready done dve".split()]
            with nc.Block() as block:
                @block.gpsimd
                def _(pool):
                    with nc.gpsimd.Fori(0, NG) as i:
                        pool.wait_ge(free, i * GRP)
                        for s in range(2):
                            last = nc.gpsimd.tensor_copy(accg[:, s, :], acc[:, s, ds(i * GRP * P, GRP * P)])
                        last.then_inc(at, 1)

                @block.tensor
                def _(pe):
                    credit(pe, back, GRP)
                    with nc.tensor.Fori(0, NG) as i:
                        pe.wait_ge(at, i + 1)
                        for n in range(GRP):
                            pe.wait_ge(back, i * GRP + n + 1)
                            for s in range(2):
                                mm = nc.tensor.transpose(PS[n][:, s * P:(s + 1) * P], accg[:, s, n * P:(n + 1) * P], ident[:, :])
                            mm.then_inc(free, 1)

                @block.vector
                def _(dve):
                    step = Chain(dve, dv)
                    hc, sq, nrm, tmp = stage[:, 0, :, :], stage[:, 1, :, :], small[:, 4, :], small[:, 6, :]
                    with nc.vector.Fori(0, NG) as i:
                        step.enter(i, 19)
                        for n in range(GRP):
                            dve.wait_ge(free, i * GRP + n + 1)
                            nc.vector.tensor_tensor(hc[:, n, :], PS[n][:, 0:F], H[:, ds(i * GRP + n, 1), :].rearrange("p a f -> p (a f)"), ALU.add).then_inc(back, 1)
                        dve.wait_ge(back, (i + 2) * GRP)
                        step(nc.vector.tensor_tensor(sq, hc, hc, ALU.mult))
                        nc.vector.tensor_reduce(nrm, sq, AX, ALU.add).then_inc(n_ask, 1)
                        dve.wait_ge(n_ready, i + 1)
                        step(nc.vector.tensor_scalar(nrm, nrm, 1.0e-15, None, ALU.max))
                        nc.vector.reciprocal(tmp, nrm).then_inc(m_ask, 1)
                        dve.wait_ge(t_ready, i + 1)
                        step(nc.vector.tensor_tensor(tmp, tmp, small[:, 5, :], ALU.mult))
                        step(nc.vector.tensor_tensor(hc, hc, bc_last(tmp, F), ALU.mult))
                        step(nc.vector.tensor_tensor(sq, hc, hc, ALU.mult))
                        nc.vector.tensor_reduce(nrm, sq, AX, ALU.add).then_inc(n_ask, 1)
                        dve.wait_ge(m_ready, i + 1)
                        step(nc.vector.tensor_scalar(tmp, nrm, 1.0e-8, None, ALU.add))
                        step(nc.vector.reciprocal(small[:, 7, :], tmp))
                        step(nc.vector.tensor_scalar(tmp, small[:, 7, :], 0.95, -1.0, ALU.mult, ALU.add))
                        step(nc.vector.tensor_scalar(nrm, nrm, 0.95, None, ALU.is_gt))
                        step(nc.vector.tensor_tensor(tmp, tmp, nrm, ALU.mult))
                        step(nc.vector.tensor_scalar(tmp, tmp, 1.0, None, ALU.add))
                        step(nc.vector.tensor_tensor(hc, hc, bc_last(tmp, F), ALU.mult))
                        step(nc.vector.tensor_tensor(hc, hc, group_rows(X, i), ALU.add))
                        layer_norm(dve, step, hc, group_rows(X, i), var_ready, std_ready, i + 1).then_inc(done, 1)
                        dve.wait_ge(done, i + 1)
                    step.leave(NG, 19)

                @block.scalar
                def _(act):
                    nrm = small[:, 4, :]
                    with nc.scalar.Fori(0, NG) as i:
                        act.wait_ge(n_ask, i * 2 + 1)
                        nc.scalar.activation(nrm, nrm, ACT.Sqrt).then_inc(n_ready, 1)
                        act.wait_ge(m_ask, i + 1)
                        nc.scalar.activation(small[:, 5, :], nrm, ACT.Tanh).then_inc(t_ready, 1)
                        act.wait_ge(n_ask, i * 2 + 2)
                        nc.scalar.activation(nrm, nrm, ACT.Sqrt).then_inc(m_ready, 1)
                        act_root(act, var_ready, std_ready, i + 1)

        def project3(layer, rows):
            ln = str(layer)
            ld, bias_ready, at, xt_ready, xt_free, mm_ready, mm_free, q_out, dv = [
                sem(f"p3{ln}_{n}") for n in "ld bias_ready at xt_ready xt_free mm_ready mm_free q_out dve".split()]
            wq = wbig[:, :, :, :].rearrange("p a k f -> p (a k f)")[:, 0:2048].rearrange("p (k f) -> p k f", k=2)
            with nc.Block() as block:
                @block.sync
                def _(sp):
                    for n, letter in enumerate("qkvs"):
                        sp.dma_start(wq[:, :, n * F:(n + 1) * F], a[f"L3_gnn_W{letter}{ln}"].rearrange("(k p) f -> p k f", p=P)).then_inc(ld, 16)
                        sp.dma_start(bc_b[:, n * F:(n + 1) * F], a[f"L3_gnn_b{letter}{ln}"].unsqueeze(0).broadcast_to([P, F])).then_inc(ld, 16)
                    sp.dma_start(bc_b2[:, 0:F], a[f"L3_gnn_be{ln}"].unsqueeze(0).broadcast_to([P, F])).then_inc(ld, 16)
                    sp.dma_start(we[:, :], a[f"L3_gnn_We{ln}"]).then_inc(ld, 16)
                    with nc.sync.Fori(0, NG) as i:
                        sp.wait_ge(mm_free, (i + 1) * GRP * 2 + 2)
                        for n, tab in enumerate((q_tab, k_tab, v_tab)):
                            sp.dma_start(table_rows(tab, i), g5[:, :, n * F:(n + 1) * F]).then_inc(q_out, 16)
                    sp.wait_ge(q_out, NG * 48)

                @block.gpsimd
                def _(pool):
                    with nc.gpsimd.Fori(0, NG) as i:
                        pool.wait_ge(xt_ready, i * GRP)
                        nc.gpsimd.tensor_copy(xg[:, :, :], group_rows(rows, i)).then_inc(at, 1)

                @block.tensor
                def _(pe):
                    credit(pe, xt_free, 2)
                    credit(pe, mm_free, 2)
                    pe.wait_ge(ld, 160)
                    with nc.tensor.Fori(0, NG) as i:
                        transpose_rows(pe, i, at, xt_free, xt_ready)
                        for n in range(GRP):
                            pe.wait_ge(xt_free, i * GRP + n + 3)
                            for b in range(2):
                                pe.wait_ge(mm_free, i * GRP * 2 + n * 2 + b + 1)
                                for k in range(2):
                                    mm = nc.tensor.matmul(PS[b][:, :], xTg[:, k, n * P:(n + 1) * P], wq[:, k, b * 512:(b + 1) * 512], start=(k == 0), stop=(k == 1))
                                mm.then_inc(mm_ready, 1)

                @block.scalar
                def _(act):
                    with nc.scalar.Fori(0, NG) as i:
                        act.wait_ge(mm_ready, i * GRP * 2)
                        for n in range(GRP):
                            act.wait_ge(xt_ready, i * GRP + n + 1)
                            nc.scalar.copy(xTg[:, :, n * P:(n + 1) * P], PS[6 + n % 2][:, 0:2 * P].rearrange("p (k c) -> p k c", k=2)).then_inc(xt_free, 1)

                @block.vector
                def _(dve):
                    step = Chain(dve, dv)
                    dve.wait_ge(ld, 160)
                    nc.vector.tensor_tensor(bc_b[:, F:2 * F], bc_b[:, F:2 * F], bc_b2[:, 0:F], ALU.add)
                    step(nc.vector.tensor_tensor(bc_b[:, 2 * F:3 * F], bc_b[:, 2 * F:3 * F], bc_b2[:, 0:F], ALU.add))
                    with nc.vector.Fori(0, NG) as i:
                        dve.wait_ge(q_out, i * 48)
                        for n in range(GRP):
                            dve.wait_ge(mm_ready, (i * GRP + n) * 2 + 1)
                            nc.vector.tensor_tensor(g5[:, n, 0:512], PS[0][:, :], bc_b[:, 0:512], ALU.add).then_inc(mm_free, 1)
                            dve.wait_ge(mm_ready, (i * GRP + n) * 2 + 2)
                            nc.vector.tensor_tensor(H[:, ds(i * GRP + n, 1), :].rearrange("p a f -> p (a f)"), PS[1][:, F:2 * F], bc_b[:, 3 * F:4 * F], ALU.add)
                            nc.vector.tensor_tensor(g5[:, n, 2 * F:3 * F], PS[1][:, 0:F], bc_b[:, 2 * F:3 * F], ALU.add).then_inc(mm_free, 1)

        a_ready = [lasting_sem(f"a_ready{h}") for h in range(2)]
        a_base, w_base = [0], [0]
        attr = a["edge_attr_128"]

        def load_attributes(sp, i, half, end=False):
            t0 = i * BODY + half * HB
            sp.dma_start(arow[:, half * HB:(half + 1) * HB - 1, :],
                         attr[ds(t0 * P, (HB - 1) * P), :].rearrange("(t p) c -> p t c", p=P)).then_inc(a_ready[half], 16)
            n = E - (ET - 1) * P if end else P
            sp.dma_start(arow[0:n, (half + 1) * HB - 1, :], attr[ds((t0 + HB - 1) * P, n), :]).then_inc(a_ready[half], 16)

        PAIRS = BODY // 2
        HP = HB // 2

        def scores3(tag, layer):
            names = "idx_ready begun places_even places_odd oht_ready tr_ready tr_taken terms_ready rows_used terms_used sums_done".split()
            idx_ready, begun, places_even, places_odd, oht_ready, tr_ready, tr_taken, terms_ready, rows_used, terms_used, sums_done = [
                sem(f"{tag}_{n}") for n in names]
            gb, ab, wb = g_base[0], a_base[0], w_base[0]
            place_b = places[:, :, :].bitcast(BF16)
            sums = accf[:, 0:BODY // 2 * F].rearrange("p (u f) -> p u f", f=F)
            ohT = oh[:, :, :, :].rearrange("p a u n -> p a (u n)")
            with nc.Block() as block:
                @block.gpsimd
                def _(pool):
                    gather_rows(pool, k_tab, F, idx_ready, rows_used, begun, per=2)

                @block.sync
                def _(sp):
                    def half_body(i, half, end=False):
                        t0 = i * BODY + half * HB
                        sp.wait_ge(oht_ready, i * 2 + half + 1)
                        sp.dma_start(place_b[:, half, :], lo_tab[2:3, ds(t0 * P, HB * P)].broadcast_to([P, HB * P])
                                     ).then_inc((places_even, places_odd)[half], 16)
                        sp.wait_ge(tr_ready, i * PAIRS + half * HP + HP)
                        load_attributes(sp, i, half, end)
                        first = window_starts(t0, mybir.EngineType.SP)
                        for u in range(HB):
                            if u % 2 == 0:
                                sp.wait_ge(terms_ready, i * PAIRS + half * HP + u // 2 + 1)
                            sp.dma_start(qrow[:, u, :], q_tab[ds(first[u], P), :]).then_inc(q_ready[u], 16)
                    credit(sp, oht_ready, 2)
                    credit(sp, tr_ready, PAIRS)
                    credit(sp, terms_ready, HP)
                    with nc.sync.Fori(0, TRIPS - 1) as i:
                        for half in range(2):
                            half_body(i, half)
                    half_body(TRIPS - 1, 0)
                    half_body(TRIPS - 1, 1, end=True)

                @block.scalar
                def _(act):
                    first_indices(act, idx_ready)
                    with nc.scalar.Fori(0, TRIPS) as i:
                        for j in range(PAIRS):
                            k = i * PAIRS + j
                            act.wait_ge(tr_ready, k + 1 + PAIRS)
                            act.wait_ge(terms_ready, k + 1 + HP - 2)
                            nc.scalar.copy(aT[:, (j % 2) * 2:(j % 2) * 2 + 2, :],
                                           PS[j % 2][:, 0:2 * P].rearrange("p (u c) -> p u c", u=2)).then_inc(tr_taken, 1)
                            if j % HP == HP - 1:
                                next_indices(act, i, j // HP, gb, idx_ready)

                @block.tensor
                def _(pe):
                    credit(pe, tr_taken, 2)
                    credit(pe, terms_used, 4)

                    def transposes(i, j):
                        if j % HP == 0:
                            pe.wait_ge(a_ready[j // HP], (ab + i + 1) * 32)
                        pe.wait_ge(tr_taken, i * PAIRS + j + 1)
                        for v in range(2):
                            mm = nc.tensor.transpose(PS[j % 2][:, v * P:(v + 1) * P], arow[:, 2 * j + v, :], ident[:, :])
                        mm.then_inc(tr_ready, 1)

                    def terms(i, j):
                        k = i * PAIRS + j
                        pe.wait_ge(tr_taken, k + 3)
                        pe.wait_ge(rows_used, k + PAIRS - 1)
                        for v in range(2):
                            nc.tensor.matmul(PS[2 + j % 2][:, v * F:(v + 1) * F], aT[:, (2 * j + v) % 4, :], we[:, :], start=True, stop=True)
                        pe.wait_ge(terms_used, k + 1)
                        if j % HP == 0:
                            pe.wait_ge(oht_ready, i * 2 + j // HP + 3)
                        for v in range(2):
                            u = (2 * j + v) % HB
                            pe.wait_ge(q_ready[u], (wb + i * 2 + j // HP + 1) * 16)
                            mm = nc.tensor.matmul(PS[4 + j % 4][:, v * F:(v + 1) * F], ohT[:, j // HP, u * P:(u + 1) * P], qrow[:, u, :], start=True, stop=True)
                        mm.then_inc(terms_ready, 1)

                    def trip(i, end):
                        for j in range(PAIRS):
                            if j + 1 < PAIRS:
                                transposes(i, j + 1)
                            elif not end:
                                transposes(i + 1, 0)
                            terms(i, j)

                    transposes(0, 0)
                    with nc.tensor.Fori(0, TRIPS - 1) as i:
                        trip(i, False)
                    trip(TRIPS - 1, True)

                @block.vector
                def _(dve):
                    def one_hots(i, half):
                        dve.wait_ge((places_even, places_odd)[half], (i + 1) * 16)
                        nc.vector.tensor_scalar(ohT[:, half, :], place_b[:, half, :], iota_p[:, 0:1], None, ALU.is_equal).then_inc(oht_ready, 1)

                    def add_rows(i, j):
                        k, s = i * PAIRS + j, 2 * j
                        dve.wait_ge(terms_ready, k + 1 + HP)
                        for v in range(2):
                            dve.wait_ge(g_ready[s + v], (gb + i + 1) * 16)
                        dve.wait_ge(sums_done, k + 1)
                        nc.vector.tensor_tensor(sums[:, s % 8:s % 8 + 2, :], grow[:, s:s + 2, 0:F], PS[2 + j % 2][:, :].rearrange("p (u f) -> p u f", u=2),
                                                ALU.add).then_inc(rows_used, 1)

                    def times_q(i, j):
                        k, two = i * PAIRS + j, sums[:, (2 * j) % 8:(2 * j) % 8 + 2, :]
                        dve.wait_ge(rows_used, k + 1 + PAIRS)
                        nc.vector.tensor_tensor(two, two, PS[4 + j % 4][:, :].rearrange("p (u f) -> p u f", u=2), ALU.mult
                                                ).then_inc(terms_used, 1)

                    def sum_channels(i, j):
                        k, two = i * PAIRS + j, sums[:, (2 * j) % 8:(2 * j) % 8 + 2, :]
                        dve.wait_ge(terms_used, k + 1 + 4)
                        nc.vector.tensor_reduce(w_e[:, ds(i * BODY + 2 * j, 2), :], two.rearrange("p u (h c) -> p u h c", h=H3),
                                                AX, ALU.add).then_inc(sums_done, 1)

                    def trip(i, begin, end):
                        for j in range(PAIRS):
                            if j == 0:
                                one_hots(i, 1)
                            if j == HP and not end:
                                one_hots(i + 1, 0)
                            if j + 1 < PAIRS:
                                add_rows(i, j + 1)
                            elif not end:
                                add_rows(i + 1, 0)
                            times_q(i, j)
                            if j > 0:
                                sum_channels(i, j - 1)
                            elif not begin:
                                sum_channels(i - 1, PAIRS - 1)

                    credit(dve, sums_done, 4)
                    one_hots(0, 0)
                    add_rows(0, 0)
                    trip(0, True, False)
                    with nc.vector.Fori(1, TRIPS - 1) as i:
                        trip(i, False, False)
                    trip(TRIPS - 1, False, True)
                    sum_channels(TRIPS - 1, PAIRS - 1)
                    dve.wait_ge(sums_done, ET // 2 + 4)
            a_base[0] += TRIPS
            w_base[0] += 2 * TRIPS

        def messages3(tag, layer):
            names = "idx_ready begun tr_ready tr_taken e_ready rows_used msg_ready oh_ready products win_free zeroed".split()
            idx_ready, begun, tr_ready, tr_taken, e_ready, rows_used, msg_ready, oh_ready, products, win_free, zeroed = [
                sem(f"{tag}_{n}") for n in names]
            gb, ab = g_base[0], a_base[0]
            with nc.Block() as block:
                @block.gpsimd
                def _(pool):
                    gather_rows(pool, v_tab, F, idx_ready, rows_used, begun, per=2)

                @block.sync
                def _(sp):
                    def half_body(i, half, end=False):
                        sp.wait_ge(tr_ready, i * PAIRS + half * HP + HP)
                        load_attributes(sp, i, half, end)
                    credit(sp, tr_ready, PAIRS)
                    with nc.sync.Fori(0, TRIPS - 1) as i:
                        for half in range(2):
                            half_body(i, half)
                    half_body(TRIPS - 1, 0)
                    half_body(TRIPS - 1, 1, end=True)

                @block.scalar
                def _(act):
                    first_indices(act, idx_ready)
                    with nc.scalar.Fori(0, TRIPS) as i:
                        for j in range(PAIRS):
                            k = i * PAIRS + j
                            act.wait_ge(tr_ready, k + 1 + PAIRS)
                            act.wait_ge(e_ready, k + 1)
                            nc.scalar.copy(aT[:, (j % 2) * 2:(j % 2) * 2 + 2, :],
                                           PS[j % 2][:, 0:2 * P].rearrange("p (u c) -> p u c", u=2)).then_inc(tr_taken, 1)
                            if j % HP == HP - 1:
                                next_indices(act, i, j // HP, gb, idx_ready)

                @block.tensor
                def _(pe):
                    credit(pe, tr_taken, 2)
                    credit(pe, e_ready, 2)
                    credit(pe, win_free, 4)

                    def transposes(i, j):
                        if j % HP == 0:
                            pe.wait_ge(a_ready[j // HP], (ab + i + 1) * 32)
                        pe.wait_ge(tr_taken, i * PAIRS + j + 1)
                        for v in range(2):
                            mm = nc.tensor.transpose(PS[j % 2][:, v * P:(v + 1) * P], arow[:, 2 * j + v, :], ident[:, :])
                        mm.then_inc(tr_ready, 1)

                    def edge_terms(i, j):
                        k = i * PAIRS + j
                        pe.wait_ge(tr_taken, k + 3)
                        pe.wait_ge(rows_used, k + PAIRS - 1)
                        for v in range(2):
                            mm = nc.tensor.matmul(PS[2 + j % 2][:, v * F:(v + 1) * F], aT[:, (2 * j + v) % 4, :], we[:, :], start=True, stop=True)
                        mm.then_inc(e_ready, 1)

                    def windows(i, j):
                        k = i * PAIRS + j
                        pe.wait_ge(msg_ready, k + 1)
                        for v in range(2):
                            s = 2 * j + v
                            pe.wait_ge(oh_ready, i * BODY + s + 1)
                            pe.wait_ge(win_free, i * BODY + s + 1)
                            for half in range(2):
                                mm = nc.tensor.matmul(PS[4 + s % 4][:, half * P:(half + 1) * P], both[:, s % 4, half * P:(half + 1) * P],
                                                      oh[:, s // HB, s % HB, :], start=True, stop=True)
                            mm.then_inc(products, 1)

                    def trip(i, end):
                        for j in range(PAIRS):
                            if j + 2 < PAIRS:
                                transposes(i, j + 2)
                            elif not end:
                                transposes(i + 1, j + 2 - PAIRS)
                            if j + 1 < PAIRS:
                                edge_terms(i, j + 1)
                            elif not end:
                                edge_terms(i + 1, 0)
                            windows(i, j)

                    transposes(0, 0)
                    transposes(0, 1)
                    edge_terms(0, 0)
                    with nc.tensor.Fori(0, TRIPS - 1) as i:
                        trip(i, False)
                    trip(TRIPS - 1, True)

                @block.vector
                def _(dve):
                    nc.vector.memset(acc[:, 0:2, :], 0.0).then_inc(zeroed, 1)
                    dve.wait_ge(zeroed, 1)

                    def one_hot(i, s):
                        t = i * BODY + s
                        nc.vector.tensor_scalar(oh[:, s // HB, s % HB, :], iota_n[:, :], dloc[:, ds(t, 1)], None, ALU.is_equal).then_inc(oh_ready, 1)

                    def add_window(t, s, start):
                        dve.wait_ge(products, t + 1)
                        dve.wait_ge(win_free, t + 4)
                        window = acc[:, 0:2, ds(start, P)]
                        nc.vector.tensor_tensor(window, window, PS[4 + s % 4][:, 0:2 * P].rearrange("p (s n) -> p s n", s=2), ALU.add).then_inc(win_free, 1)

                    def one_hot_ahead(i, s, end):
                        if s < HB:
                            one_hot(i, s + HB)
                        elif not end:
                            one_hot(i + 1, s - HB)

                    def pair(i, j, end, add_former):
                        k, s = i * PAIRS + j, 2 * j
                        two = both[:, s % 4:s % 4 + 2, :]
                        dve.wait_ge(e_ready, k + 1 + 2)
                        for v in range(2):
                            dve.wait_ge(g_ready[s + v], (gb + i + 1) * 16)
                        nc.vector.tensor_tensor(two, grow[:, s:s + 2, 0:F], PS[2 + j % 2][:, :].rearrange("p (u f) -> p u f", u=2), ALU.add
                                                ).then_inc(rows_used, 1)
                        one_hot_ahead(i, s, end)
                        dve.wait_ge(rows_used, k + 1 + PAIRS)
                        by_head = two.rearrange("p u (h c) -> p u h c", h=H3)
                        nc.vector.tensor_tensor(by_head, by_head, w_e[:, ds(i * BODY + s, 2), :].unsqueeze(3).broadcast_to([P, 2, H3, C3]),
                                                ALU.mult).then_inc(msg_ready, 1)
                        add_former(0)
                        one_hot_ahead(i, s + 1, end)
                        add_former(1)

                    def trip(i, begin, end):
                        for half in range(2):
                            back = 0 if begin and half == 0 else 2
                            t0 = i * BODY + half * HB - back
                            first = window_starts(t0, mybir.EngineType.DVE)
                            for p in range(HP):
                                j = half * HP + p

                                def add_former(v):
                                    n = 2 * p - 2 + v
                                    if n + back >= 0:
                                        add_window(i * BODY + half * HB + n, (half * HB + n) % BODY, first[n + back])
                                pair(i, j, end, add_former)

                    for s in range(HB):
                        one_hot(0, s)
                    trip(0, True, False)
                    with nc.vector.Fori(1, TRIPS - 1) as i:
                        trip(i, False, False)
                    trip(TRIPS - 1, False, True)
                    first = window_starts(ET - HB, mybir.EngineType.DVE)
                    for n in range(HB - 2, HB):
                        add_window(ET - HB + n, BODY - HB + n, first[n])
            a_base[0] += TRIPS

        def finish3(tag, last_layer):
            at, free, back, var_ready, std_ready, y_ready, y_out, dv = [
                sem(f"{tag}_{n}") for n in "at free back var_ready std_ready y_ready y_out dve".split()]
            with nc.Block() as block:
                @block.gpsimd
                def _(pool):
                    with nc.gpsimd.Fori(0, NG) as i:
                        pool.wait_ge(free, i * GRP)
                        for s in range(2):
                            last = nc.gpsimd.tensor_copy(accg[:, s, :], acc[:, s, ds(i * GRP * P, GRP * P)])
                        last.then_inc(at, 1)

                @block.tensor
                def _(pe):
                    credit(pe, back, GRP)
                    with nc.tensor.Fori(0, NG) as i:
                        pe.wait_ge(at, i + 1)
                        for n in range(GRP):
                            pe.wait_ge(back, i * GRP + n + 1)
                            for s in range(2):
                                mm = nc.tensor.transpose(PS[n][:, s * P:(s + 1) * P], accg[:, s, n * P:(n + 1) * P], ident[:, :])
                            mm.then_inc(free, 1)

                @block.vector
                def _(dve):
                    step = Chain(dve, dv)
                    rows = stage[:, 0, :, :]
                    with nc.vector.Fori(0, NG) as i:
                        step.enter(i, 7 if last_layer else 1)
                        for n in range(GRP):
                            dve.wait_ge(free, i * GRP + n + 1)
                            nc.vector.tensor_tensor(rows[:, n, :], PS[n][:, 0:F], H[:, ds(i * GRP + n, 1), :].rearrange("p a f -> p (a f)"), ALU.add).then_inc(back, 1)
                        dve.wait_ge(back, (i + 2) * GRP)
                        if last_layer:
                            step(nc.vector.tensor_tensor(rows, rows, group_rows(X, i), ALU.add))
                            layer_norm(dve, step, rows, group_rows(X, i), var_ready, std_ready, i + 1).then_inc(y_ready, 1)
                            dve.wait_ge(y_ready, i + 1)
                        else:
                            step(nc.vector.tensor_scalar(group_rows(H, i), rows, 0.0, None, ALU.max))
                    step.leave(NG, 7 if last_layer else 1)

                if last_layer:
                    @block.scalar
                    def _(act):
                        with nc.scalar.Fori(0, NG) as i:
                            act_root(act, var_ready, std_ready, i + 1)

                    @block.sync
                    def _(sp):
                        sp.wait_ge(y_ready, NG)
                        sp.dma_start(out[0:(NT - 1) * P, :].rearrange("(t p) f -> p t f", p=P), X[:, 0:NT - 1, :]).then_inc(y_out, 16)
                        sp.dma_start(out[(NT - 1) * P:N, :], X[0:TAIL, NT - 1, :]).then_inc(y_out, 16)
                        sp.wait_ge(y_out, 32)

        phases = [setup, project0, lambda: look_up("l0", [(1, 0, 2, 0)]),
                  lambda: aggregate("a0", h_tab, F + 2, "gat"), finish0,
                  lambda: aggregate("a1", x_tab, F, "rel"), finish1, project2,
                  lambda: look_up("l2", [(0, 0, 1, 0), (1, 1, 1, 1)]),
                  lambda: sum_scores(), lambda: edge_softmax("s2", 1, 1.0, 1.0e-10, -1.0e9, lambda h: s_e[:, :, 0]),
                  lambda: aggregate("a2", h2_tab, F, "one"), finish2,
                  lambda: project3(1, X), lambda: scores3("s31", 1),
                  lambda: edge_softmax("x31", H3, 0.125, 1.0e-16, None, lambda h: w_e[:, :, h]),
                  lambda: messages3("m31", 1), lambda: finish3("f31", False),
                  lambda: project3(2, H), lambda: scores3("s32", 2),
                  lambda: edge_softmax("x32", H3, 0.125, 1.0e-16, None, lambda h: w_e[:, :, h]),
                  lambda: messages3("m32", 2), lambda: finish3("f32", True)]
        for n, phase in enumerate(phases):
            if n < stop:
                phase()
                end_of_phase()
        if dump:
            d = lasting_sem("dumped")
            views = dict(X=X[:, :, :], dloc=dloc[:, :], srcT=srcT[:, :], s_tab=s_tab[:, :, :], s_e=s_e[:, :, :], acc=acc[:, :, 0:NP],
                         wbig=wbig[:, :, :, :], relw=relw[:, :], cont=cont[:, :], contn=contn[:, :], allr=allr[:, :, :], H=H[:, :, :],
                         h_tab=h_tab, w_e=w_e[:, :, 0:dump['w_e'].shape[2]] if 'w_e' in dump else None, x_tab=x_tab, k_tab=k_tab, v_tab=v_tab, q_tab=q_tab[0:NP, :], w2T=w2T[:, :, :])
            with nc.Block() as block:
                @block.sync
                def _(sp):
                    for n, o in enumerate(dump):
                        sp.dma_start(dump[o], views[o], allow_slow_non_contiguous=True).then_inc(d, 16)
                        sp.wait_ge(d, 16 * n + 16)


_INS = (["x", "src", "dst", "edge_attr_128", "edge_type_16", "L0_gnn_W1", "L0_gnn_a1", "L0_gnn_W2", "L0_gnn_a2",
         "L1_gnn_relvectors", "L1_gnn_w_ih", "L1_gnn_w_hh", "L1_gnn_b_ih", "L1_gnn_b_hh",
         "L2_gnn_W", "L2_gnn_b", "L2_gnn_mag_w", "L2_gnn_mag_b", "L2_gnn_attn_w"]
        + [f"L3_gnn_{m}{letter}{layer}" for layer in (1, 2) for letter in "qkves" for m in "Wb"])


def kernel(**inputs):
    import numpy as np
    from concourse import bacc
    from concourse.bass_utils import run_bass_kernel_spmd

    nc = bacc.Bacc("TRN2", target_bir_lowering=False, num_devices=1)
    arrays, args = {}, {}
    for name in _INS:
        arr = np.ascontiguousarray(inputs[name])
        arrays[f"in_{name}"] = arr
        args[name] = nc.dram_tensor(f"in_{name}", arr.shape, mybir.dt.from_np(arr.dtype), kind="ExternalInput").ap()
    out = nc.dram_tensor("out_nodes", (N, F), F32, kind="ExternalOutput").ap()
    graph_layers(nc, args, out)
    r = run_bass_kernel_spmd(nc, [arrays], core_ids=[0])
    return r.results[0]["out_nodes"]
```

```python
from contextlib import ExitStack

import concourse.bass as bass
from concourse import mybir

F32 = mybir.dt.float32
I32 = mybir.dt.int32
BF16 = mybir.dt.bfloat16
ALU = mybir.AluOpType
ACT = mybir.ActivationFunctionType
AX = mybir.AxisListType.X

P = 128
N, F = 3125, 256
E = 53125
NT = -(-N // P)
NP = NT * P
ET = 416
EP = ET * P
CL = 512
CP = EP // CL
J = CL // P
LOHI = P
NH = NP // P
HB = 8
BODY = 2 * HB
TRIPS = ET // BODY
GRP = 5
NG = NT // GRP
ACCW = NP + P
PADN = NP - 1
BIG = 1.0e30
H3, C3 = 4, 64
DVE_HEADS = 1
ED = 128
NREL = 16
TAIL = N - (NT - 1) * P
ETAIL = E - (CP - 1) * CL


class Chain:

    def __init__(self, eng, sem):
        self.eng, self.sem, self.base, self.n = eng, sem, 0, 0

    def __call__(self, ins):
        self.n += 1
        ins.then_inc(self.sem, 1)
        self.eng.wait_ge(self.sem, self.base + self.n)

    def enter(self, i, per_trip):
        self.start = self.base + self.n
        self.base, self.n = self.start + i * per_trip, 0

    def leave(self, trips, per_trip):
        assert self.n == per_trip, (self.n, per_trip)
        self.base, self.n = self.start + trips * per_trip, 0


def graph_layers(nc, a, out):
    ctx = ExitStack()
    with ctx:
        def sb(name, shape, dt=F32):
            return ctx.enter_context(nc.sbuf_tensor(name, shape, dt))

        phase_sems = []

        def lasting_sem(name):
            return ctx.enter_context(nc.semaphore(name))

        def sem(name):
            phase_sems.append(nc.alloc_semaphore(name=name))
            return phase_sems[-1]

        def end_of_phase():
            nc.clear_and_free_semaphores(list(phase_sems))
            phase_sems.clear()
            nc.all_engine_barrier()

        def dram(name, shape, dt=F32):
            return nc.dram_tensor(name, shape, dt, kind="Internal").ap()

        x_tab = dram("x_tab", [NP, F])
        h_tab = dram("h_tab", [NP, F + 2])
        h2_tab = dram("h2_tab", [NP, F])
        k_tab = dram("k_tab", [NP, F])
        v_tab = dram("v_tab", [NP, F])
        q_tab = dram("q_tab", [ACCW, F])
        lo_tab = dram("lo_tab", [3, EP], BF16)

        X = sb("X", [P, NT, F])
        H = sb("H", [P, NT, F])
        acc = sb("acc", [P, 3, ACCW])
        work = sb("work", [P, 13440])

        def carve(*shapes):
            at, views = 0, []
            for s in shapes:
                n = 1
                for d in s:
                    n *= d
                v = work[:, at:at + n]
                names = " ".join("abcd"[:len(s)])
                if len(s) > 1:
                    v = v.rearrange(f"p ({names}) -> p {names}", **dict(zip("abcd", s)))
                views.append(v)
                at += n
            assert at <= 13440, at
            return views

        accg, xg, xTg, g5, stage = carve((3, GRP * P), (GRP, F), (2, GRP * P), (GRP, 1024), (3, GRP, F))
        grow, qrow, oh, arow, aT, places, both = carve((BODY, F + 2), (HB, F), (2, HB, P), (BODY, ED), (4, P), (2, HB * P // 2), (4, F))
        wbig = sb("wbig", [P, 2, 2, 768])
        ident = sb("ident", [P, P])
        iota_n = sb("iota_n", [P, P])
        iota_p = sb("iota_p", [P, 1])
        sel = sb("sel", [P, 2, P])
        ones = sb("ones", [1, P])
        srcT = sb("srcT", [P, ET + BODY], I32)
        dstT = sb("dstT", [P, ET])
        dloc = sb("dloc", [P, ET])
        typT = sb("typT", [P, ET])
        hiT = sb("hiT", [P, 2, ET])
        base_i = sb("base_i", [1, ET], I32)
        idx_st = sb("idx_st", [P, 2, HB], I32)
        w_e = sb("w_e", [P, ET, H3])
        w_flat = w_e[:, :, :].rearrange("p t h -> p (t h)")
        w0 = w_flat[:, 0:2 * F].rearrange("p (k f) -> p k f", k=2)
        bc_a = w_flat[:, 2 * F:2 * F + 4 * P].rearrange("p (a c) -> p a c", a=4)
        relr = w_flat[0:NREL, 2 * F + 4 * P:3 * F + 4 * P]
        s_e = sb("s_e", [P, ET, 2])
        cont = sb("cont", [CP, CL])
        contn = sb("contn", [CP, CL])
        notn = sb("notn", [CP, CL])
        pen = sb("pen", [CP, CL])
        ends = sb("ends", [CP, 2], I32)
        endf = sb("endf", [CP, 2])
        all4 = sb("all4", [CP, 2, H3])
        allr = sb("allr", [H3, 3, CP])
        lastv = sb("lastv", [CP, H3])
        rowc = sb("rowc", [H3, 2, CP + 1])
        carry = sb("carry", [CP, H3])
        s_tab = sb("s_tab", [P, NT, 2])
        s_rem = sb("s_rem", [P, NT, 2])
        s_bf = sb("s_bf", [P, 3, 2, NT], BF16)
        w2T = sb("w2T", [P, 2, F + 1])
        bc_a2 = sb("bc_a2", [P, 2, F])
        bc_b = sb("bc_b", [P, 1024])
        bc_b2 = sb("bc_b2", [P, F + 1])
        bc_t = sb("bc_t", [P, 1024])
        relw = sb("relw", [NREL, 768])
        relT = sb("relT", [P, 2, NREL])
        small = sb("small", [P, 16, GRP])
        we = sb("we", [ED, F])

        PS = [ctx.enter_context(nc.psum_tensor(f"bank{i}", [P, 512], F32)) for i in range(8)]

        accf = acc[:, :, :].rearrange("p a b -> p (a b)")

        def ds(start, n):
            return bass.ds(start, n)

        g_ready = [lasting_sem(f"g_ready{u}") for u in range(BODY)]
        q_ready = [lasting_sem(f"q_ready{u}") for u in range(HB)]
        g_base = [0]
        stats_done = lasting_sem("stats_done")

        def setup():
            ld_w, ld_i, ld_x, ld_e = sem("ld_w"), sem("ld_i"), sem("ld_x"), sem("ld_e")
            padded, consts = sem("padded"), sem("consts")
            dv, pl = sem("setup_dve"), sem("setup_pool")
            floats_ready, t_ready, t_taken = sem("floats_ready"), sem("t_ready"), sem("t_taken")
            lo_ready, lo_out = sem("lo_ready"), sem("lo_out")
            wt_ready, wt_taken = sem("wt_ready"), sem("wt_taken")
            base_ready, base_done, rows_ready, rows_done = sem("base_ready"), sem("base_done"), sem("rows_ready"), sem("rows_done")
            rel_ready, rel_taken, relw_ready = sem("rel_ready"), sem("rel_taken"), sem("relw_ready")

            wih_r = accf[:, 0:1536].rearrange("p (o k) -> p o k", o=6)
            whh_r = accf[:, 1536:3072].rearrange("p (o k) -> p o k", o=6)
            w2_r = accf[:, 3072:3584].rearrange("p (o k) -> p o k", o=2)
            I = accf[0:CP, 3584:5120].bitcast(I32).rearrange("p (a e) -> p a e", a=3)
            Ff = accf[0:CP, 5120:7680].rearrange("p (a e) -> p a e", a=5)
            LH = accf[0:CP, 7680:9728].bitcast(I32).rearrange("p (a e) -> p a e", a=4)
            lo_b = stage[0:CP, 0, 0:4, :].rearrange("p a e -> p (a e)").bitcast(BF16)[:, 0:3 * CL].rearrange("p (a e) -> p a e", a=3)
            names = ("src", "dst", "edge_type_16")

            with nc.Block() as block:
                @block.sync
                def _(sp):
                    sp.wait_ge(padded, 1)
                    for n, name in enumerate(names):
                        whole = (CP - 1) * CL
                        sp.dma_start(I[0:CP - 1, n, :], a[name][0:whole].rearrange("(p e) -> p e", e=CL)).then_inc(ld_i, 16)
                        sp.dma_start(I[CP - 1:CP, n, 0:ETAIL], a[name][whole:E].unsqueeze(0)).then_inc(ld_i, 16)
                    sp.dma_start(ends[1:CP - 1, 0:1], a["dst"][CL - 1:CL - 1 + (CP - 2) * CL].rearrange("(p e) -> p e", e=CL)[:, 0:1],
                                 allow_slow_non_contiguous=True).then_inc(ld_e, 16)
                    sp.dma_start(ends[CP - 1:CP, 0:1], a["dst"][(CP - 1) * CL - 1:(CP - 1) * CL].unsqueeze(0)).then_inc(ld_e, 16)
                    sp.dma_start(ends[0:CP - 2, 1:2], a["dst"][CL:CL + (CP - 2) * CL].rearrange("(p e) -> p e", e=CL)[:, 0:1],
                                 allow_slow_non_contiguous=True).then_inc(ld_e, 16)
                    sp.dma_start(ends[CP - 2:CP - 1, 1:2], a["dst"][(CP - 1) * CL:(CP - 1) * CL + 1].unsqueeze(0)).then_inc(ld_e, 16)
                    sp.dma_start(wih_r, a["L1_gnn_w_ih"].rearrange("(o p) k -> p o k", p=P)).then_inc(ld_w, 16)
                    sp.dma_start(whh_r, a["L1_gnn_w_hh"].rearrange("(o p) k -> p o k", p=P)).then_inc(ld_w, 16)
                    sp.dma_start(w2_r, a["L2_gnn_W"].rearrange("(o p) k -> p o k", p=P)).then_inc(ld_w, 16)
                    sp.dma_start(relr, a["L1_gnn_relvectors"]).then_inc(ld_w, 16)
                    sp.dma_start(X[:, 0:NT - 1, :], a["x"][0:(NT - 1) * P, :].rearrange("(t p) f -> p t f", p=P)).then_inc(ld_x, 16)
                    sp.dma_start(X[0:TAIL, NT - 1, :], a["x"][(NT - 1) * P:N, :]).then_inc(ld_x, 16)
                    sp.dma_start(w0[:, :, 0:P], a["L0_gnn_W1"].rearrange("(k p) f -> p k f", p=P)).then_inc(ld_x, 16)
                    sp.dma_start(w0[:, :, P:F], a["L0_gnn_W2"].rearrange("(k p) f -> p k f", p=P)).then_inc(ld_x, 16)
                    for n, name in enumerate(("L0_gnn_a1", "L0_gnn_a2")):
                        sp.dma_start(bc_a[:, 2 * n:2 * n + 2, :].rearrange("p a c -> p (a c)"), a[name].broadcast_to([P, F])).then_inc(ld_x, 16)
                    for n in range(2):
                        sp.dma_start(bc_a2[:, n, :], a["L2_gnn_attn_w"][:, n * F:(n + 1) * F].broadcast_to([P, F])).then_inc(ld_x, 16)
                    sp.dma_start(bc_b2[:, 0:F], a["L2_gnn_b"].unsqueeze(0).broadcast_to([P, F])).then_inc(ld_x, 16)
                    sp.dma_start(bc_b2[:, F:F + 1], a["L2_gnn_mag_b"].unsqueeze(0).broadcast_to([P, 1])).then_inc(ld_x, 16)
                    for k in range(2):
                        sp.dma_start(w2T[:, k, F:F + 1], a["L2_gnn_mag_w"][0:1, k * P:(k + 1) * P].rearrange("a p -> p a"),
                                     allow_slow_non_contiguous=True).then_inc(ld_x, 16)
                    sp.dma_start(bc_t[:, 0:768], a["L1_gnn_b_ih"].unsqueeze(0).broadcast_to([P, 768])).then_inc(ld_x, 16)
                    sp.dma_start(bc_b[:, 0:768], a["L1_gnn_b_hh"].unsqueeze(0).broadcast_to([P, 768])).then_inc(ld_x, 16)
                    sp.wait_ge(lo_ready, 1)
                    for n in range(3):
                        sp.dma_start(lo_tab[n, :].rearrange("(p e) -> p e", e=CL), lo_b[:, n, :]).then_inc(lo_out, 16)
                    sp.dma_start(q_tab[NP:ACCW, :], qrow[:, 0, :]).then_inc(lo_out, 16)
                    sp.wait_ge(lo_out, 64)
                    sp.wait_ge(ld_w, 16 * 4)
                    sp.wait_ge(ld_x, 16 * 14)

                @block.gpsimd
                def _(pool):
                    nc.gpsimd.iota(iota_n[:, :], pattern=[[1, P]], base=0, channel_multiplier=0, allow_small_or_imprecise_dtypes=True)
                    nc.gpsimd.iota(iota_p[:, :], pattern=[[1, 1]], base=0, channel_multiplier=1, allow_small_or_imprecise_dtypes=True)
                    nc.gpsimd.memset(sel[:, :, :], 0.0)
                    nc.gpsimd.memset(ident[:, :], 0.0).then_inc(pl, 1)
                    pool.wait_ge(pl, 1)
                    nc.gpsimd.affine_select(out=ident[:, :], in_=ident[:, :], compare_op=ALU.not_equal, fill=1.0, base=0,
                                            pattern=[[-1, P]], channel_multiplier=1)
                    for h in range(2):
                        nc.gpsimd.memset(sel[:, h, h:h + 1], 1.0)
                    nc.gpsimd.memset(ones[:, :], 1.0).then_inc(consts, 1)

                @block.vector
                def _(dve):
                    step = Chain(dve, dv)
                    nc.vector.memset(qrow[:, 0, :], 0.0)
                    nc.vector.memset(I[:, 0, :], 0)
                    nc.vector.memset(I[:, 1, :], PADN)
                    nc.vector.memset(I[:, 2, :], 0)
                    nc.vector.memset(ends[:, :], -1)
                    nc.vector.memset(srcT[:, ET:ET + BODY], 0)
                    nc.vector.memset(X[:, NT - 1, :], 0.0).then_inc(padded, 1)
                    dve.wait_ge(ld_i, 16 * 6)
                    nc.vector.tensor_scalar(LH[:, 0:2, :], I[:, 0:2, :], 7, None, ALU.logical_shift_right)
                    step(nc.vector.tensor_scalar(LH[:, 2:4, :], I[:, 0:2, :], LOHI - 1, None, ALU.bitwise_and))
                    nc.vector.tensor_copy(Ff[:, 0:3, :], I[:, :, :])
                    nc.vector.tensor_copy(Ff[:, 3:5, :], LH[:, 0:2, :]).then_inc(floats_ready, 1)
                    nc.vector.tensor_copy(lo_b[:, 0:2, :], LH[:, 2:4, :])
                    dve.wait_ge(floats_ready, 1)
                    dst4 = Ff[:, 1, :].rearrange("p (j c) -> p j c", j=J)
                    nc.vector.tensor_tensor(lo_b[:, 2, :].rearrange("p (j c) -> p j c", j=J), dst4, dst4[:, :, 0:1].broadcast_to([CP, J, P]),
                                            ALU.subtract).then_inc(lo_ready, 1)
                    dve.wait_ge(ld_e, 64)
                    step(nc.vector.tensor_copy(endf[:, :], ends[:, :]))
                    nc.vector.tensor_tensor(cont[:, 1:CL], Ff[:, 1, 1:CL], Ff[:, 1, 0:CL - 1], ALU.is_equal)
                    nc.vector.tensor_tensor(cont[:, 0:1], Ff[:, 1, 0:1], endf[:, 0:1], ALU.is_equal)
                    nc.vector.tensor_tensor(contn[:, 0:CL - 1], Ff[:, 1, 1:CL], Ff[:, 1, 0:CL - 1], ALU.is_equal)
                    step(nc.vector.tensor_tensor(contn[:, CL - 1:CL], Ff[:, 1, CL - 1:CL], endf[:, 1:2], ALU.is_equal))
                    nc.vector.tensor_scalar(notn[:, :], contn[:, :], -1.0, 1.0, ALU.mult, ALU.add)
                    nc.vector.tensor_scalar(pen[:, :], cont[:, :], BIG, -BIG, ALU.mult, ALU.add)
                    nc.vector.tensor_reduce(all4[:, 0, 0:1], cont[:, :], AX, ALU.min)
                    step(nc.vector.tensor_reduce(all4[:, 1, 0:1], contn[:, :], AX, ALU.min))
                    for n in range(2):
                        last = nc.vector.tensor_copy(all4[:, n, 1:H3], all4[:, n, 0:1].broadcast_to([CP, H3 - 1]))
                    last.then_inc(rows_ready, 1)
                    for n in range(5):
                        dve.wait_ge(t_ready, n + 1)
                        dst_ap = (srcT[:, 0:ET], dstT[:, :], typT[:, :], hiT[:, 0, :], hiT[:, 1, :])[n]
                        nc.vector.tensor_copy(dst_ap.rearrange("q (p j) -> q j p", j=J),
                                              PS[n % 2][:, 0:ET].rearrange("q (j p) -> q j p", j=J)).then_inc(t_taken, 1)
                    dve.wait_ge(t_taken, 5)
                    nc.vector.tensor_copy(base_i[:, :], dstT[0:1, :]).then_inc(base_ready, 1)
                    dve.wait_ge(base_done, 1)
                    nc.vector.tensor_tensor(dloc[:, :], dstT[:, :], PS[2][:, 0:ET], ALU.subtract)
                    dve.wait_ge(rows_done, 1)
                    step(nc.vector.tensor_copy(allr[:, 0:2, :], PS[3][0:H3, 0:2 * CP].rearrange("h (n p) -> h n p", n=2)))
                    nc.vector.tensor_scalar(allr[:, 2, :], allr[:, 0, :], BIG, -BIG, ALU.mult, ALU.add)

                @block.tensor
                def _(pe):
                    pe.wait_ge(consts, 1)
                    pe.wait_ge(floats_ready, 1)
                    for n in range(5):
                        if n >= 2:
                            pe.wait_ge(t_taken, n - 1)
                        for j in range(J):
                            mm = nc.tensor.transpose(PS[n % 2][:, j * CP:(j + 1) * CP], Ff[:, n, j * P:(j + 1) * P], ident[0:CP, 0:CP])
                        mm.then_inc(t_ready, 1)
                    pe.wait_ge(t_taken, 2)
                    pe.wait_ge(base_ready, 1)
                    nc.tensor.matmul(PS[2][:, 0:ET], ones[:, :], dstT[0:1, :], start=True, stop=True).then_inc(base_done, 1)
                    pe.wait_ge(rows_ready, 1)
                    for n in range(2):
                        mm = nc.tensor.transpose(PS[3][0:H3, n * CP:(n + 1) * CP], all4[:, n, :], ident[0:CP, 0:CP])
                    mm.then_inc(rows_done, 1)
                    pe.wait_ge(ld_w, 64)
                    n = 0
                    for m, rows in enumerate((wih_r, whh_r)):
                        for k in range(2):
                            for half in range(2):
                                if n >= 2:
                                    pe.wait_ge(wt_taken, n - 1)
                                for o in range(3):
                                    mm = nc.tensor.transpose(PS[4 + n % 2][:, o * P:(o + 1) * P], rows[:, half * 3 + o, k * P:(k + 1) * P], ident[:, :])
                                mm.then_inc(wt_ready, 1)
                                n += 1
                    for k in range(2):
                        pe.wait_ge(wt_taken, n - 1)
                        for o in range(2):
                            mm = nc.tensor.transpose(PS[4 + n % 2][:, o * P:(o + 1) * P], w2_r[:, o, k * P:(k + 1) * P], ident[:, :])
                        mm.then_inc(wt_ready, 1)
                        n += 1
                    for k in range(2):
                        mm = nc.tensor.transpose(PS[6][:, k * NREL:(k + 1) * NREL], relr[:, k * P:(k + 1) * P], ident[0:NREL, 0:NREL])
                    mm.then_inc(rel_ready, 1)
                    pe.wait_ge(rel_taken, 1)
                    pe.wait_ge(wt_taken, 10)
                    for c0, c1, bank in ((0, 512, 4), (512, 768, 5)):
                        for k in range(2):
                            mm = nc.tensor.matmul(PS[bank][0:NREL, 0:c1 - c0], relT[:, k, :], wbig[:, 0, k, c0:c1], start=(k == 0), stop=(k == 1))
                    mm.then_inc(relw_ready, 1)

                @block.scalar
                def _(act):
                    n = 0
                    for m in range(2):
                        for k in range(2):
                            for half in range(2):
                                act.wait_ge(wt_ready, n + 1)
                                nc.scalar.copy(wbig[:, m, k, half * 384:(half + 1) * 384], PS[4 + n % 2][:, 0:384]).then_inc(wt_taken, 1)
                                n += 1
                    act.wait_ge(ld_x, 16 * 14)
                    for k in range(2):
                        act.wait_ge(wt_ready, n + 1)
                        nc.scalar.copy(w2T[:, k, 0:F], PS[4 + n % 2][:, 0:F]).then_inc(wt_taken, 1)
                        n += 1
                    act.wait_ge(rel_ready, 1)
                    nc.scalar.copy(relT[:, :, :], PS[6][:, 0:2 * NREL].rearrange("p (k r) -> p k r", k=2)).then_inc(rel_taken, 1)
                    act.wait_ge(relw_ready, 1)
                    nc.scalar.copy(relw[:, 0:512], PS[4][0:NREL, :])
                    nc.scalar.copy(relw[:, 512:768], PS[5][0:NREL, 0:256])


        def credit(eng, signal, n):
            eng.sem_inc(signal, n)

        def group_rows(t, i):
            return t[:, ds(i * GRP, GRP), :]

        def table_rows(tab, i, width=F):
            return tab[ds(i * GRP * P, GRP * P), :].rearrange("(t p) f -> p t f", p=P)

        def bc_last(ap, n):
            return ap.unsqueeze(2).broadcast_to([P, GRP, n])

        def layer_norm(dve, step, rows, i, var_ready, std_ready, count):
            stats = small[:, 8:14, :].rearrange("p a n -> p (a n)").rearrange("p (n a) -> p n a", n=GRP)
            mv = small[:, 14:16, :].rearrange("p a n -> p (a n)").rearrange("p (n a) -> p n a", n=GRP)
            for n in range(GRP):
                last = nc.vector.bn_stats(stats[:, n, :], rows[:, n, :])
            step(last)
            dve.sem_inc(stats_done, 1)
            for n in range(GRP):
                last = nc.vector.bn_aggr(mv[:, n, :], stats[:, n, :])
            step(last)
            nc.vector.tensor_scalar(small[:, 1, :], mv[:, :, 1], 1.0e-5, None, ALU.add).then_inc(var_ready, 1)
            dve.wait_ge(std_ready, count)
            step(nc.vector.reciprocal(small[:, 3, :], small[:, 2, :]))
            for n in range(GRP):
                last = nc.vector.tensor_scalar(X[:, ds(i * GRP + n, 1), :].rearrange("p a f -> p (a f)"), rows[:, n, :],
                                               mv[:, n, 0:1], small[:, 3, n:n + 1], ALU.subtract, ALU.mult)
            return last

        def act_root(act, var_ready, std_ready, count):
            act.wait_ge(var_ready, count)
            nc.scalar.activation(small[:, 2, :], small[:, 1, :], ACT.Sqrt).then_inc(std_ready, 1)

        def project0():
            names = "rows_at rows_free xt_free h_ready h_free hrow_ready hrow_out scal_dve".split()
            rows_at, rows_free, xt_free, h_ready, h_free, hrow_ready, hrow_out, dv = [sem("p0_" + n) for n in names]
            hrow = g5[:, :, 0:F + 2]
            with nc.Block() as block:
                @block.gpsimd
                def _(pool):
                    with nc.gpsimd.Fori(0, NG) as i:
                        nc.gpsimd.tensor_copy(xg[:, :, :], group_rows(X, i)).then_inc(rows_at, 1)
                        pool.wait_ge(rows_free, (i + 1) * GRP)

                @block.tensor
                def _(pe):
                    credit(pe, xt_free, 2)
                    credit(pe, h_free, GRP)
                    with nc.tensor.Fori(0, NG) as i:
                        pe.wait_ge(rows_at, i + 1)
                        for n in range(GRP):
                            pe.wait_ge(xt_free, i * GRP + n + 1)
                            for k in range(2):
                                mm = nc.tensor.transpose(PS[6 + n % 2][:, k * P:(k + 1) * P], xg[:, n, k * P:(k + 1) * P], ident[:, :])
                            mm.then_inc(rows_free, 1)
                        for n in range(GRP):
                            pe.wait_ge(xt_free, i * GRP + n + 3)
                            pe.wait_ge(h_free, i * GRP + n + 1)
                            for k in range(2):
                                mm = nc.tensor.matmul(PS[n][:, 0:F], xTg[:, k, n * P:(n + 1) * P], w0[:, k, :], start=(k == 0), stop=(k == 1))
                            mm.then_inc(h_ready, 1)

                @block.scalar
                def _(act):
                    with nc.scalar.Fori(0, NG) as i:
                        for n in range(GRP):
                            act.wait_ge(rows_free, i * GRP + n + 1)
                            nc.scalar.copy(xTg[:, :, n * P:(n + 1) * P], PS[6 + n % 2][:, 0:2 * P].rearrange("p (k c) -> p k c", k=2)).then_inc(xt_free, 1)
                        act.wait_ge(hrow_out, (i + 1) * 16)
                        for n in range(GRP):
                            act.wait_ge(h_ready, i * GRP + n + 1)
                            last = nc.scalar.copy(hrow[:, n, 0:F], PS[n][:, 0:F])
                            last.then_inc(h_free, 1)
                        act.wait_ge(h_ready, (i + 1) * GRP)

                @block.vector
                def _(dve):
                    step = Chain(dve, dv)
                    with nc.vector.Fori(0, NG) as i:
                        step.enter(i, 3)
                        dve.wait_ge(h_free, (i + 2) * GRP)
                        for lr in range(2):
                            prod = stage[:, lr, :, :].rearrange("p t (h c) -> p t h c", h=2)
                            for h in range(2):
                                last = nc.vector.tensor_tensor(prod[:, :, h, :], hrow[:, :, h * P:(h + 1) * P],
                                                               bc_a[:, 2 * h + lr, :].unsqueeze(1).broadcast_to([P, GRP, P]), ALU.mult)
                            step(last)
                        step(nc.vector.tensor_reduce(s_tab[:, ds(i * GRP, GRP), 0:2], stage[:, 0, :, :].rearrange("p t (h c) -> p t h c", h=2), AX, ALU.add))
                        nc.vector.tensor_reduce(hrow[:, :, F:F + 2], stage[:, 1, :, :].rearrange("p t (h c) -> p t h c", h=2), AX, ALU.add).then_inc(hrow_ready, 1)
                        dve.wait_ge(hrow_ready, i + 1)
                    step.leave(NG, 3)
                    split3(step, 2)

                @block.sync
                def _(sp):
                    credit(sp, hrow_out, 16)
                    with nc.sync.Fori(0, NG) as i:
                        sp.wait_ge(hrow_ready, i + 1)
                        sp.dma_start(table_rows(h_tab, i), hrow).then_inc(hrow_out, 16)
                    sp.wait_ge(hrow_out, (NG + 1) * 16)

        def split3(step, c):
            s = s_tab[:, :, 0:c]
            bf = lambda part: s_bf[:, part, 0:c, :].rearrange("p c t -> p t c")
            step(nc.vector.tensor_copy(bf(0), s))
            step(nc.vector.tensor_tensor(s_rem[:, :, 0:c], s, bf(0), ALU.subtract))
            step(nc.vector.tensor_copy(bf(1), s_rem[:, :, 0:c]))
            step(nc.vector.tensor_tensor(s_rem[:, :, 0:c], s_rem[:, :, 0:c], bf(1), ALU.subtract))
            step(nc.vector.tensor_copy(bf(2), s_rem[:, :, 0:c]))

        def look_up(tag, jobs):
            lo_0, lo_1, lo_2, lo_3, oht_ready, hi_ready, mm_ready, prod_ready, taken = [
                sem(f"{tag}_{n}") for n in "lo_0 lo_1 lo_2 lo_3 oht_ready hi_ready mm_ready prod_ready taken".split()]
            lo_ready = (lo_0, lo_1, lo_2, lo_3)
            lo_b = g5[:, 0:2, :].rearrange("p a b -> p (a b)").rearrange("p (q e) -> p q e", q=4).bitcast(BF16)
            oht = g5[:, 2, :].rearrange("p (q e) -> p q e", q=2).bitcast(BF16)
            ohh = stage[:, 0, :, :].rearrange("p a b -> p (a b)")[:, 0:2 * HB * NH].rearrange("p (x u t) -> p x u t", x=2, u=HB)
            halves, trips = ET // HB, ET // HB // 4
            with nc.Block() as block:
                @block.sync
                def _(sp):
                    credit(sp, oht_ready, 4)
                    for jn, (end, c0, c, e0) in enumerate(jobs):
                        with nc.sync.Fori(0, trips) as i:
                            for q in range(4):
                                sp.wait_ge(oht_ready, jn * halves + i * 4 + q + 1)
                                sp.dma_start(lo_b[:, q, :], lo_tab[end:end + 1, ds((i * 4 + q) * HB * P, HB * P)].broadcast_to([P, HB * P])
                                             ).then_inc(lo_ready[q], 16)

                @block.vector
                def _(dve):
                    def job(jn, end, c0, c, e0):
                        prod = stage[:, 1:3, :, :].rearrange("p a b c -> p (a b c)")[:, 0:2 * HB * c * NH].rearrange(
                            "p (x u c t) -> p x u c t", x=2, u=HB, c=c)

                        def one_hots(i, q):
                            g, half = jn * halves + i * 4 + q, q % 2
                            dve.wait_ge(lo_ready[q], (jn * trips + i + 1) * 16)
                            nc.vector.tensor_scalar(oht[:, half, :], lo_b[:, q, :], iota_p[:, 0:1], None, ALU.is_equal).then_inc(oht_ready, 1)
                            dve.wait_ge(prod_ready, g + 1)
                            nc.vector.tensor_tensor(ohh[:, half, :, :], iota_n[:, 0:NH].unsqueeze(1).broadcast_to([P, HB, NH]),
                                                    hiT[:, end, ds((i * 4 + q) * HB, HB)].unsqueeze(2).broadcast_to([P, HB, NH]),
                                                    ALU.is_equal).then_inc(hi_ready, 1)

                        def select(i, q):
                            g, half = jn * halves + i * 4 + q, q % 2
                            dve.wait_ge(mm_ready, g + 1)
                            dve.wait_ge(hi_ready, g + 1)
                            dve.wait_ge(taken, g + 1)
                            ps = PS[half][:, 0:HB * c * NH].rearrange("p (u c t) -> p u c t", u=HB, c=c)
                            for cc in range(c):
                                last = nc.vector.tensor_tensor(prod[:, half, :, cc, :], ps[:, :, cc, :], ohh[:, half, :, :], ALU.mult)
                            last.then_inc(prod_ready, 1)

                        def add_up(i, q):
                            g, half = jn * halves + i * 4 + q, q % 2
                            dve.wait_ge(prod_ready, g + 3)
                            nc.vector.tensor_reduce(s_e[:, ds((i * 4 + q) * HB, HB), e0:e0 + c], prod[:, half, :, :, :], AX, ALU.add).then_inc(taken, 1)

                        def trip(i, begin, end_trip):
                            for q in range(4):
                                if q < 3:
                                    one_hots(i, q + 1)
                                elif not end_trip:
                                    one_hots(i + 1, 0)
                                select(i, q)
                                if q > 0:
                                    add_up(i, q - 1)
                                elif not begin:
                                    add_up(i - 1, 3)

                        one_hots(0, 0)
                        trip(0, True, False)
                        with nc.vector.Fori(1, trips - 1) as i:
                            trip(i, False, False)
                        trip(trips - 1, False, True)
                        add_up(trips - 1, 3)

                    credit(dve, taken, 2)
                    for jn, args in enumerate(jobs):
                        job(jn, *args)
                    dve.wait_ge(taken, len(jobs) * halves + 2)

                @block.tensor
                def _(pe):
                    credit(pe, prod_ready, 2)
                    for jn, (end, c0, c, e0) in enumerate(jobs):
                        with nc.tensor.Fori(0, trips) as i:
                            for q in range(4):
                                g, half = jn * halves + i * 4 + q, q % 2
                                pe.wait_ge(oht_ready, g + 5)
                                pe.wait_ge(prod_ready, g + 1)
                                for u in range(HB):
                                    for part in range(3):
                                        mm = nc.tensor.matmul(PS[half][:, u * c * NH:(u + 1) * c * NH], oht[:, half, u * P:(u + 1) * P],
                                                              s_bf[:, part, c0:c0 + c, :], start=(part == 0), stop=(part == 2))
                                mm.then_inc(mm_ready, 1)


        def gather_rows(pool, tab, width, idx_ready, rows_used, begun, per=1):
            base = g_base[0]
            credit(pool, rows_used, BODY // per)
            with nc.gpsimd.Fori(0, TRIPS) as i:
                for s in range(BODY):
                    if s % HB == 0:
                        pool.wait_ge(idx_ready, i * 2 + s // HB + 1)
                    if s % per == 0:
                        pool.wait_ge(rows_used, i * (BODY // per) + s // per + 1)
                    pool.sem_inc(begun, 1)
                    nc.gpsimd.indirect_dma_start(out=grow[:, s, 0:width], out_offset=None, in_=tab,
                                                 in_offset=bass.IndirectOffsetOnAxis(ap=idx_st[:, s // HB, s % HB:s % HB + 1], axis=0)
                                                 ).then_inc(g_ready[s], 16)
            g_base[0] = base + TRIPS

        def first_indices(act, idx_ready):
            for half in range(2):
                nc.scalar.copy(idx_st[:, half, :], srcT[:, half * HB:(half + 1) * HB]).then_inc(idx_ready, 1)

        def next_indices(act, i, half, gb, idx_ready):
            for u in range(HB):
                act.wait_ge(g_ready[half * HB + u], (gb + i + 1) * 16)
            nc.scalar.copy(idx_st[:, half, :], srcT[:, ds((i + 1) * BODY + half * HB, HB)]).then_inc(idx_ready, 1)

        def window_starts(i0, eng):
            return nc.values_load_multi_w_load_instructions(base_i[0:1, ds(i0, HB)], engines=[eng], min_val=0, max_val=NP - 1,
                                                                 skip_runtime_bounds_check_because="every destination is a node")[1]

        def aggregate(tag, tab, width, mode):
            names = "idx_ready products begun z_ready w_ready oh_ready win_free zeroed dve".split()
            idx_ready, products, begun, z_ready, w_ready, oh_ready, win_free, zeroed, dv = [sem(f"{tag}_{n}") for n in names]
            slots = 2 if mode == "one" else 3
            gb = g_base[0]
            zl = both[:, 0, 0:2 * HB * 2].rearrange("p (h u c) -> p h u c", h=2, u=HB)
            wl = both[:, 1, 0:2 * HB * 2].rearrange("p (h u c) -> p h u c", h=2, u=HB)
            oh2 = oh[:, :, :, :].rearrange("p a u n -> p (a u) n").rearrange("p (u a) n -> p u a n", a=2)
            with nc.Block() as block:
                @block.gpsimd
                def _(pool):
                    gather_rows(pool, tab, width, idx_ready, products, begun)

                @block.scalar
                def _(act):
                    first_indices(act, idx_ready)
                    with nc.scalar.Fori(0, TRIPS) as i:
                        for half in range(2):
                            if mode == "gat":
                                act.wait_ge(z_ready, i * 2 + half + 1)
                                nc.scalar.activation(wl[:, half, :, :], zl[:, half, :, :], ACT.Exp, scale=-1.0).then_inc(w_ready, 1)
                            next_indices(act, i, half, gb, idx_ready)

                @block.vector
                def _(dve):
                    nc.vector.memset(acc[:, :, :], 0.0).then_inc(zeroed, 1)
                    dve.wait_ge(zeroed, 1)
                    step = Chain(dve, dv)

                    def logits(i, half):
                        for u in range(HB):
                            dve.wait_ge(g_ready[half * HB + u], (gb + i + 1) * 16)
                        step(nc.vector.tensor_tensor(zl[:, half, :, :], grow[:, half * HB:(half + 1) * HB, F:F + 2],
                                                     s_e[:, ds(i * BODY + half * HB, HB), :], ALU.add))
                        nc.vector.scalar_tensor_tensor(zl[:, half, :, :], zl[:, half, :, :], 0.2, zl[:, half, :, :],
                                                       ALU.mult, ALU.max).then_inc(z_ready, 1)

                    def one_hot(i, half, u):
                        t = i * BODY + half * HB + u
                        d = dloc[:, ds(t, 1)]
                        if mode == "gat":
                            if u == 0:
                                dve.wait_ge(w_ready, i * 2 + half + 1)
                            for h in range(2):
                                last = nc.vector.tensor_scalar(oh2[:, u, h, :], iota_n[:, :], d, wl[:, half, u, h:h + 1],
                                                               ALU.is_equal, ALU.mult)
                        elif mode == "rel":
                            nc.vector.tensor_scalar(oh2[:, u, 0, :], iota_n[:, :], d, None, ALU.is_equal)
                            last = nc.vector.tensor_scalar(oh2[:, u, 1, :], iota_n[:, :], typT[:, ds(t, 1)], None, ALU.is_equal)
                        else:
                            last = nc.vector.tensor_scalar(oh2[:, u, 0, :], iota_n[:, :], d, w_e[:, ds(t, 1), 0:1].rearrange("p a b -> p (a b)"),
                                                           ALU.is_equal, ALU.mult)
                        last.then_inc(oh_ready, 1)

                    def add_window(i, half, u, first):
                        t = i * BODY + half * HB + u
                        dve.wait_ge(products, t + 1 + BODY)
                        dve.wait_ge(win_free, t + HB)
                        window = acc[:, 0:slots, ds(first[u], P)]
                        nc.vector.tensor_tensor(window, window, PS[u][:, 0:slots * P].rearrange("p (s n) -> p s n", s=slots),
                                                ALU.add).then_inc(win_free, 1)

                    def trip(i, end):
                        for half in range(2):
                            first = window_starts(i * BODY + half * HB, mybir.EngineType.DVE)
                            nxt = (i, 1) if half == 0 else None if end else (i + 1, 0)
                            if mode == "gat" and nxt:
                                logits(*nxt)
                            for u in range(HB):
                                add_window(i, half, u, first)
                                if nxt and (mode != "gat" or u):
                                    one_hot(*nxt, u - (mode == "gat"))
                            if nxt and mode == "gat":
                                one_hot(*nxt, HB - 1)

                    if mode == "gat":
                        logits(0, 0)
                    for u in range(HB):
                        one_hot(0, 0, u)
                    per = 2 if mode == "gat" else 0
                    with nc.vector.Fori(0, TRIPS - 1) as i:
                        step.enter(i, per)
                        trip(i, False)
                    step.leave(TRIPS - 1, per)
                    trip(TRIPS - 1, True)

                @block.tensor
                def _(pe):
                    credit(pe, win_free, HB)
                    with nc.tensor.Fori(0, TRIPS) as i:
                        for s in range(BODY):
                            u = s % HB
                            pe.wait_ge(g_ready[s], (gb + i + 1) * 16)
                            pe.wait_ge(oh_ready, i * BODY + s + 1)
                            pe.wait_ge(win_free, i * BODY + s + 1)
                            ps = PS[u]
                            for half in range(2):
                                rhs = oh2[:, u, half if mode == "gat" else 0, :]
                                mm = nc.tensor.matmul(ps[:, half * P:(half + 1) * P], grow[:, s, half * P:(half + 1) * P], rhs, start=True, stop=True)
                            if mode == "gat":
                                for h in range(2):
                                    mm = nc.tensor.matmul(ps[:, 2 * P:3 * P], sel[:, h, :], oh2[:, u, h, :], start=(h == 0), stop=(h == 1))
                            elif mode == "rel":
                                mm = nc.tensor.matmul(ps[:, 2 * P:3 * P], oh2[:, u, 1, :], oh2[:, u, 0, :], start=True, stop=True)
                            mm.then_inc(products, 1)

        def finish0():
            at, free, back, m_ready, e_ready, var_ready, std_ready, x_out, x_ready, dv = [
                sem("f0_" + n) for n in "at free back m_ready e_ready var_ready std_ready x_out x_ready dve".split()]
            with nc.Block() as block:
                @block.gpsimd
                def _(pool):
                    with nc.gpsimd.Fori(0, NG) as i:
                        for s in range(3):
                            last = nc.gpsimd.tensor_copy(accg[:, s, :], acc[:, s, ds(i * GRP * P, GRP * P)])
                        last.then_inc(at, 1)
                        pool.wait_ge(free, (i + 1) * GRP)

                @block.tensor
                def _(pe):
                    credit(pe, back, 1)
                    with nc.tensor.Fori(0, NG) as i:
                        pe.wait_ge(at, i + 1)
                        pe.wait_ge(back, i + 1)
                        for n in range(GRP):
                            for s in range(3):
                                mm = nc.tensor.transpose(PS[n][:, s * P:(s + 1) * P], accg[:, s, n * P:(n + 1) * P], ident[:, :])
                            mm.then_inc(free, 1)

                @block.vector
                def _(dve):
                    step = Chain(dve, dv)
                    rows, low = stage[:, 0, :, :], stage[:, 1, :, :]
                    den = small[:, 4:6, :].rearrange("p h n -> p n h")
                    with nc.vector.Fori(0, NG) as i:
                        step.enter(i, 7)
                        for n in range(GRP):
                            dve.wait_ge(free, i * GRP + n + 1)
                            last = nc.vector.tensor_scalar(den[:, n, :], PS[n][:, 2 * P:2 * P + 2], 1.0e-38, None, ALU.max)
                        step(last)
                        step(nc.vector.reciprocal(small[:, 6:8, :], small[:, 4:6, :]))
                        rden = small[:, 6:8, :].rearrange("p h n -> p n h")
                        for n in range(GRP):
                            for h in range(2):
                                last = nc.vector.tensor_scalar(rows[:, n, h * P:(h + 1) * P], PS[n][:, h * P:(h + 1) * P], rden[:, n, h:h + 1], None, ALU.mult)
                        last.then_inc(back, 1)
                        dve.wait_ge(back, i + 2)
                        nc.vector.tensor_scalar(low, rows, 0.0, None, ALU.min).then_inc(m_ready, 1)
                        dve.wait_ge(e_ready, i + 1)
                        step(nc.vector.scalar_tensor_tensor(rows, rows, 0.0, low, ALU.max, ALU.add))
                        step(nc.vector.scalar_tensor_tensor(rows, rows, -1.0, group_rows(X, i), ALU.add, ALU.add))
                        layer_norm(dve, step, rows, i, var_ready, std_ready, i + 1).then_inc(x_ready, 1)
                        dve.wait_ge(x_ready, i + 1)
                    step.leave(NG, 7)

                @block.scalar
                def _(act):
                    with nc.scalar.Fori(0, NG) as i:
                        act.wait_ge(m_ready, i + 1)
                        nc.scalar.activation(stage[:, 1, :, :], stage[:, 1, :, :], ACT.Exp).then_inc(e_ready, 1)
                        act_root(act, var_ready, std_ready, i + 1)

                @block.sync
                def _(sp):
                    with nc.sync.Fori(0, NG) as i:
                        sp.wait_ge(x_ready, i + 1)
                        sp.dma_start(table_rows(x_tab, i), group_rows(X, i)).then_inc(x_out, 16)
                    sp.wait_ge(x_out, NG * 16)


        def transpose_rows(pe, i, at, xt_free, xt_ready):
            pe.wait_ge(at, i + 1)
            for n in range(GRP):
                pe.wait_ge(xt_free, i * GRP + n + 1)
                for k in range(2):
                    mm = nc.tensor.transpose(PS[6 + n % 2][:, k * P:(k + 1) * P], xg[:, n, k * P:(k + 1) * P], ident[:, :])
                mm.then_inc(xt_ready, 1)

        def take_transposed(act, i, xt_ready, xt_free):
            for n in range(GRP):
                act.wait_ge(xt_ready, i * GRP + n + 1)
                nc.scalar.copy(xTg[:, :, n * P:(n + 1) * P], PS[6 + n % 2][:, 0:2 * P].rearrange("p (k c) -> p k c", k=2)).then_inc(xt_free, 1)

        def finish1():
            x_at, at, xt_ready, xt_free, mm_ready, mm_free, sig_ready, tanh_ask, tanh_ready, var_ready, std_ready, done, dv = [
                sem("f1_" + n) for n in "x_at at xt_ready xt_free mm_ready mm_free sig_ready tanh_ask tanh_ready var_ready std_ready done dve".split()]
            with nc.Block() as block:
                @block.gpsimd
                def _(pool):
                    def rows(i, n):
                        t = i * GRP + n
                        pool.wait_ge(xt_ready, t + 1)
                        nc.gpsimd.tensor_copy(xg[:, n, :], X[:, ds(t, 1), :].rearrange("p a f -> p (a f)")).then_inc(x_at, 1)

                    def sums(i, n):
                        t = i * GRP + n
                        pool.wait_ge(mm_ready, t + 1)
                        nc.gpsimd.tensor_copy(accg[:, :, n * P:(n + 1) * P], acc[:, :, ds(t * P, P)]).then_inc(at, 1)

                    for n in range(GRP):
                        rows(0, n)
                    for n in range(GRP):
                        sums(0, n)
                    with nc.gpsimd.Fori(1, NG) as i:
                        for n in range(GRP):
                            rows(i, n)
                            sums(i, n)

                @block.tensor
                def _(pe):
                    credit(pe, xt_ready, GRP)
                    credit(pe, mm_ready, GRP)
                    credit(pe, mm_free, 3)

                    def transposes(i, n):
                        t = i * GRP + n
                        pe.wait_ge(x_at, t + 1)
                        pe.wait_ge(xt_free, t + 1)
                        for k in range(2):
                            mm = nc.tensor.transpose(PS[6 + n % 2][:, k * P:(k + 1) * P], xg[:, n, k * P:(k + 1) * P], ident[:, :])
                        mm.then_inc(xt_ready, 1)

                    def products(i, n):
                        t = i * GRP + n
                        pe.wait_ge(at, t + 1)
                        pe.wait_ge(xt_free, t + 2)
                        pe.wait_ge(mm_free, t + 1 if n > 1 else t + 2)
                        rz, nn = PS[2 * (n % 3)], PS[2 * (n % 3) + 1]
                        cols = slice(n * P, (n + 1) * P)
                        for ps, c0, c1, gates in ((rz[:, :], 0, 512, "ih"), (nn[:, 0:F], 512, 768, "i"), (nn[:, F:512], 512, 768, "h")):
                            terms = []
                            if "i" in gates:
                                terms += [(accg[:, k, cols], wbig[:, 0, k, c0:c1]) for k in range(2)]
                                terms += [(accg[0:NREL, 2, cols], relw[:, c0:c1])]
                            if "h" in gates:
                                terms += [(xTg[:, k, cols], wbig[:, 1, k, c0:c1]) for k in range(2)]
                            for m, (left, right) in enumerate(terms):
                                mm = nc.tensor.matmul(ps, left, right, start=(m == 0), stop=(m == len(terms) - 1))
                        mm.then_inc(mm_ready, 1)

                    def group(i, end):
                        for n in range(GRP):
                            products(i, n)
                            if not end:
                                transposes(i + 1, n)

                    credit(pe, xt_free, 1)
                    for n in range(GRP):
                        transposes(0, n)
                    with nc.tensor.Fori(0, NG - 1) as i:
                        group(i, False)
                    group(NG - 1, True)

                @block.scalar
                def _(act):
                    def take_transposed_tile(i, n):
                        t = i * GRP + n
                        act.wait_ge(xt_ready, t + 1 + GRP)
                        act.wait_ge(mm_ready, t + 1)
                        nc.scalar.copy(xTg[:, :, n * P:(n + 1) * P], PS[6 + n % 2][:, 0:2 * P].rearrange("p (k c) -> p k c", k=2)).then_inc(xt_free, 1)

                    def group(i, end):
                        for n in range(0 if end else GRP):
                            take_transposed_tile(i + 1, n)
                        act.wait_ge(mm_free, (i + 1) * GRP + 3)
                        nc.scalar.activation(g5[:, :, 0:512], g5[:, :, 0:512], ACT.Sigmoid).then_inc(sig_ready, 1)
                        act.wait_ge(tanh_ask, i + 1)
                        nc.scalar.activation(stage[:, 0, :, :], stage[:, 0, :, :], ACT.Tanh).then_inc(tanh_ready, 1)
                        act_root(act, var_ready, std_ready, i + 1)

                    for n in range(GRP):
                        take_transposed_tile(0, n)
                    with nc.scalar.Fori(0, NG - 1) as i:
                        group(i, False)
                    group(NG - 1, True)

                @block.vector
                def _(dve):
                    step = Chain(dve, dv)
                    step(nc.vector.tensor_tensor(bc_t[:, 0:512], bc_t[:, 0:512], bc_b[:, 0:512], ALU.add))
                    nn, u = stage[:, 0, :, :], stage[:, 1, :, :]
                    r, z, n_i, n_h = (g5[:, :, q * F:(q + 1) * F] for q in range(4))
                    with nc.vector.Fori(0, NG) as i:
                        step.enter(i, 8)
                        for n in range(GRP):
                            dve.wait_ge(mm_ready, (i + 1) * GRP + n + 1)
                            nc.vector.tensor_tensor(g5[:, n, 0:512], PS[2 * (n % 3)][:, :], bc_t[:, 0:512], ALU.add)
                            nc.vector.tensor_tensor(n_i[:, n, :], PS[2 * (n % 3) + 1][:, 0:F], bc_t[:, 512:768], ALU.add)
                            last = nc.vector.tensor_tensor(n_h[:, n, :], PS[2 * (n % 3) + 1][:, F:512], bc_b[:, 512:768], ALU.add)
                            last.then_inc(mm_free, 1)
                        dve.wait_ge(mm_free, (i + 1) * GRP + 3)
                        dve.wait_ge(sig_ready, i + 1)
                        step(nc.vector.tensor_tensor(nn, r, n_h, ALU.mult))
                        nc.vector.tensor_tensor(nn, nn, n_i, ALU.add).then_inc(tanh_ask, 1)
                        dve.wait_ge(tanh_ready, i + 1)
                        step(nc.vector.tensor_tensor(u, group_rows(X, i), nn, ALU.subtract))
                        step(nc.vector.tensor_tensor(u, u, z, ALU.mult))
                        step(nc.vector.tensor_tensor(nn, nn, u, ALU.add))
                        step(nc.vector.tensor_tensor(nn, nn, group_rows(X, i), ALU.add))
                        layer_norm(dve, step, nn, i, var_ready, std_ready, i + 1).then_inc(done, 1)
                        dve.wait_ge(done, i + 1)
                    step.leave(NG, 8)

        def project2():
            at, xt_ready, xt_free, mm_ready, mm_free, nrm_ask, nrm_ready, h_ready, h_out, dv = [
                sem("p2_" + n) for n in "at xt_ready xt_free mm_ready mm_free nrm_ask nrm_ready h_ready h_out dve".split()]
            with nc.Block() as block:
                @block.gpsimd
                def _(pool):
                    with nc.gpsimd.Fori(0, NG) as i:
                        nc.gpsimd.tensor_copy(xg[:, :, :], group_rows(X, i)).then_inc(at, 1)
                        pool.wait_ge(xt_ready, (i + 1) * GRP)

                @block.tensor
                def _(pe):
                    credit(pe, xt_free, 2)
                    credit(pe, mm_free, GRP)
                    with nc.tensor.Fori(0, NG) as i:
                        transpose_rows(pe, i, at, xt_free, xt_ready)
                        for n in range(GRP):
                            pe.wait_ge(xt_free, i * GRP + n + 3)
                            pe.wait_ge(mm_free, i * GRP + n + 1)
                            for k in range(2):
                                mm = nc.tensor.matmul(PS[n][:, 0:F + 1], xTg[:, k, n * P:(n + 1) * P], w2T[:, k, :], start=(k == 0), stop=(k == 1))
                            mm.then_inc(mm_ready, 1)

                @block.scalar
                def _(act):
                    with nc.scalar.Fori(0, NG) as i:
                        take_transposed(act, i, xt_ready, xt_free)
                        act.wait_ge(nrm_ask, i + 1)
                        nc.scalar.activation(small[:, 5, :], small[:, 5, :], ACT.Sqrt)
                        nc.scalar.activation(small[:, 4, :], small[:, 4, :], ACT.Sigmoid).then_inc(nrm_ready, 1)
                        act.wait_ge(mm_ready, (i + 1) * GRP)

                @block.vector
                def _(dve):
                    step = Chain(dve, dv)
                    hr, sq, mag, nrm = stage[:, 0, :, :], stage[:, 1, :, :], small[:, 4, :], small[:, 5, :]
                    with nc.vector.Fori(0, NG) as i:
                        step.enter(i, 8)
                        for n in range(GRP):
                            dve.wait_ge(mm_ready, i * GRP + n + 1)
                            nc.vector.tensor_tensor(hr[:, n, :], PS[n][:, 0:F], bc_b2[:, 0:F], ALU.add)
                            nc.vector.tensor_tensor(mag[:, n:n + 1], PS[n][:, F:F + 1], bc_b2[:, F:F + 1], ALU.add).then_inc(mm_free, 1)
                        dve.wait_ge(mm_free, (i + 2) * GRP)
                        step(nc.vector.tensor_tensor(sq, hr, hr, ALU.mult))
                        nc.vector.tensor_reduce(nrm, sq, AX, ALU.add).then_inc(nrm_ask, 1)
                        dve.wait_ge(nrm_ready, i + 1)
                        step(nc.vector.tensor_scalar(nrm, nrm, 1.0e-12, None, ALU.max))
                        step(nc.vector.reciprocal(small[:, 6, :], nrm))
                        step(nc.vector.scalar_tensor_tensor(small[:, 7, :], mag, 1.5, small[:, 6, :], ALU.mult, ALU.mult))
                        nc.vector.tensor_tensor(group_rows(H, i), hr, bc_last(small[:, 7, :], F), ALU.mult).then_inc(h_ready, 1)
                        dve.wait_ge(h_ready, i + 1)
                        for st in range(2):
                            step(nc.vector.tensor_tensor(sq, group_rows(H, i), bc_a2[:, st, :].unsqueeze(1).broadcast_to([P, GRP, F]), ALU.mult))
                            step(nc.vector.tensor_reduce(s_tab[:, ds(i * GRP, GRP), st:st + 1].rearrange("p t a -> p (t a)"), sq, AX, ALU.add))
                    step.leave(NG, 8)
                    split3(step, 2)

                @block.sync
                def _(sp):
                    with nc.sync.Fori(0, NG) as i:
                        sp.wait_ge(h_ready, i + 1)
                        sp.dma_start(table_rows(h2_tab, i), group_rows(H, i)).then_inc(h_out, 16)
                    sp.wait_ge(h_out, NG * 16)

        xc, Rc, Tc = (accf[0:CP, q * H3 * CL:(q + 1) * H3 * CL].rearrange("p (h e) -> p h e", h=H3) for q in range(3))

        def edge_softmax(tag, heads, scale, eps, least, read):
            c_ready, c_taken, l_ask, l_ready, b_ask, b_ready, e_ask, e_ready, w_ask, w_ready, w_taken, dv = [
                sem(f"{tag}_{n}") for n in "c_ready c_taken l_ask l_ready b_ask b_ready e_ask e_ready w_ask w_ready w_taken dve".split()]

            def carries(dve, step, n, backward, maximum):
                dve.wait_ge(l_ready, n + 1)
                step(nc.vector.tensor_copy(rowc[0:heads, 1, 0:CP], PS[4][0:heads, 0:CP]))
                start = -BIG if maximum else 0.0
                op0, op1 = (ALU.add, ALU.max) if maximum else (ALU.mult, ALU.add)
                keep = allr[0:heads, 2 if maximum else (1 if backward else 0), :]
                if backward:
                    nc.vector.memset(rowc[0:heads, 0, CP:CP + 1], start)
                    nc.vector.tensor_tensor_scan(rowc[0:heads, 0, 0:CP][:, ::-1], keep[:, ::-1], rowc[0:heads, 1, 0:CP][:, ::-1], start, op0, op1).then_inc(b_ask, 1)
                else:
                    nc.vector.memset(rowc[0:heads, 0, 0:1], start)
                    nc.vector.tensor_tensor_scan(rowc[0:heads, 0, 1:CP + 1], keep, rowc[0:heads, 1, 0:CP], start, op0, op1).then_inc(b_ask, 1)
                dve.wait_ge(b_ready, n + 1)
                step(nc.vector.tensor_copy(carry[:, 0:heads], PS[5][0:CP, 0:heads]))

            def totals(dve, step, n, maximum):
                op0, op1 = (ALU.add, ALU.max) if maximum else (ALU.mult, ALU.add)
                keep = pen if maximum else cont
                for again in range(2):
                    for h in range(heads):
                        start = carry[:, h:h + 1] if again else (-BIG if maximum else 0.0)
                        last = nc.vector.tensor_tensor_scan(Rc[:, h, :], keep[:, :], xc[:, h, :], start, op0, op1)
                    step(last)
                    if not again:
                        nc.vector.tensor_copy(lastv[:, 0:heads], Rc[:, 0:heads, CL - 1:CL].rearrange("p h e -> p (h e)")).then_inc(l_ask, 1)
                        carries(dve, step, n, False, maximum)
                step(nc.vector.tensor_tensor(Tc[:, 0:heads, :], Rc[:, 0:heads, :], notn[:, :].unsqueeze(1).broadcast_to([CP, heads, CL]), ALU.mult))
                for again in range(2):
                    for h in range(heads):
                        start = carry[:, h:h + 1] if again else 0.0
                        last = nc.vector.tensor_tensor_scan(Rc[:, h, :][:, ::-1], contn[:, :][:, ::-1], Tc[:, h, :][:, ::-1], start, ALU.mult, ALU.add)
                    step(last)
                    if not again:
                        nc.vector.tensor_copy(lastv[:, 0:heads], Rc[:, 0:heads, 0:1].rearrange("p h e -> p (h e)")).then_inc(l_ask, 1)
                        carries(dve, step, n + 1, True, False)

            with nc.Block() as block:
                @block.vector
                def _(dve):
                    step = Chain(dve, dv)
                    for h in range(heads):
                        dve.wait_ge(c_ready, h + 1)
                        nc.vector.tensor_scalar(xc[:, h, :], PS[h][0:CP, :], scale, None, ALU.mult).then_inc(c_taken, 1)
                    dve.wait_ge(c_taken, heads)
                    totals(dve, step, 0, True)
                    if least is not None:
                        step(nc.vector.tensor_scalar(Rc[:, 0:heads, :], Rc[:, 0:heads, :], least, None, ALU.max))
                    nc.vector.tensor_tensor(xc[:, 0:heads, :], xc[:, 0:heads, :], Rc[:, 0:heads, :], ALU.subtract).then_inc(e_ask, 1)
                    dve.wait_ge(e_ready, 1)
                    totals(dve, step, 2, False)
                    step(nc.vector.tensor_scalar(Rc[:, 0:heads, :], Rc[:, 0:heads, :], eps, None, ALU.add))
                    step(nc.vector.reciprocal(Tc[:, 0:heads, :], Rc[:, 0:heads, :]))
                    nc.vector.tensor_tensor(xc[:, 0:heads, :], xc[:, 0:heads, :], Tc[:, 0:heads, :], ALU.mult).then_inc(w_ask, 1)
                    for h in range(heads):
                        dve.wait_ge(w_ready, h + 1)
                        nc.vector.tensor_copy(w_e[:, :, h].rearrange("q (p j) -> q j p", j=J), PS[h][:, 0:ET].rearrange("q (j p) -> q j p", j=J)).then_inc(w_taken, 1)
                    dve.wait_ge(w_taken, heads)

                @block.scalar
                def _(act):
                    act.wait_ge(e_ask, 1)
                    nc.scalar.activation(xc[:, 0:heads, :], xc[:, 0:heads, :], ACT.Exp).then_inc(e_ready, 1)

                @block.tensor
                def _(pe):
                    for h in range(heads):
                        for j in range(J):
                            mm = nc.tensor.transpose(PS[h][0:CP, j * P:(j + 1) * P], read(h)[:, j::J], ident[:, :])
                        mm.then_inc(c_ready, 1)
                    for n in range(4):
                        pe.wait_ge(l_ask, n + 1)
                        nc.tensor.transpose(PS[4][0:heads, 0:CP], lastv[:, 0:heads], ident[0:CP, 0:CP]).then_inc(l_ready, 1)
                        pe.wait_ge(b_ask, n + 1)
                        row = rowc[0:heads, 0, 1:CP + 1] if n % 2 else rowc[0:heads, 0, 0:CP]
                        nc.tensor.transpose(PS[5][0:CP, 0:heads], row, ident[0:heads, 0:heads]).then_inc(b_ready, 1)
                    pe.wait_ge(w_ask, 1)
                    for h in range(heads):
                        for j in range(J):
                            mm = nc.tensor.transpose(PS[h][:, j * CP:(j + 1) * CP], xc[:, h, j * P:(j + 1) * P], ident[0:CP, 0:CP])
                        mm.then_inc(w_ready, 1)

        def sum_scores():
            dv = sem("score_sum")
            with nc.Block() as block:
                @block.vector
                def _(dve):
                    nc.vector.tensor_tensor(s_e[:, :, 0], s_e[:, :, 0], s_e[:, :, 1], ALU.add).then_inc(dv, 1)
                    dve.wait_ge(dv, 1)

        def finish2():
            at, free, back, n_ask, n_ready, t_ready, m_ask, m_ready, var_ready, std_ready, done, dv = [
                sem("f2_" + n) for n in "at free back n_ask n_ready t_ready m_ask m_ready var_ready std_ready done dve".split()]
            with nc.Block() as block:
                @block.gpsimd
                def _(pool):
                    with nc.gpsimd.Fori(0, NG) as i:
                        for s in range(2):
                            last = nc.gpsimd.tensor_copy(accg[:, s, :], acc[:, s, ds(i * GRP * P, GRP * P)])
                        last.then_inc(at, 1)
                        pool.wait_ge(free, (i + 1) * GRP)

                @block.tensor
                def _(pe):
                    credit(pe, back, GRP)
                    with nc.tensor.Fori(0, NG) as i:
                        pe.wait_ge(at, i + 1)
                        for n in range(GRP):
                            pe.wait_ge(back, i * GRP + n + 1)
                            for s in range(2):
                                mm = nc.tensor.transpose(PS[n][:, s * P:(s + 1) * P], accg[:, s, n * P:(n + 1) * P], ident[:, :])
                            mm.then_inc(free, 1)

                @block.vector
                def _(dve):
                    step = Chain(dve, dv)
                    hc, sq, nrm, tmp = stage[:, 0, :, :], stage[:, 1, :, :], small[:, 4, :], small[:, 6, :]
                    with nc.vector.Fori(0, NG) as i:
                        step.enter(i, 16)
                        for n in range(GRP):
                            dve.wait_ge(free, i * GRP + n + 1)
                            nc.vector.tensor_tensor(hc[:, n, :], PS[n][:, 0:F], H[:, ds(i * GRP + n, 1), :].rearrange("p a f -> p (a f)"), ALU.add).then_inc(back, 1)
                        dve.wait_ge(back, (i + 2) * GRP)
                        step(nc.vector.tensor_tensor(sq, hc, hc, ALU.mult))
                        nc.vector.tensor_reduce(nrm, sq, AX, ALU.add).then_inc(n_ask, 1)
                        dve.wait_ge(n_ready, i + 1)
                        step(nc.vector.tensor_scalar(nrm, nrm, 1.0e-15, None, ALU.max))
                        nc.vector.reciprocal(tmp, nrm).then_inc(m_ask, 1)
                        dve.wait_ge(t_ready, i + 1)
                        step(nc.vector.tensor_tensor(tmp, tmp, small[:, 5, :], ALU.mult))
                        step(nc.vector.tensor_tensor(hc, hc, bc_last(tmp, F), ALU.mult))
                        step(nc.vector.tensor_tensor(sq, hc, hc, ALU.mult))
                        nc.vector.tensor_reduce(nrm, sq, AX, ALU.add).then_inc(n_ask, 1)
                        dve.wait_ge(m_ready, i + 1)
                        step(nc.vector.tensor_scalar(tmp, nrm, 1.0e-8, None, ALU.add))
                        step(nc.vector.reciprocal(small[:, 7, :], tmp))
                        step(nc.vector.tensor_scalar(tmp, small[:, 7, :], 0.95, -1.0, ALU.mult, ALU.add))
                        step(nc.vector.tensor_scalar(nrm, nrm, 0.95, None, ALU.is_gt))
                        step(nc.vector.tensor_tensor(tmp, tmp, nrm, ALU.mult))
                        step(nc.vector.tensor_scalar(tmp, tmp, 1.0, None, ALU.add))
                        step(nc.vector.tensor_tensor(hc, hc, bc_last(tmp, F), ALU.mult))
                        step(nc.vector.tensor_tensor(hc, hc, group_rows(X, i), ALU.add))
                        layer_norm(dve, step, hc, i, var_ready, std_ready, i + 1).then_inc(done, 1)
                        dve.wait_ge(done, i + 1)
                    step.leave(NG, 16)

                @block.scalar
                def _(act):
                    nrm = small[:, 4, :]
                    with nc.scalar.Fori(0, NG) as i:
                        act.wait_ge(n_ask, i * 2 + 1)
                        nc.scalar.activation(nrm, nrm, ACT.Sqrt).then_inc(n_ready, 1)
                        act.wait_ge(m_ask, i + 1)
                        nc.scalar.activation(small[:, 5, :], nrm, ACT.Tanh).then_inc(t_ready, 1)
                        act.wait_ge(n_ask, i * 2 + 2)
                        nc.scalar.activation(nrm, nrm, ACT.Sqrt).then_inc(m_ready, 1)
                        act_root(act, var_ready, std_ready, i + 1)

        def project3(layer, rows):
            ln = str(layer)
            ld, at, xt_ready, xt_free, mm_ready, mm_free, q_out, dv = [
                sem(f"p3{ln}_{n}") for n in "ld at xt_ready xt_free mm_ready mm_free q_out dve".split()]
            wq = wbig[:, :, :, :].rearrange("p a k f -> p (a k f)")[:, 0:2048].rearrange("p (k f) -> p k f", k=2)
            with nc.Block() as block:
                @block.sync
                def _(sp):
                    for n, letter in enumerate("qkvs"):
                        sp.dma_start(wq[:, :, n * F:(n + 1) * F], a[f"L3_gnn_W{letter}{ln}"].rearrange("(k p) f -> p k f", p=P)).then_inc(ld, 16)
                        sp.dma_start(bc_b[:, n * F:(n + 1) * F], a[f"L3_gnn_b{letter}{ln}"].unsqueeze(0).broadcast_to([P, F])).then_inc(ld, 16)
                    sp.dma_start(bc_b2[:, 0:F], a[f"L3_gnn_be{ln}"].unsqueeze(0).broadcast_to([P, F])).then_inc(ld, 16)
                    sp.dma_start(we[:, :], a[f"L3_gnn_We{ln}"]).then_inc(ld, 16)
                    with nc.sync.Fori(0, NG) as i:
                        sp.wait_ge(mm_free, (i + 1) * GRP * 2 + 6)
                        for n, tab in enumerate((q_tab, k_tab, v_tab)):
                            sp.dma_start(table_rows(tab, i), g5[:, :, n * F:(n + 1) * F]).then_inc(q_out, 16)
                    sp.wait_ge(q_out, NG * 48)

                @block.gpsimd
                def _(pool):
                    with nc.gpsimd.Fori(0, NG) as i:
                        nc.gpsimd.tensor_copy(xg[:, :, :], group_rows(rows, i)).then_inc(at, 1)
                        pool.wait_ge(xt_ready, (i + 1) * GRP)

                @block.tensor
                def _(pe):
                    credit(pe, xt_free, 2)
                    credit(pe, mm_free, 6)
                    pe.wait_ge(ld, 160)
                    with nc.tensor.Fori(0, NG) as i:
                        transpose_rows(pe, i, at, xt_free, xt_ready)
                        for n in range(GRP):
                            pe.wait_ge(xt_free, i * GRP + n + 3)
                            for b in range(2):
                                pe.wait_ge(mm_free, (i * GRP + n) * 2 + b + (1 if n > 1 else 3))
                                for k in range(2):
                                    mm = nc.tensor.matmul(PS[2 * (n % 3) + b][:, :], xTg[:, k, n * P:(n + 1) * P], wq[:, k, b * 512:(b + 1) * 512], start=(k == 0), stop=(k == 1))
                                mm.then_inc(mm_ready, 1)

                @block.scalar
                def _(act):
                    with nc.scalar.Fori(0, NG) as i:
                        for n in range(GRP):
                            act.wait_ge(xt_ready, i * GRP + n + 1)
                            nc.scalar.copy(xTg[:, :, n * P:(n + 1) * P], PS[6 + n % 2][:, 0:2 * P].rearrange("p (k c) -> p k c", k=2)).then_inc(xt_free, 1)
                        act.wait_ge(mm_ready, (i + 1) * GRP * 2)

                @block.vector
                def _(dve):
                    step = Chain(dve, dv)
                    dve.wait_ge(ld, 160)
                    nc.vector.tensor_tensor(bc_b[:, F:2 * F], bc_b[:, F:2 * F], bc_b2[:, 0:F], ALU.add)
                    step(nc.vector.tensor_tensor(bc_b[:, 2 * F:3 * F], bc_b[:, 2 * F:3 * F], bc_b2[:, 0:F], ALU.add))
                    with nc.vector.Fori(0, NG) as i:
                        for n in range(GRP):
                            dve.wait_ge(mm_ready, (i * GRP + n) * 2 + 1)
                            nc.vector.tensor_tensor(g5[:, n, 0:512], PS[2 * (n % 3)][:, :], bc_b[:, 0:512], ALU.add).then_inc(mm_free, 1)
                            dve.wait_ge(mm_ready, (i * GRP + n) * 2 + 2)
                            nc.vector.tensor_tensor(H[:, ds(i * GRP + n, 1), :].rearrange("p a f -> p (a f)"), PS[2 * (n % 3) + 1][:, F:2 * F], bc_b[:, 3 * F:4 * F], ALU.add)
                            nc.vector.tensor_tensor(g5[:, n, 2 * F:3 * F], PS[2 * (n % 3) + 1][:, 0:F], bc_b[:, 2 * F:3 * F], ALU.add).then_inc(mm_free, 1)
                        dve.wait_ge(q_out, (i + 1) * 48)

        a_ready = [lasting_sem(f"a_ready{h}") for h in range(2)]
        a_base, w_base = [0], [0]
        attr = a["edge_attr_128"]

        def load_attributes(sp, i, half, end=False):
            t0 = i * BODY + half * HB
            sp.dma_start(arow[:, half * HB:(half + 1) * HB - 1, :],
                         attr[ds(t0 * P, (HB - 1) * P), :].rearrange("(t p) c -> p t c", p=P)).then_inc(a_ready[half], 16)
            n = E - (ET - 1) * P if end else P
            sp.dma_start(arow[0:n, (half + 1) * HB - 1, :], attr[ds((t0 + HB - 1) * P, n), :]).then_inc(a_ready[half], 16)

        PAIRS = BODY // 2
        HP = HB // 2

        def scores3(tag):
            names = "idx_ready begun places_even places_odd oht_ready tr_ready tr_taken terms_ready rows_used terms_used sums_done".split()
            idx_ready, begun, places_even, places_odd, oht_ready, tr_ready, tr_taken, terms_ready, rows_used, terms_used, sums_done = [
                sem(f"{tag}_{n}") for n in names]
            gb, ab, wb = g_base[0], a_base[0], w_base[0]
            place_b = places[:, :, :].bitcast(BF16)
            sums = accf[:, 0:BODY // 2 * F].rearrange("p (u f) -> p u f", f=F)
            ohT = oh[:, :, :, :].rearrange("p a u n -> p a (u n)")
            with nc.Block() as block:
                @block.gpsimd
                def _(pool):
                    gather_rows(pool, k_tab, F, idx_ready, rows_used, begun, per=2)

                @block.sync
                def _(sp):
                    def half_body(i, half, end=False):
                        t0 = i * BODY + half * HB
                        sp.wait_ge(oht_ready, i * 2 + half + 1)
                        sp.dma_start(place_b[:, half, :], lo_tab[2:3, ds(t0 * P, HB * P)].broadcast_to([P, HB * P])
                                     ).then_inc((places_even, places_odd)[half], 16)
                        sp.wait_ge(tr_ready, i * PAIRS + half * HP + HP)
                        load_attributes(sp, i, half, end)
                        first = window_starts(t0, mybir.EngineType.SP)
                        for u in range(HB):
                            if u % 2 == 0:
                                sp.wait_ge(terms_ready, i * PAIRS + half * HP + u // 2 + 1)
                            sp.dma_start(qrow[:, u, :], q_tab[ds(first[u], P), :]).then_inc(q_ready[u], 16)
                    credit(sp, oht_ready, 2)
                    credit(sp, tr_ready, PAIRS)
                    credit(sp, terms_ready, HP)
                    with nc.sync.Fori(0, TRIPS - 1) as i:
                        for half in range(2):
                            half_body(i, half)
                    half_body(TRIPS - 1, 0)
                    half_body(TRIPS - 1, 1, end=True)

                @block.scalar
                def _(act):
                    first_indices(act, idx_ready)
                    with nc.scalar.Fori(0, TRIPS) as i:
                        for j in range(PAIRS):
                            k = i * PAIRS + j
                            act.wait_ge(tr_ready, k + 1 + PAIRS)
                            act.wait_ge(terms_ready, k + 1 + HP - 2)
                            nc.scalar.copy(aT[:, (j % 2) * 2:(j % 2) * 2 + 2, :],
                                           PS[j % 2][:, 0:2 * P].rearrange("p (u c) -> p u c", u=2)).then_inc(tr_taken, 1)
                            if j % HP == HP - 1:
                                next_indices(act, i, j // HP, gb, idx_ready)

                @block.tensor
                def _(pe):
                    credit(pe, tr_taken, 2)
                    credit(pe, terms_used, 4)

                    def transposes(i, j):
                        if j % HP == 0:
                            pe.wait_ge(a_ready[j // HP], (ab + i + 1) * 32)
                        pe.wait_ge(tr_taken, i * PAIRS + j + 1)
                        for v in range(2):
                            mm = nc.tensor.transpose(PS[j % 2][:, v * P:(v + 1) * P], arow[:, 2 * j + v, :], ident[:, :])
                        mm.then_inc(tr_ready, 1)

                    def terms(i, j):
                        k = i * PAIRS + j
                        pe.wait_ge(tr_taken, k + 3)
                        pe.wait_ge(rows_used, k + PAIRS - 1)
                        for v in range(2):
                            nc.tensor.matmul(PS[2 + j % 2][:, v * F:(v + 1) * F], aT[:, (2 * j + v) % 4, :], we[:, :], start=True, stop=True)
                        pe.wait_ge(terms_used, k + 1)
                        if j % HP == 0:
                            pe.wait_ge(oht_ready, i * 2 + j // HP + 3)
                        for v in range(2):
                            u = (2 * j + v) % HB
                            pe.wait_ge(q_ready[u], (wb + i * 2 + j // HP + 1) * 16)
                            mm = nc.tensor.matmul(PS[4 + j % 4][:, v * F:(v + 1) * F], ohT[:, j // HP, u * P:(u + 1) * P], qrow[:, u, :], start=True, stop=True)
                        mm.then_inc(terms_ready, 1)

                    def trip(i, end):
                        for j in range(PAIRS):
                            if j + 1 < PAIRS:
                                transposes(i, j + 1)
                            elif not end:
                                transposes(i + 1, 0)
                            terms(i, j)

                    transposes(0, 0)
                    with nc.tensor.Fori(0, TRIPS - 1) as i:
                        trip(i, False)
                    trip(TRIPS - 1, True)

                @block.vector
                def _(dve):
                    def one_hots(i, half):
                        dve.wait_ge((places_even, places_odd)[half], (i + 1) * 16)
                        nc.vector.tensor_scalar(ohT[:, half, :], place_b[:, half, :], iota_p[:, 0:1], None, ALU.is_equal).then_inc(oht_ready, 1)

                    def add_rows(i, j):
                        k, s = i * PAIRS + j, 2 * j
                        dve.wait_ge(terms_ready, k + 1 + HP)
                        for v in range(2):
                            dve.wait_ge(g_ready[s + v], (gb + i + 1) * 16)
                        dve.wait_ge(sums_done, k + 1)
                        nc.vector.tensor_tensor(sums[:, s % 8:s % 8 + 2, :], grow[:, s:s + 2, 0:F], PS[2 + j % 2][:, :].rearrange("p (u f) -> p u f", u=2),
                                                ALU.add).then_inc(rows_used, 1)

                    def times_q(i, j):
                        k, two = i * PAIRS + j, sums[:, (2 * j) % 8:(2 * j) % 8 + 2, :]
                        dve.wait_ge(rows_used, k + 1 + PAIRS)
                        nc.vector.tensor_tensor(two, two, PS[4 + j % 4][:, :].rearrange("p (u f) -> p u f", u=2), ALU.mult
                                                ).then_inc(terms_used, 1)

                    def sum_channels(i, j):
                        k, two = i * PAIRS + j, sums[:, (2 * j) % 8:(2 * j) % 8 + 2, :]
                        dve.wait_ge(terms_used, k + 1 + 4)
                        nc.vector.tensor_reduce(w_e[:, ds(i * BODY + 2 * j, 2), :], two.rearrange("p u (h c) -> p u h c", h=H3),
                                                AX, ALU.add).then_inc(sums_done, 1)

                    def trip(i, begin, end):
                        for j in range(PAIRS):
                            if j == 0:
                                one_hots(i, 1)
                            if j == HP and not end:
                                one_hots(i + 1, 0)
                            if j + 1 < PAIRS:
                                add_rows(i, j + 1)
                            elif not end:
                                add_rows(i + 1, 0)
                            times_q(i, j)
                            if j > 0:
                                sum_channels(i, j - 1)
                            elif not begin:
                                sum_channels(i - 1, PAIRS - 1)

                    credit(dve, sums_done, 4)
                    one_hots(0, 0)
                    add_rows(0, 0)
                    trip(0, True, False)
                    with nc.vector.Fori(1, TRIPS - 1) as i:
                        trip(i, False, False)
                    trip(TRIPS - 1, False, True)
                    sum_channels(TRIPS - 1, PAIRS - 1)
                    dve.wait_ge(sums_done, ET // 2 + 4)
            a_base[0] += TRIPS
            w_base[0] += 2 * TRIPS

        def messages3(tag):
            names = "idx_ready begun tr_ready tr_taken e_ready rows_used msg_ready msg_act_ready oh_ready products win_free zeroed".split()
            idx_ready, begun, tr_ready, tr_taken, e_ready, rows_used, msg_ready, msg_act_ready, oh_ready, products, win_free, zeroed = [
                sem(f"{tag}_{n}") for n in names]
            gb, ab = g_base[0], a_base[0]
            msgs = qrow
            with nc.Block() as block:
                @block.gpsimd
                def _(pool):
                    gather_rows(pool, v_tab, F, idx_ready, rows_used, begun, per=2)

                @block.sync
                def _(sp):
                    def half_body(i, half, end=False):
                        sp.wait_ge(tr_ready, i * PAIRS + half * HP + HP)
                        load_attributes(sp, i, half, end)
                    credit(sp, tr_ready, PAIRS)
                    with nc.sync.Fori(0, TRIPS - 1) as i:
                        for half in range(2):
                            half_body(i, half)
                    half_body(TRIPS - 1, 0)
                    half_body(TRIPS - 1, 1, end=True)

                @block.scalar
                def _(act):
                    def take_transposed_pair(i, j):
                        k = i * PAIRS + j
                        act.wait_ge(tr_ready, k + 1 + PAIRS)
                        act.wait_ge(e_ready, k + 1)
                        nc.scalar.copy(aT[:, (j % 2) * 2:(j % 2) * 2 + 2, :],
                                       PS[j % 2][:, 0:2 * P].rearrange("p (u c) -> p u c", u=2)).then_inc(tr_taken, 1)

                    def weight_last_heads(i, j):
                        act.wait_ge(rows_used, i * PAIRS + j + 1 + PAIRS)
                        for v in range(2):
                            s = 2 * j + v
                            for h in range(DVE_HEADS, H3):
                                msg = msgs[:, s % 8, h * C3:(h + 1) * C3]
                                last = nc.scalar.activation(msg, msg, ACT.Copy, scale=w_e[:, ds(i * BODY + s, 1), h:h + 1].rearrange("p a h -> p (a h)"))
                        last.then_inc(msg_act_ready, 1)

                    def trip(i, end):
                        for j in range(PAIRS):
                            weight_last_heads(i, j)
                            if j + 3 < PAIRS:
                                take_transposed_pair(i, j + 3)
                            elif not end:
                                take_transposed_pair(i + 1, j + 3 - PAIRS)
                            if j % HP == 1:
                                next_indices(act, i, j // HP, gb, idx_ready)

                    first_indices(act, idx_ready)
                    for j in range(3):
                        take_transposed_pair(0, j)
                    with nc.scalar.Fori(0, TRIPS - 1) as i:
                        trip(i, False)
                    trip(TRIPS - 1, True)

                @block.tensor
                def _(pe):
                    credit(pe, tr_taken, 2)
                    credit(pe, e_ready, 2)
                    credit(pe, win_free, 4)

                    def transposes(i, j):
                        if j % HP == 0:
                            pe.wait_ge(a_ready[j // HP], (ab + i + 1) * 32)
                        pe.wait_ge(tr_taken, i * PAIRS + j + 1)
                        for v in range(2):
                            mm = nc.tensor.transpose(PS[j % 2][:, v * P:(v + 1) * P], arow[:, 2 * j + v, :], ident[:, :])
                        mm.then_inc(tr_ready, 1)

                    def edge_terms(i, j):
                        k = i * PAIRS + j
                        pe.wait_ge(tr_taken, k + 3)
                        pe.wait_ge(rows_used, k + PAIRS - 1)
                        for v in range(2):
                            mm = nc.tensor.matmul(PS[2 + j % 2][:, v * F:(v + 1) * F], aT[:, (2 * j + v) % 4, :], we[:, :], start=True, stop=True)
                        mm.then_inc(e_ready, 1)

                    def windows(i, j):
                        k = i * PAIRS + j
                        pe.wait_ge(msg_ready, k + 1)
                        pe.wait_ge(msg_act_ready, k + 1)
                        for v in range(2):
                            s = 2 * j + v
                            pe.wait_ge(oh_ready, i * BODY + s + 1)
                            pe.wait_ge(win_free, i * BODY + s + 1)
                            for half in range(2):
                                mm = nc.tensor.matmul(PS[4 + s % 4][:, half * P:(half + 1) * P], msgs[:, s % 8, half * P:(half + 1) * P],
                                                      oh[:, s // HB, s % HB, :], start=True, stop=True)
                            mm.then_inc(products, 1)

                    def trip(i, begin, end):
                        for j in range(PAIRS):
                            if j + 3 < PAIRS:
                                transposes(i, j + 3)
                            elif not end:
                                transposes(i + 1, j + 3 - PAIRS)
                            if j + 2 < PAIRS:
                                edge_terms(i, j + 2)
                            elif not end:
                                edge_terms(i + 1, j + 2 - PAIRS)
                            if j > 0:
                                windows(i, j - 1)
                            elif not begin:
                                windows(i - 1, PAIRS - 1)

                    transposes(0, 0)
                    transposes(0, 1)
                    edge_terms(0, 0)
                    transposes(0, 2)
                    edge_terms(0, 1)
                    trip(0, True, False)
                    with nc.tensor.Fori(1, TRIPS - 1) as i:
                        trip(i, False, False)
                    trip(TRIPS - 1, False, True)
                    windows(TRIPS - 1, PAIRS - 1)

                @block.vector
                def _(dve):
                    nc.vector.memset(acc[:, 0:2, :], 0.0).then_inc(zeroed, 1)
                    dve.wait_ge(zeroed, 1)

                    def one_hot(i, s):
                        t = i * BODY + s
                        nc.vector.tensor_scalar(oh[:, s // HB, s % HB, :], iota_n[:, :], dloc[:, ds(t, 1)], None, ALU.is_equal).then_inc(oh_ready, 1)

                    def add_window(t, s, start):
                        dve.wait_ge(products, t + 1)
                        dve.wait_ge(win_free, t + 4)
                        window = acc[:, 0:2, ds(start, P)]
                        nc.vector.tensor_tensor(window, window, PS[4 + s % 4][:, 0:2 * P].rearrange("p (s n) -> p s n", s=2), ALU.add).then_inc(win_free, 1)

                    def one_hot_ahead(i, s, end):
                        if s < HB:
                            one_hot(i, s + HB)
                        elif not end:
                            one_hot(i + 1, s - HB)

                    def pair(i, j, end, add_former):
                        k, s = i * PAIRS + j, 2 * j
                        two = msgs[:, s % 8:s % 8 + 2, :]
                        dve.wait_ge(e_ready, k + 1 + 2)
                        for v in range(2):
                            dve.wait_ge(g_ready[s + v], (gb + i + 1) * 16)
                        nc.vector.tensor_tensor(two, grow[:, s:s + 2, 0:F], PS[2 + j % 2][:, :].rearrange("p (u f) -> p u f", u=2), ALU.add
                                                ).then_inc(rows_used, 1)
                        one_hot_ahead(i, s, end)
                        dve.wait_ge(rows_used, k + 1 + PAIRS)
                        by_head = two.rearrange("p u (h c) -> p u h c", h=H3)[:, :, 0:DVE_HEADS, :]
                        nc.vector.tensor_tensor(by_head, by_head, w_e[:, ds(i * BODY + s, 2), 0:DVE_HEADS].unsqueeze(3).broadcast_to([P, 2, DVE_HEADS, C3]),
                                                ALU.mult).then_inc(msg_ready, 1)
                        add_former(0)
                        one_hot_ahead(i, s + 1, end)
                        add_former(1)

                    def trip(i, begin, end):
                        for half in range(2):
                            back = 0 if begin and half == 0 else 4
                            t0 = i * BODY + half * HB - back
                            first = window_starts(t0, mybir.EngineType.DVE)
                            for p in range(HP):
                                j = half * HP + p

                                def add_former(v):
                                    n = 2 * p - 4 + v
                                    if n + back >= 0:
                                        add_window(i * BODY + half * HB + n, (half * HB + n) % BODY, first[n + back])
                                pair(i, j, end, add_former)

                    for s in range(HB):
                        one_hot(0, s)
                    trip(0, True, False)
                    with nc.vector.Fori(1, TRIPS - 1) as i:
                        trip(i, False, False)
                    trip(TRIPS - 1, False, True)
                    first = window_starts(ET - HB, mybir.EngineType.DVE)
                    for n in range(HB - 4, HB):
                        add_window(ET - HB + n, BODY - HB + n, first[n])
            a_base[0] += TRIPS

        def finish3(tag, last_layer):
            at, free, back, var_ready, std_ready, y_ready, y_out, dv = [
                sem(f"{tag}_{n}") for n in "at free back var_ready std_ready y_ready y_out dve".split()]
            with nc.Block() as block:
                @block.gpsimd
                def _(pool):
                    with nc.gpsimd.Fori(0, NG) as i:
                        for s in range(2):
                            last = nc.gpsimd.tensor_copy(accg[:, s, :], acc[:, s, ds(i * GRP * P, GRP * P)])
                        last.then_inc(at, 1)
                        pool.wait_ge(free, (i + 1) * GRP)

                @block.tensor
                def _(pe):
                    credit(pe, back, GRP)
                    with nc.tensor.Fori(0, NG) as i:
                        pe.wait_ge(at, i + 1)
                        for n in range(GRP):
                            pe.wait_ge(back, i * GRP + n + 1)
                            for s in range(2):
                                mm = nc.tensor.transpose(PS[n][:, s * P:(s + 1) * P], accg[:, s, n * P:(n + 1) * P], ident[:, :])
                            mm.then_inc(free, 1)

                @block.vector
                def _(dve):
                    step = Chain(dve, dv)
                    rows = stage[:, 0, :, :]
                    with nc.vector.Fori(0, NG) as i:
                        step.enter(i, 4 if last_layer else 1)
                        for n in range(GRP):
                            dve.wait_ge(free, i * GRP + n + 1)
                            nc.vector.tensor_tensor(rows[:, n, :], PS[n][:, 0:F], H[:, ds(i * GRP + n, 1), :].rearrange("p a f -> p (a f)"), ALU.add).then_inc(back, 1)
                        dve.wait_ge(back, (i + 2) * GRP)
                        if last_layer:
                            step(nc.vector.tensor_tensor(rows, rows, group_rows(X, i), ALU.add))
                            layer_norm(dve, step, rows, i, var_ready, std_ready, i + 1).then_inc(y_ready, 1)
                            dve.wait_ge(y_ready, i + 1)
                        else:
                            step(nc.vector.tensor_scalar(group_rows(H, i), rows, 0.0, None, ALU.max))
                    step.leave(NG, 4 if last_layer else 1)

                if last_layer:
                    @block.scalar
                    def _(act):
                        with nc.scalar.Fori(0, NG) as i:
                            act_root(act, var_ready, std_ready, i + 1)

                    @block.sync
                    def _(sp):
                        sp.wait_ge(y_ready, NG)
                        sp.dma_start(out[0:(NT - 1) * P, :].rearrange("(t p) f -> p t f", p=P), X[:, 0:NT - 1, :]).then_inc(y_out, 16)
                        sp.dma_start(out[(NT - 1) * P:N, :], X[0:TAIL, NT - 1, :]).then_inc(y_out, 16)
                        sp.wait_ge(y_out, 32)

        phases = [setup, project0, lambda: look_up("l0", [(1, 0, 2, 0)]),
                  lambda: aggregate("a0", h_tab, F + 2, "gat"), finish0,
                  lambda: aggregate("a1", x_tab, F, "rel"), finish1, project2,
                  lambda: look_up("l2", [(0, 0, 1, 0), (1, 1, 1, 1)]),
                  lambda: sum_scores(), lambda: edge_softmax("s2", 1, 1.0, 1.0e-10, -1.0e9, lambda h: s_e[:, :, 0]),
                  lambda: aggregate("a2", h2_tab, F, "one"), finish2,
                  lambda: project3(1, X), lambda: scores3("s31"),
                  lambda: edge_softmax("x31", H3, 0.125, 1.0e-16, None, lambda h: w_e[:, :, h]),
                  lambda: messages3("m31"), lambda: finish3("f31", False),
                  lambda: project3(2, H), lambda: scores3("s32"),
                  lambda: edge_softmax("x32", H3, 0.125, 1.0e-16, None, lambda h: w_e[:, :, h]),
                  lambda: messages3("m32"), lambda: finish3("f32", True)]
        for phase in phases:
            phase()
            end_of_phase()


_INS = (["x", "src", "dst", "edge_attr_128", "edge_type_16", "L0_gnn_W1", "L0_gnn_a1", "L0_gnn_W2", "L0_gnn_a2",
         "L1_gnn_relvectors", "L1_gnn_w_ih", "L1_gnn_w_hh", "L1_gnn_b_ih", "L1_gnn_b_hh",
         "L2_gnn_W", "L2_gnn_b", "L2_gnn_mag_w", "L2_gnn_mag_b", "L2_gnn_attn_w"]
        + [f"L3_gnn_{m}{letter}{layer}" for layer in (1, 2) for letter in "qkves" for m in "Wb"])


def kernel(**inputs):
    import numpy as np
    from concourse import bacc
    from concourse.bass_utils import run_bass_kernel_spmd

    nc = bacc.Bacc("TRN2", target_bir_lowering=False, num_devices=1)
    arrays, args = {}, {}
    for name in _INS:
        arr = np.ascontiguousarray(inputs[name])
        arrays[f"in_{name}"] = arr
        args[name] = nc.dram_tensor(f"in_{name}", arr.shape, mybir.dt.from_np(arr.dtype), kind="ExternalInput").ap()
    out = nc.dram_tensor("out_nodes", (N, F), F32, kind="ExternalOutput").ap()
    graph_layers(nc, args, out)
    r = run_bass_kernel_spmd(nc, [arrays], core_ids=[0])
    return r.results[0]["out_nodes"]
```
